# Optimizing a Trainium2 kernel written in Bass

```python
import numpy as np
import jax
import jax.numpy as jnp

def _softmax(x, axis=-1):
    return jax.nn.softmax(x, axis=axis)

def _gelu(x):
    return jax.nn.gelu(x, approximate=True)

def _silu(x):
    return jax.nn.silu(x)

def _sigmoid(x):
    return jax.nn.sigmoid(x)

def _layernorm(x, axis=-1, eps=1e-05):
    m = jnp.mean(x, axis=axis, keepdims=True)
    v = jnp.var(x, axis=axis, keepdims=True)
    return (x - m) / jnp.sqrt(v + eps)

def _scatter_add(tgt, idx, src, axis=0):
    return tgt.at[idx].add(src)

def _segment_sum(src, seg, n):
    return jax.ops.segment_sum(src, seg, n)
kernel_name = 'mk_sandwich_d2_jaxref_r8_311a29'

def setup_inputs(seed: int=0):
    np.random.seed(seed)
    _w = jnp.asarray

    def _L0_attn_setup():
        import jax, jax.numpy as jnp
        import numpy as np
        B, T, D = (1, 256, 512)
        H, G = (32, 8)
        HD = D // H
        REP = H // G
        KV_DIM = 2 * HD * G
        key = jax.random.key(seed)
        k0, k1, k2, k3 = jax.random.split(key, 4)
        x = jax.random.normal(k0, (B, T, D), dtype=jnp.float32)
        Wq = jax.random.normal(k1, (D, D), dtype=jnp.float32) * 0.02
        Wkv = jax.random.normal(k2, (D, KV_DIM), dtype=jnp.float32) * 0.02
        Wo = jax.random.normal(k3, (D, D), dtype=jnp.float32) * 0.02
        bo = jnp.zeros((D,), dtype=jnp.float32)
        return {'x': x, 'Wq': Wq, 'Wkv': Wkv, 'Wo': Wo, 'bo': bo}
    _L0_attn_in = _L0_attn_setup()

    def _L0_ffn_setup():
        import jax, jax.numpy as jnp
        import numpy as np
        H, FF = (512, 1792)
        B, S = (4, 256)
        key = jax.random.key(seed)
        ks = jax.random.split(key, 7)
        x = jax.random.normal(ks[0], (B, S, H), dtype=jnp.float32)
        gate_t = jax.random.randint(ks[1], (FF, H), -1, 2, dtype=jnp.int32)
        up_t = jax.random.randint(ks[2], (FF, H), -1, 2, dtype=jnp.int32)
        down_t = jax.random.randint(ks[3], (H, FF), -1, 2, dtype=jnp.int32)
        gate_s = jax.random.uniform(ks[4], (FF,), jnp.float32, 0.01, 0.1)
        up_s = jax.random.uniform(ks[5], (FF,), jnp.float32, 0.01, 0.1)
        down_s = jax.random.uniform(ks[6], (H,), jnp.float32, 0.01, 0.1)
        return {'x': x, 'gate_t': gate_t, 'up_t': up_t, 'down_t': down_t, 'gate_s': gate_s, 'up_s': up_s, 'down_s': down_s}
    _L0_ffn_in = _L0_ffn_setup()

    def _L1_attn_setup():
        import jax, jax.numpy as jnp
        import numpy as np
        import math
        FACTOR = 1
        key = jax.random.key(seed)
        x = jax.random.normal(key, (8, 64, 512), dtype=jnp.float32)
        return {'x': x}
    _L1_attn_in = _L1_attn_setup()

    def _L1_ffn_setup():
        import jax, jax.numpy as jnp
        import numpy as np
        D_MODEL = 512
        D_HIDDEN = 1376
        RANK = 16
        BATCH, SEQ = (2, 256)

        def _matmul_lora(x, w, a, b, scale=1.0):
            out = jnp.einsum('bsd,hd->bsh', x, w)
            out = out + jnp.einsum('bsr,hr->bsh', jnp.einsum('bsd,rd->bsr', x, a), b) * scale
            return out
        key = jax.random.key(seed)
        ks = jax.random.split(key, 10)
        s = 0.02
        return {'x': jax.random.normal(ks[0], (BATCH, SEQ, D_MODEL), jnp.float32), 'gate_w': jax.random.normal(ks[1], (D_HIDDEN, D_MODEL), jnp.float32) * s, 'up_w': jax.random.normal(ks[2], (D_HIDDEN, D_MODEL), jnp.float32) * s, 'down_w': jax.random.normal(ks[3], (D_MODEL, D_HIDDEN), jnp.float32) * s, 'gate_a': jax.random.normal(ks[4], (RANK, D_MODEL), jnp.float32) * s, 'gate_b': jax.random.normal(ks[5], (D_HIDDEN, RANK), jnp.float32) * s, 'up_a': jax.random.normal(ks[6], (RANK, D_MODEL), jnp.float32) * s, 'up_b': jax.random.normal(ks[7], (D_HIDDEN, RANK), jnp.float32) * s, 'down_a': jax.random.normal(ks[8], (RANK, D_HIDDEN), jnp.float32) * s, 'down_b': jax.random.normal(ks[9], (D_MODEL, RANK), jnp.float32) * s}
    _L1_ffn_in = _L1_ffn_setup()
    _d = {'L0_attn_x': _L0_attn_in['x'], 'L0_attn_Wq': _L0_attn_in['Wq'], 'L0_attn_Wkv': _L0_attn_in['Wkv'], 'L0_attn_Wo': _L0_attn_in['Wo'], 'L0_attn_bo': _L0_attn_in['bo'], 'L0_ffn_gate_t': _L0_ffn_in['gate_t'], 'L0_ffn_up_t': _L0_ffn_in['up_t'], 'L0_ffn_down_t': _L0_ffn_in['down_t'], 'L0_ffn_gate_s': _L0_ffn_in['gate_s'], 'L0_ffn_up_s': _L0_ffn_in['up_s'], 'L0_ffn_down_s': _L0_ffn_in['down_s'], 'L1_ffn_gate_w': _L1_ffn_in['gate_w'], 'L1_ffn_up_w': _L1_ffn_in['up_w'], 'L1_ffn_down_w': _L1_ffn_in['down_w'], 'L1_ffn_gate_a': _L1_ffn_in['gate_a'], 'L1_ffn_gate_b': _L1_ffn_in['gate_b'], 'L1_ffn_up_a': _L1_ffn_in['up_a'], 'L1_ffn_up_b': _L1_ffn_in['up_b'], 'L1_ffn_down_a': _L1_ffn_in['down_a'], 'L1_ffn_down_b': _L1_ffn_in['down_b']}
    _x0 = _d['L0_attn_x']
    _d['L0_attn_x'] = jax.random.normal(jax.random.fold_in(jax.random.key(seed), 1), (1, 1024, 512), dtype=_x0.dtype)
    del _x0
    return _d

def reference(L0_attn_x, L0_attn_Wq, L0_attn_Wkv, L0_attn_Wo, L0_attn_bo, L0_ffn_gate_t, L0_ffn_up_t, L0_ffn_down_t, L0_ffn_gate_s, L0_ffn_up_s, L0_ffn_down_s, L1_ffn_gate_w, L1_ffn_up_w, L1_ffn_down_w, L1_ffn_gate_a, L1_ffn_gate_b, L1_ffn_up_a, L1_ffn_up_b, L1_ffn_down_a, L1_ffn_down_b):

    def _L0_attn_ref(x, Wq, Wkv, Wo, bo):
        import jax, jax.numpy as jnp
        import numpy as np
        B, T, D = (1, 256, 512)
        H, G = (32, 8)
        HD = D // H
        REP = H // G
        KV_DIM = 2 * HD * G
        b, t, d = x.shape
        q = jnp.dot(x, Wq).reshape(b, t, H, HD).transpose(0, 2, 1, 3)
        kv = jnp.dot(x, Wkv).reshape(b, t, G, 2, HD).transpose(2, 3, 0, 1, 4)
        k, v = (kv[:, 0], kv[:, 1])
        k = jnp.broadcast_to(k[:, :, None], (G, b, REP, t, HD)).reshape(b, H, t, HD)
        v = jnp.broadcast_to(v[:, :, None], (G, b, REP, t, HD)).reshape(b, H, t, HD)
        scores = jnp.einsum('bhqd,bhkd->bhqk', q, k)
        causal = jnp.triu(jnp.ones((t, t), dtype=bool), 1)
        scores = jnp.where(causal[None, None], -jnp.inf, scores)
        weights = jax.nn.softmax(scores * (1.0 / HD ** 0.5), axis=-1)
        ctx = jnp.einsum('bhqk,bhkd->bhqd', weights, v)
        ctx = ctx.transpose(0, 2, 1, 3).reshape(b, t, d)
        return jnp.dot(ctx, Wo) + bo

    def _L0_ffn_ref(x, gate_t, up_t, down_t, gate_s, up_s, down_s):
        import jax, jax.numpy as jnp
        import numpy as np
        H, FF = (512, 1792)
        B, S = (4, 256)
        Bb, Ss, Hh = x.shape
        x_flat = x.reshape(Bb * Ss, Hh)
        gate_w = gate_t.astype(jnp.float32) * gate_s[:, None]
        up_w = up_t.astype(jnp.float32) * up_s[:, None]
        down_w = down_t.astype(jnp.float32) * down_s[:, None]
        gate_out = x_flat @ gate_w.T
        up_out = x_flat @ up_w.T
        hidden = jax.nn.silu(gate_out) * up_out
        out_flat = hidden @ down_w.T
        return out_flat.reshape(Bb, Ss, -1)

    def _L1_attn_ref(x):
        import jax, jax.numpy as jnp
        import numpy as np
        import math
        FACTOR = 1
        B, C, L = x.shape
        xh = x[:, None]
        f = jnp.fft.rfft(xh, axis=-1)
        corr = jnp.fft.irfft(f * jnp.conj(f), n=L, axis=-1)
        top_k = int(FACTOR * math.log(L))
        weights, delay = jax.lax.top_k(corr, top_k)
        tmp_corr = jax.nn.softmax(weights, axis=-1)
        init_index = jnp.arange(L)
        idx = (init_index[None, None, None, None, :] + delay[..., None]) % L
        pattern = jnp.take_along_axis(xh[:, :, :, None, :], idx, axis=-1)
        delays_agg = jnp.sum(pattern * tmp_corr[..., None], axis=-2)
        return delays_agg[:, 0]

    def _L1_ffn_ref(x, gate_w, up_w, down_w, gate_a, gate_b, up_a, up_b, down_a, down_b):
        import jax, jax.numpy as jnp
        import numpy as np
        D_MODEL = 512
        D_HIDDEN = 1376
        RANK = 16
        BATCH, SEQ = (2, 256)

        def _matmul_lora(x, w, a, b, scale=1.0):
            out = jnp.einsum('bsd,hd->bsh', x, w)
            out = out + jnp.einsum('bsr,hr->bsh', jnp.einsum('bsd,rd->bsr', x, a), b) * scale
            return out
        gate = _matmul_lora(x, gate_w, gate_a, gate_b)
        up = _matmul_lora(x, up_w, up_a, up_b)
        hidden = jax.nn.silu(gate) * up
        out = _matmul_lora(hidden, down_w, down_a, down_b)
        return out
    x = L0_attn_x
    x = x + _layernorm(_L0_attn_ref(_layernorm(x, axis=-1), L0_attn_Wq, L0_attn_Wkv, L0_attn_Wo, L0_attn_bo), axis=-1)
    x = x + _layernorm(_L0_ffn_ref(_layernorm(x, axis=-1), L0_ffn_gate_t, L0_ffn_up_t, L0_ffn_down_t, L0_ffn_gate_s, L0_ffn_up_s, L0_ffn_down_s), axis=-1)
    x = x + _layernorm(_L1_attn_ref(_layernorm(x, axis=-1)), axis=-1)
    x = x + _layernorm(_L1_ffn_ref(_layernorm(x, axis=-1), L1_ffn_gate_w, L1_ffn_up_w, L1_ffn_down_w, L1_ffn_gate_a, L1_ffn_gate_b, L1_ffn_up_a, L1_ffn_up_b, L1_ffn_down_a, L1_ffn_down_b), axis=-1)
    return x

_drawn_inputs = setup_inputs


def setup_inputs(seed=0):
    import zlib

    import numpy as np

    out = dict(_drawn_inputs(seed))
    spreads = {'L0_attn_bo': (0.0, 0.1)}
    factors = {}
    for name, (base, spread) in spreads.items():
        noise = np.random.default_rng([zlib.crc32(name.encode()), seed]).standard_normal(out[name].shape)
        drawn = base * np.exp(spread * noise) if base else spread * noise
        out[name] = jnp.asarray(drawn.astype(out[name].dtype))
    for name, factor in factors.items():
        out[name] = (out[name] * factor).astype(out[name].dtype)
    return out
```

```python
from contextlib import ExitStack

import concourse.bass as bass
from concourse import mybir

P = 128
T, D = 1024, 512
NT, ND = T // P, D // P
H, G, HD = 32, 8, 16
REP = H // G
TERMS = ((0, 0), (0, 1), (1, 0), (1, 1), (0, 2), (2, 0))
QROWS = HD * len(TERMS)
MROWS = 3
RING = 3
LEAD = 3
UNITS = REP * (NT // 2) * 3
NEG = -1.0e30
LN_EPS = 1.0e-5

FF0, FF1, RANK = 1792, 1376, 16
N0, N1 = FF0 // P, -(-FF1 // P)
TAIL = FF1 - (N1 - 1) * P
FF1P = N1 * P
LAGS = D // 2 + 1
TOPK = 6
SENT = -3.0e38
PICKED = 3.0e38
CH, SUB = T // 2, 4

F32, F16, BF16, I32 = mybir.dt.float32, mybir.dt.float16, mybir.dt.bfloat16, mybir.dt.int32
ALU = mybir.AluOpType
ACT = mybir.ActivationFunctionType


def unit_base(qt):
    return REP * qt if qt < NT // 2 else REP * (NT // 2) + 2 * REP * (qt - NT // 2)


def chunks(qt):
    if qt < NT // 2:
        return [(0, (qt + 1) * P, True)]
    return [(0, D, False), (D, (qt + 1) * P, True)]


class Chain:

    def __init__(self, engine, sem, base=0):
        self.engine, self.sem, self.n = engine, sem, base

    def later(self, instruction):
        self.n = self.n + 1
        instruction.then_inc(self.sem, 1)

    def settle(self):
        self.engine.wait_ge(self.sem, self.n)

    def __call__(self, instruction):
        self.later(instruction)
        self.settle()


def build(nc, x_in, Wq, Wkv, Wo, bo, gate_t, up_t, down_t, gate_s, up_s, down_s,
          gate_w, up_w, down_w, gate_a, gate_b, up_a, up_b, down_a, down_b, dft, power, inverse, out):
    with ExitStack() as ctx:
        def sb(name, shape, dt=F32):
            return ctx.enter_context(nc.sbuf_tensor(name, shape, dt))

        def sem(name):
            return ctx.enter_context(nc.semaphore(name))

        def dram(name, shape, dt=F32):
            return nc.dram_tensor(name, shape, dt, kind="Internal").ap()

        ARENA = 200
        arena = sb("arena", [P, ARENA * 256])

        def room(kib, shape, dt=F32):
            n = 1
            for k in shape:
                n *= k
            words = -(-n * (4 if dt in (F32, I32) else 2) // 4)
            start = int(kib * 256)
            assert start + words <= ARENA * 256
            v = arena[:, start:start + words]
            v = v if dt == F32 else v.bitcast(dt)
            names = "abcd"[:len(shape)]
            if len(shape) > 1:
                v = v.rearrange("p (" + " ".join(names) + ") -> p " + " ".join(names),
                                **{names[i]: shape[i] for i in range(len(shape))})
            return v

        x = room(0, [NT, D])
        pc = [room(16 + 4 * i, [2, T], BF16) for i in range(3)]
        res = room(28, [2, T])
        w0g = room(37, [ND, FF0], F16)
        w0u = room(51, [ND, FF0], F16)
        w0d = room(65, [N0, D], BF16)
        probs = room(80, [2, REP, T])
        qt6 = room(112, [RING, REP, T], BF16)
        kt6 = room(136, [G, T], BF16)
        ctxt = room(152, [ND, T])
        wo = room(168, [ND, D])
        osb = room(176, [T])
        recb = room(180, [T])
        ctxn = room(184, [T])
        vall = room(188, [NT, G, HD])
        junk = room(192, [REP, D], BF16)
        vcur = room(196, [NT, 32])
        strip = room(197, [D], BF16)
        wq = room(80, [ND, D])
        wkv = room(88, [ND, 2 * G * HD])
        wk = room(92, [ND, P])
        xnt = room(96, [ND, T])
        xn = room(152, [NT, D])
        prep_w = room(16, [2, D])
        prep_p = room(20, [2, D])
        prep_n = room(24, [2, 2, D], F16)
        prep_dw = room(16, [FF1])
        prep_dp = room(21.5, [FF1])
        prep_pw = room(27, [FF1])
        prep_dn = room(152, [2, FF1P], F16)
        prep_de = room(158, [FF1])
        dft_sb = room(16, [2, ND, D], F16)
        inv_sb = room(24, [2, ND, D], F16)
        pow_sb = room(32, [2, ND, LAGS], F16)
        w1d = room(37, [2, N1, D], F16)
        spec = room(59, [2, ND, CH])
        sq = room(75, [2, CH])
        w1g = room(80, [2, ND, FF1], F16)
        w1u = room(101.5, [2, ND, FF1], F16)
        xt = room(123, [2, 2, ND, CH], F16)
        y = room(139, [SUB, D])
        corr = room(147, [2, D + 2])
        u_sb = room(147, [2, CH])
        wspec = room(152, [ND, CH])
        sqp = room(160, [2, ND, CH], F16)
        wt = room(168, [2, ND, CH], F16)
        nat = room(180, [2, SUB, D], F16)
        hid = room(188, [2, 2, CH], F16)
        hs = room(192, [2, CH])
        sg = room(196, [2, CH])
        expc = room(192, [2, D])
        picked = room(196, [D + 2])
        mx = sb("mx", [P, REP, NT])
        mx2 = sb("mx2", [P, REP, NT // 2])
        mr = sb("mr", [P, REP, NT])
        m3 = sb("m3", [P, P], BF16)
        mt = sb("mt", [P, P], BF16)
        dens = sb("dens", [P, 32])
        recs = sb("recs", [P, 32])
        ident = sb("ident", [P, P])
        stats = sb("stats", [P, NT, 6])
        mv = sb("mv", [P, NT, 2])
        var = sb("var", [P, NT])
        rstd = sb("rstd", [P, NT])
        nw = sb("nw", [P, 3, NT])

        qp_d = dram("qp_d", [3, H * HD, T], BF16)
        kp_d = dram("kp_d", [3, G * HD, T], BF16)
        mt_d = dram("mt_d", [G, P, P], BF16)
        den_d = dram("den_d", [G, REP, T])
        rec_d = dram("rec_d", [G, REP, T])
        ctx_d = dram("ctx_d", [H * HD, T])

        ps = ctx.enter_context(nc.psum_tensor("ps", [P, 8, 512], F32))
        s_bank = lambda u: ps[:, u % 2, :]
        st_bank = lambda n: ps[:, 2 + 2 * (n % 2):4 + 2 * (n % 2), :]
        o_bank = ps[:, 6:8, :]
        o_flat = o_bank.rearrange("p b n -> p (b n)")

        x_loaded, wkv_loaded, wq_loaded, wo_loaded = [sem("x_loaded0"), sem("x_loaded1")], sem("wkv_loaded"), sem("wq_loaded"), sem("wo_loaded")
        ident_ready, ident_zero = sem("ident_ready"), sem("ident_zero")
        strip_ready = sem("strip_ready")
        dve_passed, pool_passed, sp_passed = sem("dve_passed"), sem("pool_passed"), sem("sp_passed")
        dve_chain, pool_chain = sem("dve_chain"), sem("pool_chain")
        xn_ready, xnt_psum, xnt_ready = sem("xn_ready"), sem("xnt_psum"), sem("xnt_ready")
        wk_ready = sem("wk_ready")
        proj_psum, v_psum, v_ready = sem("proj_psum"), sem("v_psum"), sem("v_ready")
        piece0, proj_free, pieces_ready, pieces_stored = sem("piece0"), sem("proj_free"), sem("pieces_ready"), [sem("pieces_stored0"), sem("pieces_stored1")]
        res_ready, piece1 = sem("res_ready"), sem("piece1")
        kt_loaded, qt_loaded, ones_ready = sem("kt_loaded"), sem("qt_loaded"), sem("ones_ready")
        s_ready, s_taken = sem("s_ready"), sem("s_taken")
        m3_ready, mt_ready, mt_stored, m_loaded = sem("m3_ready"), sem("mt_ready"), sem("mt_stored"), sem("m_loaded")
        st_ready, p_ready, masked, pv_done, vcur_ready = sem("st_ready"), sem("p_ready"), sem("masked"), sem("pv_done"), sem("vcur_ready")
        o_taken, den_stored, den_loaded, rec_ready, rec_stored, rec_loaded = sem("o_taken"), sem("den_stored"), sem("den_loaded"), sem("rec_ready"), sem("rec_stored"), sem("rec_loaded")
        ctx_ready, ctx_stored, ctx_loaded = sem("ctx_ready"), sem("ctx_stored"), sem("ctx_loaded")
        out_done = sem("out_done")

        def rsqrt(link, n):
            v, r = var[:, 0:n], rstd[:, 0:n]
            link(nc.vector.tensor_scalar(r.bitcast(I32), v.bitcast(I32), -0.5, float(0x5F3759DF), ALU.mult, ALU.add))
            for _ in range(3):
                link(nc.vector.tensor_tensor(nw[:, 0, 0:n], v, r, ALU.mult))
                link(nc.vector.tensor_tensor(nw[:, 1, 0:n], nw[:, 0, 0:n], r, ALU.mult))
                link(nc.vector.tensor_scalar(nw[:, 2, 0:n], nw[:, 1, 0:n], -0.5, 1.5, ALU.mult, ALU.add))
                link(nc.vector.tensor_tensor(r, r, nw[:, 2, 0:n], ALU.mult))

        XS, WS, TS = 2.0 ** 10, 2.0 ** 8, 2.0 ** 10
        EXPONENT = 0x7F800000

        y_ready, y_free = sem("y_ready"), sem("y_free")
        tr_done = [sem(f"tr_done{j}") for j in range(8)]
        nat_ready = sem("nat_ready")
        rows_loaded = sem("rows_loaded")
        scales0_loaded, scales0_ready = sem("scales0_loaded"), sem("scales0_ready")
        w0_cast = [sem(f"w0_cast{i}") for i in range(3)]
        w0_loaded = [sem(f"w0_loaded{i}") for i in range(3)]
        lora_in, lora_da, lora_ready, lora_taken = sem("lora_in"), sem("lora_da"), sem("lora_ready"), sem("lora_taken")
        lora_stored = [sem("lora_stored0"), sem("lora_stored1")]
        prep_loaded = [sem("prep_loaded0"), sem("prep_loaded1")]
        prep_done = sem("prep_done")
        prep_stored = [sem("prep_stored0"), sem("prep_stored1")]
        exps_ready, pw_stored, pw_loaded = sem("exps_ready"), sem("pw_stored"), sem("pw_loaded")
        pd_loaded, pd_done, pd_stored = sem("pd_loaded"), sem("pd_done"), sem("pd_stored")
        drow_stored, drow_loaded = sem("drow_stored"), sem("drow_loaded")
        w1_loaded = [sem(f"w1_loaded{i}") for i in range(3)]
        tables_loaded = sem("tables_loaded")
        gu_ready, gu_free, sg_ready, hs_ready, hi_ready, hid_ready, down_done = (
            sem("gu_ready"), sem("gu_free"), sem("sg_ready"), sem("hs_ready"), sem("hi_ready"), sem("hid_ready"), sem("down_done"))
        f_ready, f_taken, sq_ready, sqh_ready, sqp_ready, c_ready = (
            sem("f_ready"), sem("f_taken"), sem("sq_ready"), sem("sqh_ready"), sem("sqp_ready"), sem("c_ready"))
        top_ready, e_ready = sem("top_ready"), sem("e_ready")
        wf_ready, wf_taken, prod_ready, prodh_ready, prodp_ready = (
            sem("wf_ready"), sem("wf_taken"), sem("prod_ready"), sem("prodh_ready"), sem("prodp_ready"))
        f1_ready = sem("f1_ready")
        x_done, pick_done = sem("x_done"), sem("pick_done")

        w16_d = [dram("w0g_d", [FF0, D], F16), dram("w0u_d", [FF0, D], F16), dram("w0d_d", [D, FF0], BF16)]
        lora_d = dram("lora_d", [2, FF1, D])
        lorad_d = dram("lorad_d", [D, FF1])
        w1n_d = dram("w1n_d", [2, 2, FF1, D], F16)
        w1dn_d = dram("w1dn_d", [2, D, FF1P], F16)
        pw_d = dram("pw_d", [FF1P])
        drow_d = dram("drow_d", [D])

        row_b = sb("row_b", [P, D], F32)
        sc0 = sb("sc0", [P, 4, N0])
        ex0 = sb("ex0", [P, 4, N0])
        e1 = sb("e1", [P, 2, N1])
        ie1 = sb("ie1", [P, 1])
        gs1 = sb("gs1", [P, N1])
        r1 = sb("r1", [P, N1])
        pw1 = sb("pw1", [P, N1])
        f1 = sb("f1", [P, ND])
        top = sb("top", [P, 8])
        ntop = sb("ntop", [P, 2])
        etop = sb("etop", [P, 8])
        wsum = sb("wsum", [P, 8])
        rsum = sb("rsum", [P, 8])
        notdc = sb("notdc", [P, 1])

        lora_nat = [room(33.25, [N1, RANK]), room(34, [N1, RANK]), room(34.75, [ND, RANK])]
        lora_bt = [room(16, [FF1]), room(21.5, [FF1]), room(27, [D])]
        lora_a = [room(29, [D]), room(31, [D]), room(82, [FF1])]
        lora_out = room(104, [2, D])
        lora_jobs = ([("t", m, j) for m in range(3) for j in range((3, 3, 1)[m])]
                     + [("p", m, j) for m in range(2) for j in range(N1)]
                     + [("d", o, j) for o in range(ND) for j in range(4)])

        def height(m, n):
            return TAIL if m < 2 and n == N1 - 1 else P

        def sp_early(sp):
            sp.dma_start(sc0[:, 0, :], gate_s.rearrange("(n p) -> p n", p=P), allow_slow_non_contiguous=True).then_inc(scales0_loaded, 16)
            sp.dma_start(sc0[:, 1, :], up_s.rearrange("(n p) -> p n", p=P), allow_slow_non_contiguous=True).then_inc(scales0_loaded, 16)
            sp.dma_start(row_b[:, :], bo.rearrange("(a d) -> a d", a=1).broadcast_to([P, D])).then_inc(rows_loaded, 16)
            for m, b in enumerate((gate_b, up_b)):
                full = (N1 - 1) * P
                sp.dma_start(lora_nat[m][:, 0:N1 - 1, :], b[0:full, :].rearrange("(n p) r -> p n r", p=P)).then_inc(lora_in, 16)
                sp.dma_start(lora_nat[m][0:TAIL, N1 - 1, :], b[full:FF1, :]).then_inc(lora_in, 16)
            sp.dma_start(lora_nat[2][:, :, :], down_b.rearrange("(n p) r -> p n r", p=P)).then_inc(lora_in, 16)
            sp.dma_start(lora_a[0][0:RANK, :], gate_a).then_inc(lora_in, 16)
            sp.dma_start(lora_a[1][0:RANK, :], up_a).then_inc(lora_in, 16)

        def sp_weights0(sp, i):
            sp.wait_ge(w0_cast[i], 16)
            sp.dma_start_transpose((w0g, w0u, w0d)[i], w16_d[i]).then_inc(w0_loaded[i], 16)

        def transposes(sp, use, dst):
            for i in range(SUB):
                sp.wait_ge(nat_ready, SUB * use + i + 1)
                for piece in range(2):
                    sp.dma_start_transpose(dst(piece)[:, :, i * P:(i + 1) * P], nat[:, piece, i, :]).then_inc(tr_done[use], 16)

        def sp_rest(sp):
            for c in range(2):
                transposes(sp, c, lambda piece: xt[:, c, piece])
            sp.wait_ge(y_free, 4 * 2)
            sp.dma_start(row_b[:, :], down_s.rearrange("(a d) -> a d", a=1).broadcast_to([P, D])).then_inc(rows_loaded, 16)
            sp.wait_ge(lora_stored[0], 16 * 19)
            sp.wait_ge(lora_stored[1], 16 * 19)
            for m, w in enumerate((gate_w, up_w)):
                def load(ht, n, h):
                    sp.dma_start(prep_w[0:h, n % 2, :], w[bass.ds(ht * P, h), :]).then_inc(prep_loaded_of(n), 16)
                    sp.dma_start(prep_p[0:h, n % 2, :], lora_d[m, bass.ds(ht * P, h), :]).then_inc(prep_loaded_of(n), 16)

                def store(ht, n, h):
                    sp.wait_ge(prep_done, n + 1)
                    for piece in range(2):
                        sp.dma_start(w1n_d[m, piece, bass.ds(ht * P, h), :], prep_n[0:h, n % 2, piece, :]).then_inc(prep_stored_of(n), 16)

                for ht in range(N1):
                    n = m * N1 + ht
                    if n >= 2:
                        sp.wait_ge(prep_done, n - 1)
                    load(ht, n, height(m, ht))
                    if ht > 0:
                        store(ht - 1, n - 1, P)
                store(N1 - 1, m * N1 + N1 - 1, TAIL)
            sp.wait_ge(exps_ready, 1)
            sp.wait_ge(prep_stored[0], 32 * N1)
            sp.wait_ge(prep_stored[1], 32 * N1)
            sp.dma_start(pw_d.rearrange("(n p) -> p n", p=P), pw1[:, :], allow_slow_non_contiguous=True).then_inc(pw_stored, 16)
            sp.wait_ge(pw_stored, 16)
            sp.dma_start(prep_pw[:, :], pw_d[0:FF1].rearrange("(a n) -> a n", a=1).broadcast_to([P, FF1])).then_inc(pw_loaded, 16)
            for o in range(ND):
                if o > 0:
                    sp.wait_ge(pd_done, o)
                sp.dma_start(prep_dw[:, :], down_w[o * P:(o + 1) * P, :]).then_inc(pd_loaded, 16)
                sp.dma_start(prep_dp[:, :], lorad_d[o * P:(o + 1) * P, :]).then_inc(pd_loaded, 16)
                sp.wait_ge(pd_done, o + 1)
                for piece in range(2):
                    sp.dma_start(w1dn_d[piece, o * P:(o + 1) * P, :], prep_dn[:, piece, :]).then_inc(pd_stored, 16)
                sp.wait_ge(pd_stored, 32 * (o + 1))
            sp.wait_ge(f1_ready, 1)
            sp.dma_start(drow_d.rearrange("(n p) -> p n", p=P), f1[:, :], allow_slow_non_contiguous=True).then_inc(drow_stored, 16)
            sp.dma_start(dft_sb, dft.rearrange("i (c p) n -> p i c n", p=P)).then_inc(tables_loaded, 16)
            sp.dma_start(inv_sb, inverse.rearrange("i (c p) n -> p i c n", p=P)).then_inc(tables_loaded, 16)
            sp.dma_start(pow_sb, power.rearrange("i (c p) n -> p i c n", p=P)).then_inc(tables_loaded, 16)
            for m, w in enumerate((w1g, w1u)):
                for piece in range(2):
                    sp.dma_start_transpose(w[:, piece], w1n_d[m, piece]).then_inc(w1_loaded[m], 16)
            transposes(sp, 2, lambda piece: xt[:, 0, piece])
            transposes(sp, 3, lambda piece: xt[:, 1, piece])
            sp.wait_ge(gu_ready, 2 * N0)
            for piece in range(2):
                sp.dma_start_transpose(w1d[:, piece], w1dn_d[piece]).then_inc(w1_loaded[2], 16)
            sp.wait_ge(y_free, 4 * 4)
            sp.wait_ge(drow_stored, 16)
            sp.dma_start(row_b[:, :], drow_d.rearrange("(a d) -> a d", a=1).broadcast_to([P, D])).then_inc(drow_loaded, 16)
            transposes(sp, 4, lambda piece: wt[:, piece])
            sp.wait_ge(wf_ready, 4)
            transposes(sp, 5, lambda piece: wt[:, piece])
            transposes(sp, 6, lambda piece: xt[:, 0, piece])
            transposes(sp, 7, lambda piece: xt[:, 1, piece])
            for c in range(2):
                sp.wait_ge(x_done, c + 1)
                sp.dma_start(out[0].rearrange("(t p) d -> p t d", p=P)[:, SUB * c:SUB * (c + 1), :],
                             x[:, SUB * c:SUB * (c + 1), :]).then_inc(out_done, 16)
            sp.wait_ge(out_done, 32)

        prep_loaded_of = lambda n: prep_loaded[n % 2]
        prep_stored_of = lambda n: prep_stored[n % 2]

        def norm_add(dve, link, q, k, c, take, use):
            for i in range(SUB):
                dve.wait_ge(y_ready, SUB * q + i + 1)
                take(i).then_inc(y_free, 1)
            dve.wait_ge(y_free, SUB * k + SUB)
            xc = x[:, SUB * c:SUB * (c + 1), :]

            def moments(v):
                for i in range(SUB):
                    link.later(nc.vector.bn_stats(stats[:, i, :], v[:, i, :]))
                link.settle()
                for i in range(SUB):
                    link.later(nc.vector.bn_aggr(mv[:, i, :], stats[:, i, :]))
                link.settle()
                link(nc.vector.tensor_scalar(var[:, 0:SUB], mv[:, 0:SUB, 1], LN_EPS, None, ALU.add))
                rsqrt(link, SUB)

            moments(y)
            for i in range(SUB):
                link.later(nc.vector.tensor_scalar(y[:, i, :], y[:, i, :], mv[:, i, 0:1], rstd[:, i:i + 1],
                                                   ALU.subtract, ALU.mult))
            link.settle()
            if use is None:
                nc.vector.tensor_tensor(xc, xc, y, ALU.add).then_inc(x_done, 1)
                dve.wait_ge(x_done, c + 1)
                return
            link(nc.vector.tensor_tensor(xc, xc, y, ALU.add))
            moments(xc)
            link(nc.vector.tensor_scalar(rstd[:, 0:SUB], rstd[:, 0:SUB], XS, None, ALU.mult))
            for i in range(SUB):
                link.later(nc.vector.tensor_scalar(y[:, i, :], xc[:, i, :], mv[:, i, 0:1], rstd[:, i:i + 1],
                                                   ALU.subtract, ALU.mult))
            link.settle()
            pieces(dve, link, use, y)

        def pieces(dve, link, use, v):
            if use > 0:
                dve.wait_ge(tr_done[use - 1], 16 * 2 * SUB)
            for i in range(SUB):
                link.later(nc.vector.tensor_copy(nat[:, 0, i, :], v[:, i, :]))
            link.settle()
            for i in range(SUB):
                nc.vector.tensor_tensor(nat[:, 1, i, :], v[:, i, :], nat[:, 0, i, :], ALU.subtract).then_inc(nat_ready, 1)
            dve.wait_ge(nat_ready, SUB * (use + 1))

        def exponent(link, to, of, least):
            link(nc.vector.tensor_scalar(to.bitcast(I32), of.bitcast(I32), EXPONENT, None, ALU.bitwise_and))
            link(nc.vector.tensor_scalar(to, to, least, None, ALU.max))

        def inverse_of(link, to, of, shift):
            link(nc.vector.tensor_scalar(to.bitcast(I32), of.bitcast(I32), -1.0, float((254 + shift) << 23), ALU.mult, ALU.add))

        def scales0(dve, link):
            dve.wait_ge(scales0_loaded, 32)
            exponent(link, ex0[:, 0, :], sc0[:, 0, :], 2.0 ** -40)
            exponent(link, ex0[:, 1, :], sc0[:, 1, :], 2.0 ** -40)
            inverse_of(link, ex0[:, 2, :], ex0[:, 0, :], 0)
            inverse_of(link, ex0[:, 3, :], ex0[:, 1, :], 0)
            link(nc.vector.tensor_scalar(sc0[:, 2, :], sc0[:, 0, :], 1.0 / XS, None, ALU.mult))
            link(nc.vector.tensor_tensor(sc0[:, 3, :], sc0[:, 1, :], ex0[:, 2, :], ALU.mult))
            link(nc.vector.tensor_scalar(sc0[:, 3, :], sc0[:, 3, :], 1.0 / (32 * XS), None, ALU.mult))
            link(nc.vector.tensor_tensor(sc0[:, 3, :], sc0[:, 3, :], ex0[:, 3, :], ALU.mult))
            link(nc.vector.tensor_tensor(ex0[:, 0, :], ex0[:, 0, :], ex0[:, 1, :], ALU.mult))
            link(nc.vector.tensor_scalar(ex0[:, 0, :], ex0[:, 0, :], 32.0, None, ALU.mult))
            dve.wait_ge(w0_loaded[2], 16)
            for ht in range(N0):
                nc.vector.tensor_scalar(w0d[:, ht, :], w0d[:, ht, :], ex0[:, 0, ht:ht + 1], None, ALU.mult).then_inc(scales0_ready, 1)

        def prepare1(dve, link):
            link(nc.vector.memset(e1[:, :, :], 1.0))
            for m in range(2):
                for ht in range(N1):
                    n, h = m * N1 + ht, height(m, ht)
                    b = n % 2
                    dve.wait_ge(prep_loaded[b], 32 * (n // 2 + 1))
                    link(nc.vector.tensor_tensor(prep_p[0:h, b, :], prep_p[0:h, b, :], prep_w[0:h, b, :], ALU.add))
                    scaled_pieces(dve, link, prep_p[0:h, b, :], e1[0:h, m, ht:ht + 1], ie1[0:h, :],
                                  prep_n[0:h, b, 0, :], prep_n[0:h, b, 1, :], prep_done,
                                  (prep_stored[b], 32 * (n // 2)) if n >= 2 else None)
            dve.wait_ge(prep_done, 2 * N1)
            link(nc.vector.tensor_scalar(gs1[:, :], e1[:, 0, :], 1.0 / (XS * WS), None, ALU.mult))
            inverse_of(link, r1[:, :], e1[:, 0, :], 0)
            link(nc.vector.tensor_scalar(r1[:, :], r1[:, :], 1.0 / (32 * XS * WS), None, ALU.mult))
            link(nc.vector.tensor_tensor(pw1[:, :], e1[:, 0, :], e1[:, 1, :], ALU.mult))
            nc.vector.tensor_scalar(pw1[:, :], pw1[:, :], 32.0, None, ALU.mult).then_inc(exps_ready, 1)
            link(nc.vector.memset(prep_dn[:, :, FF1:FF1P], 0.0))
            dve.wait_ge(pw_loaded, 16)
            for o in range(ND):
                dve.wait_ge(pd_loaded, 32 * (o + 1))
                link(nc.vector.tensor_tensor(prep_dp[:, :], prep_dp[:, :], prep_dw[:, :], ALU.add))
                link(nc.vector.tensor_tensor(prep_de[:, :], prep_dp[:, :], prep_pw[:, :], ALU.mult))
                scaled_pieces(dve, link, prep_de[:, :], f1[:, o:o + 1], ie1[:, :],
                              prep_dn[:, 0, 0:FF1], prep_dn[:, 1, 0:FF1], pd_done,
                              (pd_stored, 32 * o) if o else None)
            dve.wait_ge(pd_done, ND)
            nc.vector.tensor_scalar(f1[:, :], f1[:, :], 1.0 / WS, None, ALU.mult).then_inc(f1_ready, 1)

        def scaled_pieces(dve, link, v, e, ie, high, low, done, stored):
            link(nc.vector.tensor_reduce(e, v, mybir.AxisListType.X, ALU.max, apply_absolute_value=True))
            exponent(link, e, e, 2.0 ** -60)
            inverse_of(link, ie, e, 8)
            if stored:
                dve.wait_ge(*stored)
            link(nc.vector.tensor_scalar(high, v, ie, None, ALU.mult))
            nc.vector.scalar_tensor_tensor(out=low, in0=v, scalar=ie, in1=high, op0=ALU.mult, op1=ALU.subtract).then_inc(done, 1)

        def top_lags(dve, link, c):
            for i in range(SUB):
                n = SUB * c + i
                dve.wait_ge(c_ready, n + 1)
                cr = corr[:, i % 2, :]
                p = ps[:, 4 + i, :]
                link(nc.vector.tensor_scalar(cr[:, 0:LAGS], p[:, 0:LAGS], 2.0 ** -14, None, ALU.mult))
                nc.vector.tensor_scalar(cr[:, LAGS:D], p[:, D - LAGS:0:-1], 2.0 ** -14, None, ALU.mult).then_inc(y_free, 1)
                dve.wait_ge(y_free, SUB * (4 + c) + i + 1)
                if n > 0:
                    dve.wait_ge(e_ready, n)
                link(nc.vector.max(out=top[:, :], in_=cr[:, 0:D]))
                link(nc.vector.tensor_scalar(ntop[:, 0:1], top[:, 0:1], -1.0, None, ALU.mult))
                nc.vector.memset(top[:, TOPK:8], SENT).then_inc(top_ready, 1)
                dve.wait_ge(top_ready, n + 1)
                link(nc.vector.match_replace(out=picked[:, :], in_to_replace=top[:, :], in_values=cr, imm_value=PICKED))
                dve.wait_ge(e_ready, n + 1)
                nc.vector.scalar_tensor_tensor(out=y[:, i, :], in0=picked[:, 0:D], scalar=PICKED, in1=expc[:, i % 2, :],
                                               op0=ALU.is_equal, op1=ALU.mult).then_inc(pick_done, 1)
                dve.wait_ge(pick_done, n + 1)
            link(nc.vector.tensor_scalar(y, y, TS, None, ALU.mult))
            pieces(dve, link, 4 + c, y)

        def spectra(dve, link, c):
            dve.wait_ge(wf_taken, 4 * (c + 1))
            half = ND // 2
            for j in range(half):
                a, b = spec[:, c, j, :], spec[:, c, half + j, :]
                al, be = wspec[:, j, :], wspec[:, half + j, :]
                t = y
                if (c, j) != (0, 0):
                    dve.wait_ge(prodp_ready, 4 * c + 2 * j)
                link.later(nc.vector.tensor_tensor(t[:, 0, :], a, al, ALU.mult))
                link.later(nc.vector.tensor_tensor(t[:, 1, :], b, be, ALU.mult))
                link.later(nc.vector.tensor_tensor(t[:, 2, :], a, be, ALU.mult))
                link.later(nc.vector.tensor_tensor(t[:, 3, :], b, al, ALU.mult))
                link.settle()
                if j == 0:
                    nc.vector.scalar_tensor_tensor(out=prod[:, 0, :], in0=t[:, 1, :], scalar=notdc[:, 0:1], in1=t[:, 0, :],
                                                   op0=ALU.mult, op1=ALU.add).then_inc(prod_ready, 1)
                    link(nc.vector.tensor_tensor(prod[:, 1, :], t[:, 2, :], t[:, 3, :], ALU.subtract))
                    nc.vector.tensor_copy(prod[0:1, 1, :], t[0:1, 1, :]).then_inc(prod_ready, 1)
                else:
                    nc.vector.tensor_tensor(prod[:, 0, :], t[:, 0, :], t[:, 1, :], ALU.add).then_inc(prod_ready, 1)
                    nc.vector.tensor_tensor(prod[:, 1, :], t[:, 2, :], t[:, 3, :], ALU.subtract).then_inc(prod_ready, 1)
                dve.wait_ge(prod_ready, 4 * c + 2 * j + 2)

        prod = sq

        def dve_rest(dve):
            link = Chain(dve, sem("dve_chain2"))
            scales0(dve, link)
            dve.wait_ge(rows_loaded, 16)

            def add_bias(i):
                return nc.vector.tensor_tensor(y[:, i, :], ps[:, 4 + i, :], row_b[:, :], ALU.add)

            def by_row_scale(i):
                return nc.vector.tensor_tensor(y[:, i, :], ps[:, 4 + i, :], row_b[:, :], ALU.mult)

            for c in range(2):
                norm_add(dve, link, c, c, c, add_bias, c)
            prepare1(dve, link)
            dve.wait_ge(rows_loaded, 32)
            for c in range(2):
                norm_add(dve, link, 2 + c, 2 + c, c, by_row_scale, 2 + c)
            link(nc.vector.memset(corr[:, :, D:D + 2], SENT))
            for c in range(2):
                top_lags(dve, link, c)
            dve.wait_ge(e_ready, 2 * SUB)
            link(nc.vector.reciprocal(rsum[:, :], wsum[:, :]))
            link(nc.vector.tensor_scalar(rsum[:, :], rsum[:, :], 2.0 ** -22, None, ALU.mult))
            link(nc.vector.memset(notdc[:, :], 1.0))
            link(nc.vector.memset(notdc[0:1, :], 0.0))
            for c in range(2):
                spectra(dve, link, c)
            for c in range(2):
                norm_add(dve, link, 4 + c, 6 + c, c,
                         lambda i: nc.vector.tensor_scalar(y[:, i, :], ps[:, 4 + i, :], rsum[:, SUB * c + i:SUB * c + i + 1],
                                                           None, ALU.mult), 6 + c)
            dve.wait_ge(drow_loaded, 16)
            for c in range(2):
                norm_add(dve, link, 6 + c, 8 + c, c, by_row_scale, None)

        def act_rest(act):
            chain = sem("act_chain")
            n = 0
            stores = 0
            for k, (kind, a, b) in enumerate(lora_jobs):
                act.wait_ge(lora_ready, k + 1)
                bank = ps[:, k % 4, :]
                if kind == "t":
                    w = min(4 * P, (FF1, FF1, D)[a] - b * 4 * P)
                    nc.scalar.copy(lora_bt[a][0:RANK, b * 512:b * 512 + w], bank[0:RANK, 0:w]).then_inc(lora_taken, 1)
                    continue
                s = stores % 2
                if stores >= 2:
                    act.wait_ge(lora_stored[s], 16 * (stores // 2))
                h, w = (height(0, b), D) if kind == "p" else (P, FF1 // 4)
                nc.scalar.copy(lora_out[0:h, s, 0:w], bank[0:h, 0:w]).then_inc(lora_taken, 1)
                act.wait_ge(lora_taken, k + 1)
                dst = (lora_d[a, b * P:b * P + h, :] if kind == "p"
                       else lorad_d[a * P:(a + 1) * P, b * w:(b + 1) * w])
                act.dma_start(dst, lora_out[0:h, s, 0:w]).then_inc(lora_stored[s], 16)
                stores += 1
            act.wait_ge(scales0_ready, 1)
            for c in range(2):
                act_ffn(act, N0 * c, N0, lambda ht: sc0[:, 2, ht], lambda ht: sc0[:, 3, ht], P, c, 2 + c)
            for c in range(2):
                for ft in range(ND):
                    act.wait_ge(f_ready, 4 * c + ft + 1)
                    nc.scalar.activation(spec[:, c, ft, :], ps[:, ft, :], ACT.Copy, scale=1.0 / (XS * TS)).then_inc(f_taken, 1)
                    k = 4 * c + ft
                    if k >= 2:
                        act.wait_ge(sqp_ready, k - 1)
                    nc.scalar.activation(sq[:, k % 2, :], ps[:, ft, :], ACT.Square, scale=1.0 / (4 * XS * TS)).then_inc(sq_ready, 1)
                    if k >= 4:
                        act.wait_ge(c_ready, 4)
                    act.wait_ge(sq_ready, k + 1)
                    nc.scalar.copy(sqp[:, 0, ft, :], sq[:, k % 2, :]).then_inc(sqh_ready, 1)
                for i in range(SUB):
                    k = SUB * c + i
                    act.wait_ge(top_ready, k + 1)
                    nc.scalar.activation(etop[:, 0:TOPK], top[:, 0:TOPK], ACT.Exp, bias=ntop[:, 0:1],
                                         accum_out=wsum[:, k:k + 1]).then_inc(chain, 1)
                    n += 1
                    act.wait_ge(chain, n)
                    if k >= 2:
                        act.wait_ge(pick_done, k - 1)
                    nc.scalar.activation(expc[:, i % 2, :], corr[:, i % 2, 0:D], ACT.Exp, bias=ntop[:, 0:1]).then_inc(e_ready, 1)
            for c in range(2):
                for ft in range(ND):
                    act.wait_ge(wf_ready, 4 * c + ft + 1)
                    if c:
                        act.wait_ge(prod_ready, 4)
                    nc.scalar.activation(wspec[:, ft, :], ps[:, ft, :], ACT.Copy, scale=16.0 / (TS * TS)).then_inc(wf_taken, 1)
                for k in range(4):
                    act.wait_ge(prod_ready, 4 * c + k + 1)
                    if c:
                        act.wait_ge(y_ready, 4 * SUB + SUB)
                    ft = (k // 2) + 2 * (k % 2)
                    nc.scalar.copy(sqp[:, 0, ft, :], prod[:, k % 2, :]).then_inc(prodh_ready, 1)
            for c in range(2):
                act_ffn(act, 2 * N0 + N1 * c, N1, lambda ht: gs1[:, ht], lambda ht: r1[:, ht], TAIL, 2 + c, 6 + c)

        def act_ffn(act, base, tiles, gate_scale, up_scale, tail, before, q):
            def tile(ht, h, first):
                n = base + ht
                b = n % 2
                act.wait_ge(gu_ready, n + 1)
                if not first or base > 0:
                    act.wait_ge(hs_ready, n - 1)
                gsc, usc = gate_scale(bass.ds(ht, 1)), up_scale(bass.ds(ht, 1))
                nc.scalar.activation(sg[0:h, b, :], ps[0:h, 2 * b, :], ACT.Silu, scale=gsc[0:h, :]).then_inc(sg_ready, 1)
                nc.scalar.activation(u_sb[0:h, b, :], ps[0:h, 2 * b + 1, :], ACT.Copy, scale=usc[0:h, :]).then_inc(gu_free, 1)

            def high(ht, h, first):
                n = base + ht
                act.wait_ge(hs_ready, n + 1)
                if not first:
                    act.wait_ge(down_done, n - 1 - before)
                elif before:
                    act.wait_ge(y_ready, SUB * q)
                nc.scalar.copy(hid[0:h, 0, n % 2, :], hs[0:h, n % 2, :]).then_inc(hi_ready, 1)

            tile(0, P, True)
            tile(1, P, True)
            high(0, P, True)
            tile(2, P, False)
            high(1, P, True)
            with act.Fori(3, tiles - 1) as ht:
                tile(ht, P, False)
                high(ht - 1, P, False)
            tile(tiles - 1, tail, False)
            high(tiles - 2, P, False)
            high(tiles - 1, tail, False)

        def pool_rest(pool):
            for c in range(2):
                pool_ffn(pool, N0 * c, N0, P)
            for k in range(8):
                pool.wait_ge(sqh_ready, k + 1)
                if k >= 4:
                    pool.wait_ge(c_ready, 4)
                nc.gpsimd.tensor_tensor(sqp[:, 1, k % 4, :], sq[:, k % 2, :], sqp[:, 0, k % 4, :], ALU.subtract).then_inc(sqp_ready, 1)
            for c in range(2):
                for k in range(4):
                    pool.wait_ge(prodh_ready, 4 * c + k + 1)
                    ft = (k // 2) + 2 * (k % 2)
                    nc.gpsimd.tensor_tensor(sqp[:, 1, ft, :], prod[:, k % 2, :], sqp[:, 0, ft, :], ALU.subtract).then_inc(prodp_ready, 1)
            for c in range(2):
                pool_ffn(pool, 2 * N0 + N1 * c, N1, TAIL)

        def pool_ffn(pool, base, tiles, tail):
            def product(ht, h, first):
                n = base + ht
                pool.wait_ge(gu_free, n + 1)
                pool.wait_ge(sg_ready, n + 1)
                if not first or base > 0:
                    pool.wait_ge(hid_ready, n - 1)
                    pool.wait_ge(hi_ready, n - 1)
                nc.gpsimd.tensor_tensor(hs[0:h, n % 2, :], sg[0:h, n % 2, :], u_sb[0:h, n % 2, :], ALU.mult).then_inc(hs_ready, 1)

            def low(ht, h, first):
                n = base + ht
                pool.wait_ge(hi_ready, n + 1)
                nc.gpsimd.tensor_tensor(hid[0:h, 1, n % 2, :], hs[0:h, n % 2, :], hid[0:h, 0, n % 2, :], ALU.subtract).then_inc(hid_ready, 1)

            product(0, P, True)
            product(1, P, True)
            low(0, P, True)
            product(2, P, False)
            low(1, P, True)
            with pool.Fori(3, tiles - 1) as ht:
                product(ht, P, False)
                low(ht - 1, P, False)
            product(tiles - 1, tail, False)
            low(tiles - 2, P, False)
            low(tiles - 1, tail, False)

        TWO = ((0, 0), (0, 1))
        THREE = ((0, 0), (0, 1), (1, 0))

        def pe_rest(pe):
            pe.wait_ge(lora_in, 16 * 7)
            pe.wait_ge(p_ready, 32 * G)
            taken = 0
            for k, (kind, a, b) in enumerate(lora_jobs):
                if k >= 4:
                    pe.wait_ge(lora_taken, k - 3)
                bank = ps[:, k % 4, :]
                if kind == "t":
                    for j in range(4 * b, min(4 * b + 4, (N1, N1, ND)[a])):
                        h = height(a, j)
                        last = nc.tensor.transpose(bank[0:RANK, (j - 4 * b) * P:(j - 4 * b) * P + h], lora_nat[a][0:h, j, :], ident[0:h, 0:h])
                    last.then_inc(lora_ready, 1)
                    continue
                pe.wait_ge(lora_taken, max(k - 3, 7))
                if kind == "p":
                    h = height(0, b)
                    nc.tensor.matmul(bank[0:h, :], lora_bt[a][0:RANK, b * P:b * P + h], lora_a[a][0:RANK, :],
                                     start=True, stop=True).then_inc(lora_ready, 1)
                else:
                    if (a, b) == (0, 0):
                        pe.wait_ge(lora_da, 16)
                    w = FF1 // 4
                    nc.tensor.matmul(bank[:, 0:w], lora_bt[2][0:RANK, a * P:(a + 1) * P], lora_a[2][0:RANK, b * w:(b + 1) * w],
                                     start=True, stop=True).then_inc(lora_ready, 1)
            pe.wait_ge(wo_loaded, 16)
            pe.wait_ge(ctx_loaded, 16)
            pe.wait_ge(o_taken, G)
            for c in range(2):
                for i in range(SUB):
                    if c:
                        pe.wait_ge(y_free, i + 1)
                    for kt in range(ND):
                        last = nc.tensor.matmul(ps[:, 4 + i, :], ctxt[:, kt, (SUB * c + i) * P:(SUB * c + i + 1) * P], wo[:, kt, :],
                                                start=kt == 0, stop=kt == ND - 1)
                    last.then_inc(y_ready, 1)
            pe.wait_ge(lora_taken, len(lora_jobs))
            for i in range(3):
                pe.wait_ge(w0_loaded[i], 16)
            pe.wait_ge(scales0_ready, N0)
            for c in range(2):
                pe.wait_ge(tr_done[c], 16 * 2 * SUB)
                pe_ffn(pe, N0 * c, N0, P, c, 2 + c, lambda p: w0g, lambda p: w0u, lambda p: w0d, TWO, ((0, 0), (1, 0)))
            pe.wait_ge(tables_loaded, 48)
            pe.wait_ge(gu_free, 2 * N0)
            pe.wait_ge(sg_ready, 2 * N0)
            for c in range(2):
                pe.wait_ge(tr_done[2 + c], 16 * 2 * SUB)
                for ft in range(ND):
                    if c:
                        pe.wait_ge(sq_ready, ft + 1)
                    product(pe, ps[:, ft, :], lambda w, kt: dft_sb[:, w, kt, ft * P:(ft + 1) * P],
                            lambda r, kt: xt[:, c, r, kt, :], f_ready)
                pe.wait_ge(sqp_ready, 4 * (c + 1))
                for i in range(SUB):
                    pe.wait_ge(y_free, SUB * (3 + c) + i + 1)
                    product(pe, ps[:, 4 + i, 0:LAGS], lambda w, kt: sqp[:, w, kt, i * P:(i + 1) * P],
                            lambda r, kt: pow_sb[:, r, kt, :], c_ready)
            for c in range(2):
                pe.wait_ge(tr_done[4 + c], 16 * 2 * SUB)
                pe.wait_ge(sq_ready, 8)
                for ft in range(ND):
                    if c:
                        pe.wait_ge(wf_taken, ft + 1)
                    product(pe, ps[:, ft, :], lambda w, kt: dft_sb[:, w, kt, ft * P:(ft + 1) * P],
                            lambda r, kt: wt[:, r, kt, :], wf_ready)
                pe.wait_ge(prodp_ready, 4 * (c + 1))
                for i in range(SUB):
                    pe.wait_ge(y_free, SUB * (5 + c) + i + 1)
                    product(pe, ps[:, 4 + i, :], lambda w, kt: sqp[:, w, kt, i * P:(i + 1) * P],
                            lambda r, kt: inv_sb[:, r, kt, :], y_ready)
            pe.wait_ge(w1_loaded[0], 32)
            pe.wait_ge(w1_loaded[1], 32)
            pe.wait_ge(w1_loaded[2], 32)
            pe.wait_ge(wf_taken, 8)
            for c in range(2):
                pe.wait_ge(tr_done[6 + c], 16 * 2 * SUB)
                pe_ffn(pe, 2 * N0 + N1 * c, N1, TAIL, c, 8 + c, lambda p: w1g[:, p], lambda p: w1u[:, p], lambda p: w1d[:, p],
                       THREE, ((0, 0), (1, 0), (0, 1)))

        def product(pe, to, lhs, rhs, ready):
            for kt in range(ND):
                for w, r in THREE:
                    last = nc.tensor.matmul(to, lhs(w, kt), rhs(r, kt), start=(kt, w, r) == (0, 0, 0),
                                            stop=(kt, w, r) == (ND - 1, 1, 0))
            last.then_inc(ready, 1)

        def pe_ffn(pe, base, tiles, tail, c, k, gate, up, down, terms, down_terms):
            def hidden(ht, h, first):
                n = base + ht
                if not first or base > 0:
                    pe.wait_ge(gu_free, n - 1)
                    pe.wait_ge(sg_ready, n - 1)
                for o, w in ((0, gate), (1, up)):
                    for kt in range(ND):
                        for t in terms:
                            last = nc.tensor.matmul(ps[0:h, 2 * (n % 2) + o, :], w(t[0])[:, kt, bass.ds(ht * P, h)],
                                                    xt[:, c, t[1], kt, :], start=(kt, t) == (0, terms[0]),
                                                    stop=(kt, t) == (ND - 1, terms[-1]))
                last.then_inc(gu_ready, 1)

            def out_of(ht, h, first, last_tile):
                n = base + ht
                pe.wait_ge(hid_ready, n + 1)
                for i in range(SUB):
                    if first:
                        pe.wait_ge(y_free, SUB * (k - 1) + i + 1)
                    for t in down_terms:
                        last = nc.tensor.matmul(ps[:, 4 + i, :], hid[0:h, t[0], n % 2, i * P:(i + 1) * P], down(t[1])[0:h, ht, :],
                                                start=first and t == down_terms[0], stop=last_tile and t == down_terms[-1])
                    if last_tile:
                        last.then_inc(y_ready, 1)
                if not last_tile:
                    last.then_inc(down_done, 1)

            hidden(0, P, True)
            hidden(1, P, True)
            hidden(2, P, False)
            out_of(0, P, True, False)
            with pe.Fori(3, tiles - 1) as ht:
                hidden(ht, P, False)
                out_of(ht - 2, P, False, False)
            hidden(tiles - 1, tail, False)
            out_of(tiles - 3, P, False, False)
            out_of(tiles - 2, P, False, False)
            out_of(tiles - 1, tail, False, True)


        block = ctx.enter_context(nc.Block())

        def for_groups(eng, body):
            body(eng, 0, 0)
            with eng.Fori(1, G - 2) as g:
                body(eng, g, 1)
            body(eng, G - 2, G - 2)
            body(eng, G - 1, G - 1)

        def load_q(sp, g):
            for s, (qp, _) in enumerate(TERMS):
                src = qp_d[qp].rearrange("(g h d) t -> g d h t", g=G, h=REP)
                sp.dma_start(qt6[HD * s:HD * (s + 1), g % RING, :, :], src[g]).then_inc(qt_loaded, 16)

        def maxima_path(sp, g):
            sp.wait_ge(m3_ready, g + 1)
            sp.sem_inc(sp_passed)
            sp.dma_start_transpose(mt[:, :], m3[:, :]).then_inc(mt_ready, 16)
            sp.wait_ge(mt_ready, 16 * (g + 1))
            sp.dma_start(mt_d[g], mt[:, :]).then_inc(mt_stored, 16)
            sp.wait_ge(mt_stored, 16 * (g + 1))
            sp.dma_start(qt6[QROWS:QROWS + MROWS, g % RING, :, :],
                         mt_d[g, 0:MROWS * REP * NT, :].rearrange("(i r) q -> i (r q)", i=MROWS)
                         .rearrange("i (h t) -> i h t", h=REP)).then_inc(m_loaded, 16)

        def den_path(sp, g):
            sp.wait_ge(o_taken, g + 1)
            sp.dma_start(den_d[g], osb[HD:P:32, :]).then_inc(den_stored, 16)
            sp.wait_ge(den_stored, 16 * (g + 1))
            sp.dma_start(dens[:, :], den_d[g].rearrange("h (a b) -> (h a) b", b=32)).then_inc(den_loaded, 16)
            sp.wait_ge(rec_ready, g + 1)
            sp.dma_start(rec_d[g].rearrange("h (a b) -> (h a) b", b=32), recs[:, :]).then_inc(rec_stored, 16)
            sp.wait_ge(rec_stored, 16 * (g + 1))
            for h in range(REP):
                sp.dma_start(recb[32 * h:32 * h + 32, :], rec_d[g, h:h + 1, :].broadcast_to([32, T])).then_inc(rec_loaded, 16)

        def ctx_store(sp, g):
            sp.wait_ge(ctx_ready, g + 1)
            dst = ctx_d.rearrange("(g h d) t -> g h d t", g=G, h=REP)
            for h in range(REP):
                sp.dma_start(dst[g, h], ctxn[32 * h:32 * h + HD, :]).then_inc(ctx_stored, 16)

        def sp_group(sp, g, shape):
            if shape < G - 2:
                if shape > 0:
                    sp.wait_ge(st_ready, 32 * g)
                else:
                    sp.wait_ge(qt_loaded, 2 * 16 * len(TERMS))
                load_q(sp, g + 2)
            if shape > 0:
                den_path(sp, g - 1)
            if shape < G - 1:
                maxima_path(sp, g + 1)
            if shape > 0:
                ctx_store(sp, g - 1)
            if shape in (0, G - 2, G - 1):
                sp_weights0(sp, (0, G - 2, G - 1).index(shape))

        def pool_norm(pool, g):
            pool.wait_ge(rec_loaded, 16 * REP * (g + 1))
            if not isinstance(g, int) or g > 0:
                pool.wait_ge(ctx_stored, 16 * REP * g)
            nc.gpsimd.tensor_tensor(ctxn[:, :], osb[:, :], recb[:, :], ALU.mult).then_inc(ctx_ready, 1)

        def pool_group(pool, g, shape):
            for kt in range(NT):
                pool.wait_ge(p_ready, 32 * g + 4 * kt + 4)
                diag = probs[:, kt % 2, :, kt * P:(kt + 1) * P]
                pool.sem_inc(pool_passed)
                nc.gpsimd.affine_select(out=diag, in_=diag, compare_op=ALU.is_ge, fill=0.0, base=0,
                                        pattern=[[0, REP], [1, P]], channel_multiplier=-1).then_inc(masked, 1)
                if kt == 0:
                    if shape > 0:
                        pool.wait_ge(pv_done, NT * g)
                    nc.gpsimd.tensor_copy(vcur[:, :, 0:HD], vall[:, :, g, :]).then_inc(vcur_ready, 1)
                if kt == 5 and shape > 0:
                    pool_norm(pool, g - 1)

        def row_max(dve, g, qt, first):
            for h in range(REP):
                for c, (k0, k1, diagonal) in enumerate(chunks(qt)):
                    u = unit_base(qt) + len(chunks(qt)) * h + c
                    dve.wait_ge(s_ready, UNITS * g + u + 1)
                    w = k1 - k0
                    if diagonal:
                        to = mx[:, h, qt:qt + 1] if c == 0 else mx2[:, h, qt - NT // 2:qt - NT // 2 + 1]
                        back = UNITS * g + u + 1 - (REP if c == 0 else 2 * REP) 
                        if first != 0 or u >= 8:
                            dve.wait_ge(s_taken, back if first != 0 or u >= 8 else 0)
                        elif u >= REP:
                            dve.wait_ge(s_taken, u + 1 - REP)
                        dve.sem_inc(dve_passed)
                        nc.vector.tensor_tensor_reduce(
                            out=junk[:, h, 0:w], in0=s_bank(u)[:, 0:w], in1=strip[:, D - w:D], scale=1.0, scalar=3.0 * NEG,
                            op0=ALU.add, op1=ALU.max, accum_out=to).then_inc(s_taken, 1)
                    else:
                        nc.vector.reduce_max(mx[:, h, qt:qt + 1], s_bank(u)[:, 0:w],
                                             mybir.AxisListType.X).then_inc(s_taken, 1)

        def max_pieces(dve, g):
            dve.wait_ge(s_taken, UNITS * (g + 1))
            n = Chain(dve, max_chain, 4 * g)
            half = NT // 2
            n(nc.vector.tensor_tensor(mx[:, :, half:NT], mx[:, :, half:NT], mx2[:, :, :], ALU.max))
            p3 = m3[:, 0:MROWS * REP * NT].rearrange("p (i h t) -> p i h t", i=MROWS, h=REP)
            if not isinstance(g, int) or g > 0:
                dve.wait_ge(mt_ready, 16 * g)
            n(nc.vector.tensor_scalar(p3[:, 0], mx[:, :, :], -1.0, None, ALU.mult))
            n(nc.vector.scalar_tensor_tensor(out=mr[:, :, :], in0=mx[:, :, :], scalar=-1.0, in1=p3[:, 0],
                                             op0=ALU.mult, op1=ALU.subtract))
            n(nc.vector.tensor_copy(p3[:, 1], mr[:, :, :]))
            nc.vector.tensor_tensor(p3[:, 2], mr[:, :, :], p3[:, 1], ALU.subtract).then_inc(m3_ready, 1)
            dve.wait_ge(m3_ready, g + 1)

        max_chain = sem("max_chain")

        def ahead(g, kt, shape):
            n = NT + kt + LEAD
            if shape + n // NT >= G:
                return None
            return g + n // NT, n % NT

        def dve_group(dve, g, shape):
            for kt in range(NT):
                to = ahead(g, kt, shape)
                if to:
                    row_max(dve, *to, 1)
                    if to[1] == NT - 1:
                        max_pieces(dve, to[0])
                if kt == 3 and shape > 0:
                    dve.wait_ge(den_loaded, 16 * g)
                    dve.wait_ge(rec_stored, 16 * (g - 1)) if shape > 1 or not isinstance(g, int) else None
                    nc.vector.reciprocal(recs[:, :], dens[:, :]).then_inc(rec_ready, 1)

        def take_o(act, g):
            act.wait_ge(pv_done, NT * (g + 1))
            if not isinstance(g, int) or g > 0:
                act.wait_ge(ctx_ready, g)
            nc.scalar.copy(osb[:, :], o_flat).then_inc(o_taken, 1)

        def act_group(act, g, shape):
            for kt in range(NT):
                for h in range(REP):
                    n = 32 * g + 4 * kt + h
                    act.wait_ge(st_ready, n + 1)
                    if h == 0 and (kt >= 2 or shape > 0):
                        act.wait_ge(pv_done, NT * g + kt - 1)
                    nc.scalar.activation(probs[:, kt % 2, h, kt * P:T],
                                         st_bank(h).rearrange("p b n -> p (b n)")[:, kt * P:T],
                                         ACT.Exp, scale=HD ** -0.5).then_inc(p_ready, 1)
                    if kt == 1 and h == 0 and shape > 0:
                        take_o(act, g - 1)

        def scores(pe, g, qt, h, first):
            if h == 0 and qt == 0:
                pe.wait_ge(qt_loaded, 16 * len(TERMS) * (g + 1))
            for c, (k0, k1, _) in enumerate(chunks(qt)):
                u = unit_base(qt) + len(chunks(qt)) * h + c
                if first or u >= 2:
                    pe.wait_ge(s_taken, UNITS * g + u - 1)
                nc.tensor.matmul(s_bank(u)[:, 0:k1 - k0], qt6[0:QROWS, g % RING, h, qt * P:(qt + 1) * P],
                                 kt6[0:QROWS, g, k0:k1], start=True, stop=True).then_inc(s_ready, 1)

        def scores_t(pe, g, kt, h, shape):
            n = 4 * kt + h
            if shape > 0 or n >= 2:
                pe.wait_ge(p_ready, 32 * g + n - 1)
            lhs = kt6[0:QROWS + MROWS, g, kt * P:(kt + 1) * P]
            for b in range(kt // 4, 2):
                q0, q1 = max(kt * P, b * 512), (b + 1) * 512
                last = nc.tensor.matmul(st_bank(h)[:, b, q0 - b * 512:512], lhs, qt6[0:QROWS + MROWS, g % RING, h, q0:q1],
                                        start=True, stop=True)
            last.then_inc(st_ready, 1)

        def weighted(pe, g, kt, shape):
            pe.wait_ge(p_ready, 32 * g + 4 * kt + 4)
            pe.wait_ge(masked, NT * g + kt + 1)
            if kt == 0:
                pe.wait_ge(vcur_ready, g + 1)
                if shape > 0:
                    pe.wait_ge(o_taken, g)
            for b in range(kt // 4, 2):
                q0, q1 = max(kt * P, b * 512), (b + 1) * 512
                for h in range(REP):
                    last = nc.tensor.matmul(o_bank[32 * h:32 * h + 32, b, q0 - b * 512:512], vcur[:, kt, :],
                                            probs[:, kt % 2, h, q0:q1], start=kt == 0, stop=kt == 4 * b + 3,
                                            tile_position=(0, 32 * h))
            last.then_inc(pv_done, 1)

        def pe_group(pe, g, shape):
            pe.wait_ge(m_loaded, 16 * (g + 1))
            for kt in range(NT):
                to = ahead(g, kt, shape)
                for h in range(REP):
                    if to:
                        scores(pe, *to, h, 1)
                    scores_t(pe, g, kt, h, shape)
                if kt > 0:
                    weighted(pe, g, kt - 1, shape)
                elif shape > 0:
                    weighted(pe, g - 1, NT - 1, 1)


        @block.sync
        def _(sp):
            for half in range(2):
                sp.dma_start(x[:, 4 * half:4 * half + 4, :], x_in[0].rearrange("(t p) d -> p t d", p=P)[:, 4 * half:4 * half + 4, :]).then_inc(x_loaded[half], 16)
            sp.dma_start(wkv, Wkv.rearrange("(c p) n -> p c n", p=P)).then_inc(wkv_loaded, 16)
            sp.dma_start(wq, Wq.rearrange("(c p) n -> p c n", p=P)).then_inc(wq_loaded, 16)
            sp.dma_start(wo[:, :, :], Wo.rearrange("(c p) n -> p c n", p=P)).then_inc(wo_loaded, 16)
            for j in range(1 + ND):
                sp.wait_ge(pieces_ready, j + 1)
                for i in range(3):
                    dst = kp_d[i] if j == 0 else qp_d[i, (j - 1) * P:j * P, :]
                    sp.dma_start(dst, pc[i][:, j % 2, :]).then_inc(pieces_stored[j % 2], 16)
                if j == 0:
                    sp.wait_ge(pieces_stored[0], 48)
                    for s, (_, kp) in enumerate(TERMS):
                        sp.dma_start(kt6[HD * s:HD * (s + 1), :, :],
                                     kp_d[kp].rearrange("(g d) t -> d g t", g=G)).then_inc(kt_loaded, 16)
                if j == 1:
                    sp.wait_ge(pieces_stored[1], 48)
                    load_q(sp, 0)
                    sp.wait_ge(qt_loaded, 16 * len(TERMS))
            sp.wait_ge(pieces_stored[0], 48 * 3)
            sp.wait_ge(pieces_stored[1], 48 * 2)
            sp_early(sp)
            load_q(sp, 1)
            maxima_path(sp, 0)
            for_groups(sp, sp_group)
            sp.wait_ge(pv_done, NT * G)
            sp.dma_start(lora_a[2][0:RANK, :], down_a).then_inc(lora_da, 16)
            den_path(sp, G - 1)
            ctx_store(sp, G - 1)
            sp.wait_ge(ctx_stored, 16 * REP * G)
            sp.dma_start(ctxt[:, :, :], ctx_d.rearrange("(c p) t -> p c t", p=P)).then_inc(ctx_loaded, 16)
            sp_rest(sp)

        @block.gpsimd
        def _(pool):
            nc.gpsimd.memset(ident[:, :], 0.0).then_inc(ident_zero, 1)
            pool.wait_ge(ident_zero, 1)
            nc.gpsimd.affine_select(out=ident[:, :], in_=ident[:, :], compare_op=ALU.not_equal, fill=1.0,
                                    base=0, pattern=[[-1, P]], channel_multiplier=1).then_inc(ident_ready, 1)
            nc.gpsimd.memset(strip[:, :], 0.0).then_inc(pool_chain, 1)
            pool.wait_ge(pool_chain, 1)
            nc.gpsimd.affine_select(out=strip[:, D - P:D], in_=strip[:, D - P:D], compare_op=ALU.is_ge, fill=NEG,
                                    base=0, pattern=[[-1, P]], channel_multiplier=1).then_inc(strip_ready, 1)
            pool.wait_ge(x_loaded[1], 16)
            for i, w in enumerate((gate_t, up_t, down_t)):
                pool.dma_start(w16_d[i], w).then_inc(w0_cast[i], 16)
            nc.gpsimd.memset(vcur[:, :, HD:HD + 1], 1.0).then_inc(pool_chain, 1)
            nc.gpsimd.memset(vcur[:, :, HD + 1:32], 0.0).then_inc(pool_chain, 1)
            pool.wait_ge(pool_chain, 3)
            nc.gpsimd.memset(kt6[QROWS:P, :, :], 1.0).then_inc(ones_ready, 1)
            pool.wait_ge(ones_ready, 1)
            pool.wait_ge(v_ready, 1)
            for_groups(pool, pool_group)
            pool_norm(pool, G - 1)
            pool_rest(pool)

        @block.vector
        def _(dve):
            link = Chain(dve, dve_chain)
            link(nc.vector.memset(m3[:, :], 0.0))
            dve.wait_ge(x_loaded[0], 16)
            for t in range(NT):
                if t == 4:
                    dve.wait_ge(x_loaded[1], 16)
                link.later(nc.vector.bn_stats(stats[:, t, :], x[:, t, :]))
            link.settle()
            for t in range(NT):
                link.later(nc.vector.bn_aggr(mv[:, t, :], stats[:, t, :]))
            link.settle()
            link(nc.vector.tensor_scalar(var[:, :], mv[:, :, 1], LN_EPS, None, ALU.add))
            rsqrt(link, NT)
            for t in range(NT):
                nc.vector.tensor_scalar(xn[:, t, :], x[:, t, :], mv[:, t, 0:1], rstd[:, t:t + 1],
                                        ALU.subtract, ALU.mult).then_inc(xn_ready, 1)
            for j in range(1 + ND):
                b = j % 2
                dve.wait_ge(piece0, j + 1)
                nc.vector.tensor_tensor(res[:, b, :], ps[:, 2 * b + 0:2 * b + 2, :].rearrange("p b n -> p (b n)"), pc[0][:, b, :],
                                        ALU.subtract).then_inc(res_ready, 1)
                dve.wait_ge(res_ready, j + 1)
                link(nc.vector.tensor_copy(pc[1][:, b, :], res[:, b, :]))
                nc.vector.tensor_tensor(pc[2][:, b, :], res[:, b, :], pc[1][:, b, :], ALU.subtract).then_inc(pieces_ready, 1)
            dve.wait_ge(strip_ready, 1)
            for qt in range(NT):
                row_max(dve, 0, qt, 0)
            max_pieces(dve, 0)
            for qt in range(LEAD):
                row_max(dve, 1, qt, 1)
            for_groups(dve, dve_group)
            dve.wait_ge(den_loaded, 16 * G)
            nc.vector.reciprocal(recs[:, :], dens[:, :]).then_inc(rec_ready, 1)
            dve_rest(dve)

        @block.scalar
        def _(act):
            act.wait_ge(wkv_loaded, 16)
            nc.scalar.copy(wk.rearrange("p c (g d) -> p c g d", g=G),
                           wkv.rearrange("p c (g two d) -> p c g two d", g=G, two=2)[:, :, :, 0, :]).then_inc(wk_ready, 1)
            for t in range(NT):
                act.wait_ge(xnt_psum, t + 1)
                nc.scalar.copy(xnt[:, :, t * P:(t + 1) * P],
                               ps[:, t, :].rearrange("p (c q) -> p c q", c=ND)).then_inc(xnt_ready, 1)
            for j in range(1 + ND):
                b = j % 2
                act.wait_ge(proj_psum, j + 1)
                if j >= 2:
                    act.wait_ge(pieces_stored[b], 48 * (j // 2))
                    act.wait_ge(pieces_ready, j - 1)
                nc.scalar.copy(pc[0][:, b, :], ps[:, 2 * b:2 * b + 2, :].rearrange("p b n -> p (b n)")).then_inc(piece0, 1)
                if j == 0:
                    act.wait_ge(v_psum, 1)
                    nc.scalar.copy(vall[:, :, :, :].rearrange("p t g d -> p (t g d)"),
                                   ps[:, 4:6, :].rearrange("p b n -> p (b n)")).then_inc(v_ready, 1)
            for_groups(act, act_group)
            take_o(act, G - 1)
            act_rest(act)

        @block.tensor
        def _(pe):
            pe.wait_ge(ident_ready, 1)
            for t in range(NT):
                pe.wait_ge(xn_ready, t + 1)
                for c in range(ND):
                    last = nc.tensor.transpose(ps[:, t, c * P:(c + 1) * P], xn[:, t, c * P:(c + 1) * P], ident[:, :])
                last.then_inc(xnt_psum, 1)
            pe.wait_ge(xnt_ready, NT)
            pe.wait_ge(wkv_loaded, 16)
            kvw = wkv.rearrange("p c (g two d) -> p c g two d", g=G, two=2)

            def project(j, weights):
                for half in range(2):
                    for c in range(ND):
                        last = nc.tensor.matmul(ps[:, 2 * (j % 2) + half, :], weights(c), xnt[:, c, half * 512:(half + 1) * 512],
                                                start=c == 0, stop=c == ND - 1)
                last.then_inc(proj_psum, 1)

            pe.wait_ge(wk_ready, 1)
            project(0, lambda c: wk[:, c, :])
            for t in range(NT):
                for c in range(ND):
                    last = nc.tensor.matmul(ps[:, 4 + t // 4, (t % 4) * P:(t % 4 + 1) * P], xnt[:, c, t * P:(t + 1) * P],
                                            kvw[:, c, :, 1, :], start=c == 0, stop=c == ND - 1)
            last.then_inc(v_psum, 1)
            pe.wait_ge(wq_loaded, 16)
            for j in range(1, 1 + ND):
                if j >= 2:
                    pe.wait_ge(res_ready, j - 1)
                project(j, lambda c: wq[:, c, (j - 1) * P:j * P])
            pe.wait_ge(kt_loaded, 16 * len(TERMS))
            pe.wait_ge(res_ready, 1 + ND)
            for qt in range(NT):
                for h in range(REP):
                    scores(pe, 0, qt, h, 0)
            for qt in range(LEAD):
                for h in range(REP):
                    scores(pe, 1, qt, h, 1)
            pe.wait_ge(ones_ready, 1)
            pe.wait_ge(v_ready, 1)
            for_groups(pe, pe_group)
            weighted(pe, G - 1, NT - 1, 1)
            pe_rest(pe)


def tables():
    import numpy as np
    n, half = np.arange(D), D // 2

    def angle(a, b):
        return 2 * np.pi * (np.outer(a, b) % D) / D

    def in_pieces(a):
        high = a.astype(np.float16)
        return np.stack([high, (a - high).astype(np.float16)])

    f = np.arange(half)
    forward = np.concatenate([np.cos(angle(n, f)), np.sin(angle(n, f))], 1)
    forward[:, half] = np.cos(angle(n, [half]))[:, 0]
    twice = np.where(f == 0, 1.0, 2.0)[:, None] / D
    power = np.concatenate([twice * np.cos(angle(f, n)), 2.0 / D * np.cos(angle(f, n))], 0)
    back = np.concatenate([twice * np.cos(angle(f, n)), -2.0 / D * np.sin(angle(f, n))], 0)
    power[half] = back[half] = np.cos(angle([half], n))[0] / D
    return in_pieces(forward * 2.0 ** 10), in_pieces(power[:, :LAGS] * 2.0 ** 18), in_pieces(back * 2.0 ** 18)


_INS = ["L0_attn_x", "L0_attn_Wq", "L0_attn_Wkv", "L0_attn_Wo", "L0_attn_bo",
        "L0_ffn_gate_t", "L0_ffn_up_t", "L0_ffn_down_t", "L0_ffn_gate_s", "L0_ffn_up_s", "L0_ffn_down_s",
        "L1_ffn_gate_w", "L1_ffn_up_w", "L1_ffn_down_w", "L1_ffn_gate_a", "L1_ffn_gate_b",
        "L1_ffn_up_a", "L1_ffn_up_b", "L1_ffn_down_a", "L1_ffn_down_b"]
_OUTS = [((1, T, D), "float32")]


def kernel(**inputs):
    import numpy as _np
    import concourse.bacc as _bacc
    from concourse import mybir as _mybir
    from concourse.bass_utils import run_bass_kernel_spmd as _run

    nc = _bacc.Bacc("TRN2", target_bir_lowering=False, num_devices=1)
    arrays, args = {}, []

    def give(name, a):
        arrays[name] = a
        args.append(nc.dram_tensor(name, a.shape, _mybir.dt.from_np(a.dtype), kind="ExternalInput").ap())

    for name in _INS:
        give(f"in_{name}_dram", _np.ascontiguousarray(inputs[name]))
    for name, a in zip(("dft", "power", "inverse"), tables()):
        give(f"table_{name}_dram", a)
    for i, (shape, dtype) in enumerate(_OUTS):
        args.append(nc.dram_tensor(f"out_{i}_dram", shape, _mybir.dt.from_np(_np.dtype(dtype)), kind="ExternalOutput").ap())
    build(nc, *args)
    r = _run(nc, [arrays], core_ids=[0])
    return r.results[0]["out_0_dram"]
```

```python
from contextlib import ExitStack

import concourse.bass as bass
from concourse import mybir

P = 128
T, D = 1024, 512
NT, ND = T // P, D // P
H, G, HD = 32, 8, 16
REP = H // G
TERMS = ((0, 0), (0, 1), (1, 0), (1, 1), (0, 2), (2, 0))
QROWS = HD * len(TERMS)
MROWS = 3
RING = 3
LEAD = 5
UNITS = REP * (NT // 2) * 3
NEG = -1.0e30
LN_EPS = 1.0e-5

FF0, FF1, RANK = 1792, 1376, 16
N0, N1 = FF0 // P, -(-FF1 // P)
TAIL = FF1 - (N1 - 1) * P
FF1P = N1 * P
LAGS = D // 2 + 1
TOPK = 6
SENT = -3.0e38
PICKED = 3.0e38
CH, SUB = T // 2, 4

F32, F16, BF16, I32 = mybir.dt.float32, mybir.dt.float16, mybir.dt.bfloat16, mybir.dt.int32
ALU = mybir.AluOpType
ACT = mybir.ActivationFunctionType


def row_tile(pos):
    return NT - 1 - (pos - LEAD) % NT


def unit(pos, h, c):
    before = sum(REP * len(chunks(row_tile(i))) for i in range(pos))
    return before + len(chunks(row_tile(pos))) * h + c


def chunks(qt):
    if qt < NT // 2:
        return [(0, (qt + 1) * P, True)]
    return [(0, D, False), (D, (qt + 1) * P, True)]


class Chain:

    def __init__(self, engine, sem, base=0):
        self.engine, self.sem, self.n = engine, sem, base

    def later(self, instruction):
        self.n = self.n + 1
        instruction.then_inc(self.sem, 1)

    def settle(self):
        self.engine.wait_ge(self.sem, self.n)

    def __call__(self, instruction):
        self.later(instruction)
        self.settle()


def build(nc, x_in, Wq, Wkv, Wo, bo, gate_t, up_t, down_t, gate_s, up_s, down_s,
          gate_w, up_w, down_w, gate_a, gate_b, up_a, up_b, down_a, down_b, dft, power, inverse, out):
    with ExitStack() as ctx:
        def sb(name, shape, dt=F32):
            return ctx.enter_context(nc.sbuf_tensor(name, shape, dt))

        def sem(name):
            return ctx.enter_context(nc.semaphore(name))

        def dram(name, shape, dt=F32):
            return nc.dram_tensor(name, shape, dt, kind="Internal").ap()

        ARENA = 200
        arena = sb("arena", [P, ARENA * 256])

        def room(kib, shape, dt=F32):
            n = 1
            for k in shape:
                n *= k
            words = -(-n * (4 if dt in (F32, I32) else 2) // 4)
            start = int(kib * 256)
            assert start + words <= ARENA * 256
            v = arena[:, start:start + words]
            v = v if dt == F32 else v.bitcast(dt)
            names = "abcd"[:len(shape)]
            if len(shape) > 1:
                v = v.rearrange("p (" + " ".join(names) + ") -> p " + " ".join(names),
                                **{names[i]: shape[i] for i in range(len(shape))})
            return v

        x = room(0, [NT, D])
        pc = [room(16 + 4 * i, [2, T], BF16) for i in range(3)]
        res = room(28, [2, T])
        w0g = room(37, [ND, FF0], F16)
        w0u = room(51, [ND, FF0], F16)
        w0d = room(65, [N0, D], BF16)
        probs = room(80, [2, REP, T])
        qt6 = room(112, [RING, REP, T], BF16)
        kt6 = room(136, [G, T], BF16)
        ctxt = room(152, [ND, T])
        wo = room(168, [ND, D])
        osb = room(176, [T])
        recb = room(180, [T])
        ctxn = room(184, [T])
        vall = room(188, [NT, G, HD])
        junk = room(192, [REP, D], BF16)
        vcur = room(196, [NT, 32])
        strip = room(197, [D], BF16)
        wq = room(80, [ND, D])
        wkv = room(88, [ND, 2 * G * HD])
        wk = room(92, [ND, P])
        xnt = room(96, [ND, T])
        xn = room(152, [NT, D])
        prep_p = room(96, [2, 2, D])
        prep_n = room(104, [2, 4, D], F16)
        prep_dp = [room(174, [FF1]), room(29, [FF1])]
        prep_dn = [room(152, [2, FF1P], F16), room(157.5, [2, FF1P], F16)]
        prep_de = room(163, [FF1])
        prep_pw = room(168.5, [FF1])
        dft_sb = room(16, [2, ND, D], F16)
        pow_sb = room(24, [2, ND, LAGS], F16)
        inv_sb = room(28.5, [2, ND, D], F16)
        w1d = room(37, [2, N1, D], F16)
        spec = room(59, [2, ND, CH])
        sq = room(75, [2, CH])
        w1g = room(80, [2, ND, FF1], F16)
        w1u = room(101.5, [2, ND, FF1], F16)
        xt = room(123, [2, 2, ND, CH], F16)
        y = room(139, [SUB, D])
        corr = room(147, [2, D + 2])
        u_sb = room(147, [2, CH])
        wspec = room(152, [ND, CH])
        sqp = room(160, [2, ND, CH], F16)
        wt = room(168, [2, ND, CH], F16)
        nat = room(180, [SUB, 2, D], F16)
        hid = room(188, [2, 2, CH], F16)
        prod2 = room(188, [2, CH])
        hs = room(192, [2, CH])
        sg = room(196, [2, CH])
        expc = room(192, [2, D])
        picked = room(196, [D + 2])
        mx = sb("mx", [P, REP, NT])
        mx2 = sb("mx2", [P, REP, NT // 2])
        mr = sb("mr", [P, REP, NT])
        m3 = sb("m3", [P, P], BF16)
        mt = sb("mt", [P, P], BF16)
        dens = sb("dens", [P, 32])
        recs = sb("recs", [P, 32])
        ident = sb("ident", [P, P])
        stats = sb("stats", [P, NT, 6])
        mv = sb("mv", [P, NT, 2])
        var = sb("var", [P, NT])
        rstd = sb("rstd", [P, NT])
        nw = sb("nw", [P, 3, NT])

        qp_d = dram("qp_d", [3, H * HD, T], BF16)
        kp_d = dram("kp_d", [3, G * HD, T], BF16)
        mt_d = dram("mt_d", [G, P, P], BF16)
        den_d = dram("den_d", [G, REP, T])
        rec_d = dram("rec_d", [G, REP, T])

        ps = ctx.enter_context(nc.psum_tensor("ps", [P, 8, 512], F32))
        s_bank = lambda u: ps[:, u % 2, :]
        st_bank = lambda n: ps[:, 2 + 2 * (n % 2):4 + 2 * (n % 2), :]
        o_bank = ps[:, 6:8, :]
        o_flat = o_bank.rearrange("p b n -> p (b n)")

        x_loaded, wkv_loaded, wq_loaded, wo_loaded = [sem("x_loaded0"), sem("x_loaded1")], sem("wkv_loaded"), sem("wq_loaded"), sem("wo_loaded")
        ident_ready, ident_zero = sem("ident_ready"), sem("ident_zero")
        strip_ready = sem("strip_ready")
        dve_passed, pool_passed, sp_passed = sem("dve_passed"), sem("pool_passed"), sem("sp_passed")
        dve_chain, pool_chain = sem("dve_chain"), sem("pool_chain")
        xn_ready, xnt_psum, xnt_ready = sem("xn_ready"), sem("xnt_psum"), sem("xnt_ready")
        wk_ready = sem("wk_ready")
        proj_psum, v_psum, v_ready = sem("proj_psum"), sem("v_psum"), sem("v_ready")
        piece0, proj_free, pieces_ready, pieces_stored = sem("piece0"), sem("proj_free"), sem("pieces_ready"), [sem("pieces_stored0"), sem("pieces_stored1")]
        res_ready, piece1 = sem("res_ready"), sem("piece1")
        kt_loaded, qt_loaded, ones_ready = sem("kt_loaded"), sem("qt_loaded"), sem("ones_ready")
        s_ready, s_taken = sem("s_ready"), sem("s_taken")
        m3_ready, mt_ready, mt_stored, m_loaded = sem("m3_ready"), sem("mt_ready"), sem("mt_stored"), sem("m_loaded")
        st_ready, p_ready, masked, pv_done, vcur_ready = sem("st_ready"), sem("p_ready"), sem("masked"), sem("pv_done"), sem("vcur_ready")
        o_taken, den_stored, den_loaded = sem("o_taken"), sem("den_stored"), sem("den_loaded")
        rec_ready, rec_stored, rec_loaded = sem("rec_ready"), sem("rec_stored"), sem("rec_loaded")
        ctx_ready, ctx_stored, ctx_stored_last = sem("ctx_ready"), sem("ctx_stored"), sem("ctx_stored_last")
        out_done = sem("out_done")

        def rsqrt(link, n):
            v, r = var[:, 0:n], rstd[:, 0:n]
            link(nc.vector.tensor_scalar(r.bitcast(I32), v.bitcast(I32), -0.5, float(0x5F3759DF), ALU.mult, ALU.add))
            for _ in range(3):
                link(nc.vector.tensor_tensor(nw[:, 0, 0:n], r, r, ALU.mult))
                link(nc.vector.scalar_tensor_tensor(out=nw[:, 1, 0:n], in0=nw[:, 0, 0:n], scalar=-0.5, in1=v,
                                                    op0=ALU.mult, op1=ALU.mult))
                link(nc.vector.scalar_tensor_tensor(out=r, in0=nw[:, 1, 0:n], scalar=1.5, in1=r,
                                                    op0=ALU.add, op1=ALU.mult))

        XS, WS, TS = 2.0 ** 10, 2.0 ** 8, 2.0 ** 10
        EXPONENT = 0x7F800000

        y_ready, y_free = sem("y_ready"), sem("y_free")
        tr_done = [sem(f"tr_done{j}") for j in range(8)]
        nat_ready = sem("nat_ready")
        rows_loaded = sem("rows_loaded")
        scales0_loaded, scales0_ready = sem("scales0_loaded"), sem("scales0_ready")
        w0_cast = [sem(f"w0_cast{i}") for i in range(3)]
        w0_loaded = [sem(f"w0_loaded{i}") for i in range(3)]
        lora_added = sem("lora_added")
        lora_clear, lora_split, lora_stacked = sem("lora_clear"), sem("lora_split"), sem("lora_stacked")
        lora_w_loaded = [sem(f"lora_w_loaded{i}") for i in range(4)]
        lora_in, lora_ready, lora_taken = sem("lora_in"), sem("lora_ready"), sem("lora_taken")
        lora_stored = [sem(f"lora_stored{i}") for i in range(4)]
        prep_loaded = [sem("prep_loaded0"), sem("prep_loaded1")]
        prep_done = sem("prep_done")
        prep_stored = [sem("prep_stored0"), sem("prep_stored1")]
        exps_ready, pw_stored, pw_loaded = sem("exps_ready"), sem("pw_stored"), sem("pw_loaded")
        prep_chain = sem("prep_chain")
        pd_loaded, pd_done, pd_stored = [sem("pd_loaded0"), sem("pd_loaded1")], sem("pd_done"), [sem("pd_stored0"), sem("pd_stored1")]
        drow_stored, drow_loaded = sem("drow_stored"), sem("drow_loaded")
        w1_loaded = [sem(f"w1_loaded{i}") for i in range(3)]
        tables_loaded, inverse_loaded = sem("tables_loaded"), sem("inverse_loaded")
        gu_ready, gu_free, sg_ready, hs_ready, hi_ready, hid_ready, down_done = (
            sem("gu_ready"), sem("gu_free"), sem("sg_ready"), sem("hs_ready"), sem("hi_ready"), sem("hid_ready"), sem("down_done"))
        f_ready, f_taken, sq_ready, sqh_ready, sqp_ready, c_ready = (
            sem("f_ready"), sem("f_taken"), sem("sq_ready"), sem("sqh_ready"), sem("sqp_ready"), sem("c_ready"))
        top_ready, e_ready = sem("top_ready"), sem("e_ready")
        wf_ready, wf_taken, prod_ready, prodh_ready, prodp_ready = (
            sem("wf_ready"), sem("wf_taken"), sem("prod_ready"), sem("prodh_ready"), sem("prodp_ready"))
        f1_ready = sem("f1_ready")
        x_done, pick_done = sem("x_done"), sem("pick_done")

        w16_d = [dram("w0g_d", [FF0, D], F16), dram("w0u_d", [FF0, D], F16), dram("w0d_d", [D, FF0], BF16)]
        lora_d = dram("lora_d", [2, FF1, D])
        lorad_d = dram("lorad_d", [D, FF1])
        w1n_d = dram("w1n_d", [4, FF1, D], F16)
        w1dn_d = dram("w1dn_d", [2, D, FF1P], F16)
        pw_d = dram("pw_d", [FF1P])
        drow_d = dram("drow_d", [D])

        row_b = sb("row_b", [P, D], F32)
        sc0 = sb("sc0", [P, 4, N0])
        ex0 = sb("ex0", [P, 4, N0])
        e1 = sb("e1", [P, 2, N1])
        ie1 = sb("ie1", [P, 2, 1])
        gs1 = sb("gs1", [P, N1])
        r1 = sb("r1", [P, N1])
        pw1 = sb("pw1", [P, N1])
        f1 = sb("f1", [P, ND])
        top = sb("top", [P, 8])
        ntop = sb("ntop", [P, 2])
        etop = sb("etop", [P, 8])
        wsum = sb("wsum", [P, 8])
        rsum = sb("rsum", [P, 8])
        notdc = sb("notdc", [P, 1])

        NB = 2 * N1 + ND
        A_AT = (0, D, 2 * D)
        NA = 2 * D + FF1
        lora_a = room(112, [NA])
        lora_ares = room(122, [NA])
        lora_ap = room(37, [3, NA], BF16)
        lora_at = room(51.5, [NA], BF16)
        lora_bs = room(56.5, [NB, P], BF16)
        lora_bt = room(63, [NB, P], BF16)
        lora_b = room(69.5, [NB, RANK])
        lora_bres = room(71.25, [NB, RANK])
        lora_out = room(176, [4, D])
        lora_w = room(152, [4, D])
        lora_jobs = [(m, n, 0) for m in range(2) for n in range(N1)] + [(2, n, j) for n in range(ND) for j in range(4)]

        def height(m, n):
            return TAIL if m < 2 and n == N1 - 1 else P

        def sp_early(sp):
            sp.dma_start(sc0[:, 0, :], gate_s.rearrange("(n p) -> p n", p=P), allow_slow_non_contiguous=True).then_inc(scales0_loaded, 16)
            sp.dma_start(sc0[:, 1, :], up_s.rearrange("(n p) -> p n", p=P), allow_slow_non_contiguous=True).then_inc(scales0_loaded, 16)
            sp.dma_start(row_b[:, :], bo.rearrange("(a d) -> a d", a=1).broadcast_to([P, D])).then_inc(rows_loaded, 16)

        def sp_lora(sp):
            full = (N1 - 1) * P
            for m, b in enumerate((gate_b, up_b)):
                sp.dma_start(lora_b[:, m * N1:(m + 1) * N1 - 1, :], b[0:full, :].rearrange("(n p) r -> p n r", p=P)).then_inc(lora_in, 16)
                sp.dma_start(lora_b[0:TAIL, (m + 1) * N1 - 1, :], b[full:FF1, :]).then_inc(lora_in, 16)
            sp.dma_start(lora_b[:, 2 * N1:NB, :], down_b.rearrange("(n p) r -> p n r", p=P)).then_inc(lora_in, 16)
            for at, a in zip(A_AT, (gate_a, up_a, down_a)):
                sp.dma_start(lora_a[0:RANK, at:at + a.shape[1]], a).then_inc(lora_in, 16)

        def sp_lora_stack(sp):
            sp.wait_ge(lora_split, 1)
            sp.dma_start_transpose(lora_bt[:, :, :], lora_bs.rearrange("p n c -> p (n c)")).then_inc(lora_stacked, 16)
            for t, (_, piece) in enumerate(TERMS):
                sp.dma_start(lora_at[RANK * t:RANK * (t + 1), :], lora_ap[0:RANK, piece, :]).then_inc(lora_stacked, 16)

        def lora_tile(w, m, n, j):
            if m < 2:
                return w[m][n * P:n * P + height(m, n), :]
            return w[2][n * P:(n + 1) * P, j * (FF1 // 4):(j + 1) * (FF1 // 4)]

        def sp_weights0(sp, i):
            sp.wait_ge(w0_cast[i], 16)
            sp.dma_start_transpose((w0g, w0u, w0d)[i], w16_d[i]).then_inc(w0_loaded[i], 16)

        def transposes(sp, use, dst):
            for i in range(SUB):
                sp.wait_ge(nat_ready, SUB * use + i + 1)
                sp.dma_start_transpose(dst.rearrange("p i c n -> p (i c) n")[:, :, i * P:(i + 1) * P],
                                       nat[:, i, :, :].rearrange("p i d -> p (i d)")).then_inc(tr_done[use], 16)

        def prep_load(sp, ht, b, h):
            sp.dma_start(prep_p[0:h, b, :, :], lora_d[:, bass.ds(ht * P, h), :].rearrange("m p d -> p m d")).then_inc(prep_loaded[b], 16)

        def prep_store(sp, ht, b, h):
            sp.wait_ge(prep_done, 2 * (ht + 1))
            sp.dma_start(w1n_d[:, bass.ds(ht * P, h), :].rearrange("i p d -> p i d"), prep_n[0:h, b, :, :]).then_inc(prep_stored[b], 16)

        def down_load(sp, o):
            sp.dma_start(prep_dp[o % 2], lorad_d[o * P:(o + 1) * P, :]).then_inc(pd_loaded[o % 2], 16)

        def sp_rest(sp):
            all_lora_stored(sp)
            for ht in range(2):
                prep_load(sp, ht, ht, P)
            for c in range(2):
                transposes(sp, c, xt[:, c])
            sp.wait_ge(y_free, 4 * 2)
            sp.dma_start(row_b[:, :], down_s.rearrange("(a d) -> a d", a=1).broadcast_to([P, D])).then_inc(rows_loaded, 16)
            with sp.Fori(0, (N1 - 3) // 2) as pair:
                for b in range(2):
                    prep_store(sp, 2 * pair + b, b, P)
                    prep_load(sp, 2 * pair + b + 2, b, P)
            prep_store(sp, N1 - 3, 0, P)
            prep_load(sp, N1 - 1, 0, TAIL)
            prep_store(sp, N1 - 2, 1, P)
            prep_store(sp, N1 - 1, 0, TAIL)
            sp.wait_ge(exps_ready, 1)
            sp.dma_start(pw_d.rearrange("(n p) -> p n", p=P), pw1[:, :], allow_slow_non_contiguous=True).then_inc(pw_stored, 16)
            down_load(sp, 0)
            down_load(sp, 1)
            sp.dma_start(dft_sb, dft.rearrange("i (c p) n -> p i c n", p=P)).then_inc(tables_loaded, 16)
            sp.dma_start(pow_sb, power.rearrange("i (c p) n -> p i c n", p=P)).then_inc(tables_loaded, 16)
            sp.wait_ge(pw_stored, 16)
            sp.dma_start(prep_pw[:, :], pw_d[0:FF1].rearrange("(a n) -> a n", a=1).broadcast_to([P, FF1])).then_inc(pw_loaded, 16)
            sp.wait_ge(prep_stored[0], 16 * (N1 // 2 + 1))
            sp.wait_ge(prep_stored[1], 16 * (N1 // 2))
            for m, w in enumerate((w1g, w1u)):
                for piece in range(2):
                    sp.dma_start_transpose(w[:, piece], w1n_d[2 * m + piece]).then_inc(w1_loaded[m], 16)
            transposes(sp, 2, xt[:, 0])
            for o in range(ND):
                sp.wait_ge(pd_done, o + 1)
                sp.dma_start(w1dn_d[:, o * P:(o + 1) * P, :].rearrange("i p n -> p i n"), prep_dn[o % 2]).then_inc(pd_stored[o % 2], 16)
                if o + 2 < ND:
                    down_load(sp, o + 2)
            for b in range(2):
                sp.wait_ge(pd_stored[b], 16 * ND // 2)
            sp.wait_ge(f1_ready, 1)
            sp.dma_start(drow_d.rearrange("(n p) -> p n", p=P), f1[:, :], allow_slow_non_contiguous=True).then_inc(drow_stored, 16)
            sp.dma_start(inv_sb, inverse.rearrange("i (c p) n -> p i c n", p=P)).then_inc(inverse_loaded, 16)
            transposes(sp, 3, xt[:, 1])
            sp.wait_ge(gu_ready, 2 * N0)
            for piece in range(2):
                sp.dma_start_transpose(w1d[:, piece], w1dn_d[piece]).then_inc(w1_loaded[2], 16)
            sp.wait_ge(y_free, 4 * 4)
            sp.wait_ge(drow_stored, 16)
            sp.dma_start(row_b[:, :], drow_d.rearrange("(a d) -> a d", a=1).broadcast_to([P, D])).then_inc(drow_loaded, 16)
            transposes(sp, 4, wt)
            sp.wait_ge(wf_ready, 4)
            transposes(sp, 5, wt)
            transposes(sp, 6, xt[:, 0])
            transposes(sp, 7, xt[:, 1])
            for c in range(2):
                sp.wait_ge(x_done, c + 1)
                sp.dma_start(out[0].rearrange("(t p) d -> p t d", p=P)[:, SUB * c:SUB * (c + 1), :],
                             x[:, SUB * c:SUB * (c + 1), :]).then_inc(out_done, 16)
            sp.wait_ge(out_done, 32)

        def norm_add(dve, link, q, k, c, take, use):
            for i in range(SUB):
                dve.wait_ge(y_ready, SUB * q + i + 1)
                take(i).then_inc(y_free, 1)
                dve.wait_ge(y_free, SUB * k + i + 1)
                link.later(nc.vector.bn_stats(stats[:, i, :], y[:, i, :]))
            xc = x[:, SUB * c:SUB * (c + 1), :]

            def moments():
                link.settle()
                for i in range(SUB):
                    link.later(nc.vector.bn_aggr(mv[:, i, :], stats[:, i, :]))
                link.settle()
                link(nc.vector.tensor_scalar(var[:, 0:SUB], mv[:, 0:SUB, 1], LN_EPS, None, ALU.add))
                rsqrt(link, SUB)

            moments()
            for i in range(SUB):
                link.later(nc.vector.tensor_scalar(y[:, i, :], y[:, i, :], mv[:, i, 0:1], rstd[:, i:i + 1],
                                                   ALU.subtract, ALU.mult))
            link.settle()
            if use is None:
                nc.vector.tensor_tensor(xc, xc, y, ALU.add).then_inc(x_done, 1)
                dve.wait_ge(x_done, c + 1)
                return
            link(nc.vector.tensor_tensor(xc, xc, y, ALU.add))
            for i in range(SUB):
                link.later(nc.vector.bn_stats(stats[:, i, :], xc[:, i, :]))
            moments()
            link(nc.vector.tensor_scalar(rstd[:, 0:SUB], rstd[:, 0:SUB], XS, None, ALU.mult))
            for i in range(SUB):
                link.later(nc.vector.tensor_scalar(y[:, i, :], xc[:, i, :], mv[:, i, 0:1], rstd[:, i:i + 1],
                                                   ALU.subtract, ALU.mult))
            link.settle()
            pieces(dve, link, use, y)

        def pieces(dve, link, use, v):
            if use > 0:
                dve.wait_ge(tr_done[use - 1], 16 * SUB)
            for i in range(SUB):
                link.later(nc.vector.tensor_copy(nat[:, i, 0, :], v[:, i, :]))
            link.settle()
            for i in range(SUB):
                nc.vector.tensor_tensor(nat[:, i, 1, :], v[:, i, :], nat[:, i, 0, :], ALU.subtract).then_inc(nat_ready, 1)
            dve.wait_ge(nat_ready, SUB * (use + 1))

        def exponent(link, to, of, least):
            link(nc.vector.tensor_scalar(to.bitcast(I32), of.bitcast(I32), EXPONENT, None, ALU.bitwise_and))
            link(nc.vector.tensor_scalar(to, to, least, None, ALU.max))

        def inverse_of(link, to, of, shift):
            link(nc.vector.tensor_scalar(to.bitcast(I32), of.bitcast(I32), -1.0, float((254 + shift) << 23), ALU.mult, ALU.add))

        def lora_pieces(dve, link):
            dve.wait_ge(lora_in, 16 * 8)
            b, r, p = lora_b[:, :, :], lora_bres[:, :, :], lora_bs.rearrange("p n (s r) -> p n s r", r=RANK)
            slots = [[t for t in range(len(TERMS)) if TERMS[t][0] == piece] for piece in range(3)]
            a, ar = lora_a[0:RANK, :], lora_ares[0:RANK, :]
            ap = [lora_ap[0:RANK, i, :] for i in range(3)]
            link.later(nc.vector.tensor_copy(p[:, :, slots[0][0], :], b))
            link(nc.vector.tensor_copy(ap[0], a))
            link.later(nc.vector.tensor_tensor(r, b, p[:, :, slots[0][0], :], ALU.subtract))
            link(nc.vector.tensor_tensor(ar, a, ap[0], ALU.subtract))
            link.later(nc.vector.tensor_copy(p[:, :, slots[1][0], :], r))
            link(nc.vector.tensor_copy(ap[1], ar))
            link.later(nc.vector.tensor_tensor(p[:, :, slots[2][0], :], r, p[:, :, slots[1][0], :], ALU.subtract))
            for piece in range(2):
                for t in slots[piece][1:]:
                    link.later(nc.vector.tensor_copy(p[:, :, t, :], p[:, :, slots[piece][0], :]))
            link.settle()
            nc.vector.tensor_tensor(ap[2], ar, ap[1], ALU.subtract).then_inc(lora_split, 1)

        def scales0(dve, link):
            dve.wait_ge(scales0_loaded, 32)
            exponent(link, ex0[:, 0, :], sc0[:, 0, :], 2.0 ** -40)
            exponent(link, ex0[:, 1, :], sc0[:, 1, :], 2.0 ** -40)
            inverse_of(link, ex0[:, 2, :], ex0[:, 0, :], 0)
            inverse_of(link, ex0[:, 3, :], ex0[:, 1, :], 0)
            link(nc.vector.tensor_scalar(sc0[:, 2, :], sc0[:, 0, :], 1.0 / XS, None, ALU.mult))
            link(nc.vector.tensor_tensor(sc0[:, 3, :], sc0[:, 1, :], ex0[:, 2, :], ALU.mult))
            link(nc.vector.tensor_scalar(sc0[:, 3, :], sc0[:, 3, :], 1.0 / (32 * XS), None, ALU.mult))
            link(nc.vector.tensor_tensor(sc0[:, 3, :], sc0[:, 3, :], ex0[:, 3, :], ALU.mult))
            link(nc.vector.tensor_tensor(ex0[:, 0, :], ex0[:, 0, :], ex0[:, 1, :], ALU.mult))
            link(nc.vector.tensor_scalar(ex0[:, 0, :], ex0[:, 0, :], 32.0, None, ALU.mult))
            dve.wait_ge(w0_loaded[2], 16)
            for ht in range(N0):
                nc.vector.tensor_scalar(w0d[:, ht, :], w0d[:, ht, :], ex0[:, 0, ht:ht + 1], None, ALU.mult).then_inc(scales0_ready, 1)

        def prepare_hidden(dve, link):
            link(nc.vector.memset(e1[:, :, :], 1.0))

            def tile(ht, b, h, use):
                chain = Chain(dve, prep_chain, PREP_LINKS * ht)
                p, e = prep_p[0:h, b, :, :], e1[0:h, :, bass.ds(ht, 1)]
                dve.wait_ge(prep_loaded[b], 16 * (use + 1))
                chain(nc.vector.tensor_reduce(e, p, mybir.AxisListType.X, ALU.max, apply_absolute_value=True))
                exponent(chain, e, e, 2.0 ** -60)
                inverse_of(chain, ie1[0:h, :, :], e, 8)
                if not isinstance(use, int) or use > 0:
                    dve.wait_ge(prep_stored[b], 16 * use)
                for m in range(2):
                    chain.later(nc.vector.tensor_scalar(prep_n[0:h, b, 2 * m, :], p[:, m, :], ie1[0:h, m, :], None, ALU.mult))
                chain.settle()
                for m in range(2):
                    nc.vector.scalar_tensor_tensor(out=prep_n[0:h, b, 2 * m + 1, :], in0=p[:, m, :], scalar=ie1[0:h, m, :],
                                                   in1=prep_n[0:h, b, 2 * m, :], op0=ALU.mult, op1=ALU.subtract).then_inc(prep_done, 1)

            tile(0, 0, P, 0)
            tile(1, 1, P, 0)
            with dve.Fori(1, (N1 - 1) // 2) as pair:
                for b in range(2):
                    tile(2 * pair + b, b, P, pair)
            tile(N1 - 1, 0, TAIL, (N1 - 1) // 2)
            dve.wait_ge(prep_done, 2 * N1)
            link(nc.vector.tensor_scalar(gs1[:, :], e1[:, 0, :], 1.0 / (XS * WS), None, ALU.mult))
            inverse_of(link, r1[:, :], e1[:, 0, :], 0)
            link(nc.vector.tensor_scalar(r1[:, :], r1[:, :], 1.0 / (32 * XS * WS), None, ALU.mult))
            link(nc.vector.tensor_tensor(pw1[:, :], e1[:, 0, :], e1[:, 1, :], ALU.mult))
            nc.vector.tensor_scalar(pw1[:, :], pw1[:, :], 32.0, None, ALU.mult).then_inc(exps_ready, 1)

        PREP_LINKS = 6

        def prepare_down(dve, link):
            for b in range(2):
                link(nc.vector.memset(prep_dn[b][:, :, FF1:FF1P], 0.0))
            dve.wait_ge(pw_loaded, 16)
            for o in range(ND):
                b = o % 2
                dp, dn = prep_dp[b], prep_dn[b]
                dve.wait_ge(pd_loaded[b], 16 * (o // 2 + 1))
                link(nc.vector.tensor_tensor(prep_de[:, :], dp, prep_pw[:, :], ALU.mult))
                scaled_pieces(dve, link, prep_de[:, :], f1[:, o:o + 1], ie1[:, 0, :], dn[:, 0, 0:FF1], dn[:, 1, 0:FF1], pd_done,
                              (pd_stored[b], 16 * (o // 2)) if o >= 2 else None)
                dve.wait_ge(pd_done, o + 1)
            nc.vector.tensor_scalar(f1[:, :], f1[:, :], 1.0 / WS, None, ALU.mult).then_inc(f1_ready, 1)

        def scaled_pieces(dve, link, v, e, ie, high, low, done, stored):
            link(nc.vector.tensor_reduce(e, v, mybir.AxisListType.X, ALU.max, apply_absolute_value=True))
            exponent(link, e, e, 2.0 ** -60)
            inverse_of(link, ie, e, 8)
            if stored:
                dve.wait_ge(*stored)
            link(nc.vector.tensor_scalar(high, v, ie, None, ALU.mult))
            nc.vector.scalar_tensor_tensor(out=low, in0=v, scalar=ie, in1=high, op0=ALU.mult, op1=ALU.subtract).then_inc(done, 1)

        def top_lags(dve, link, c):
            for i in range(SUB):
                n = SUB * c + i
                dve.wait_ge(c_ready, n + 1)
                cr = corr[:, i % 2, :]
                p = ps[:, 4 + i, :]
                link(nc.vector.tensor_scalar(cr[:, 0:LAGS], p[:, 0:LAGS], 2.0 ** -14, None, ALU.mult))
                nc.vector.tensor_scalar(cr[:, LAGS:D], p[:, D - LAGS:0:-1], 2.0 ** -14, None, ALU.mult).then_inc(y_free, 1)
                dve.wait_ge(y_free, SUB * (4 + c) + i + 1)
                if n > 0:
                    dve.wait_ge(e_ready, n)
                link(nc.vector.max(out=top[:, :], in_=cr[:, 0:D]))
                link(nc.vector.tensor_scalar(ntop[:, 0:1], top[:, 0:1], -1.0, None, ALU.mult))
                nc.vector.memset(top[:, TOPK:8], SENT).then_inc(top_ready, 1)
                dve.wait_ge(top_ready, n + 1)
                link(nc.vector.match_replace(out=picked[:, :], in_to_replace=top[:, :], in_values=cr, imm_value=PICKED))
                dve.wait_ge(e_ready, n + 1)
                nc.vector.scalar_tensor_tensor(out=y[:, i, :], in0=picked[:, 0:D], scalar=PICKED, in1=expc[:, i % 2, :],
                                               op0=ALU.is_equal, op1=ALU.mult).then_inc(pick_done, 1)
                dve.wait_ge(pick_done, n + 1)
            link(nc.vector.tensor_scalar(y, y, TS, None, ALU.mult))
            pieces(dve, link, 4 + c, y)

        def spectra(dve, link, c):
            dve.wait_ge(wf_taken, 4 * (c + 1))
            half = ND // 2
            for j in range(half):
                a, b = spec[:, c, j, :], spec[:, c, half + j, :]
                al, be = wspec[:, j, :], wspec[:, half + j, :]
                t = y
                if c:
                    dve.wait_ge(prodp_ready, 2 * j + 2)
                link.later(nc.vector.tensor_tensor(t[:, 0, :], a, al, ALU.mult))
                link.later(nc.vector.tensor_tensor(t[:, 1, :], b, be, ALU.mult))
                link.later(nc.vector.tensor_tensor(t[:, 2, :], a, be, ALU.mult))
                link.later(nc.vector.tensor_tensor(t[:, 3, :], b, al, ALU.mult))
                link.settle()
                if j == 0:
                    nc.vector.scalar_tensor_tensor(out=prod[2 * j], in0=t[:, 1, :], scalar=notdc[:, 0:1], in1=t[:, 0, :],
                                                   op0=ALU.mult, op1=ALU.add).then_inc(prod_ready, 1)
                    link(nc.vector.tensor_tensor(prod[2 * j + 1], t[:, 2, :], t[:, 3, :], ALU.subtract))
                    nc.vector.tensor_copy(prod[1][0:1, :], t[0:1, 1, :]).then_inc(prod_ready, 1)
                else:
                    nc.vector.tensor_tensor(prod[2 * j], t[:, 0, :], t[:, 1, :], ALU.add).then_inc(prod_ready, 1)
                    nc.vector.tensor_tensor(prod[2 * j + 1], t[:, 2, :], t[:, 3, :], ALU.subtract).then_inc(prod_ready, 1)
                dve.wait_ge(prod_ready, 4 * c + 2 * j + 2)

        prod = [sq[:, 0, :], sq[:, 1, :], prod2[:, 0, :], prod2[:, 1, :]]

        def dve_rest(dve):
            link = Chain(dve, sem("dve_chain2"))
            scales0(dve, link)
            dve.wait_ge(rows_loaded, 16)

            def add_bias(i):
                return nc.vector.tensor_tensor(y[:, i, :], ps[:, 4 + i, :], row_b[:, :], ALU.add)

            def by_row_scale(i):
                return nc.vector.tensor_tensor(y[:, i, :], ps[:, 4 + i, :], row_b[:, :], ALU.mult)

            for c in range(2):
                norm_add(dve, link, c, c, c, add_bias, c)
            prepare_hidden(dve, link)
            dve.wait_ge(rows_loaded, 32)
            norm_add(dve, link, 2, 2, 0, by_row_scale, 2)
            prepare_down(dve, link)
            norm_add(dve, link, 3, 3, 1, by_row_scale, 3)
            link(nc.vector.memset(corr[:, :, D:D + 2], SENT))
            for c in range(2):
                top_lags(dve, link, c)
            dve.wait_ge(e_ready, 2 * SUB)
            link(nc.vector.reciprocal(rsum[:, :], wsum[:, :]))
            link(nc.vector.tensor_scalar(rsum[:, :], rsum[:, :], 2.0 ** -22, None, ALU.mult))
            link(nc.vector.memset(notdc[:, :], 1.0))
            link(nc.vector.memset(notdc[0:1, :], 0.0))
            for c in range(2):
                spectra(dve, link, c)
            for c in range(2):
                norm_add(dve, link, 4 + c, 6 + c, c,
                         lambda i: nc.vector.tensor_scalar(y[:, i, :], ps[:, 4 + i, :], rsum[:, SUB * c + i:SUB * c + i + 1],
                                                           None, ALU.mult), 6 + c)
            dve.wait_ge(drow_loaded, 16)
            for c in range(2):
                norm_add(dve, link, 6 + c, 8 + c, c, by_row_scale, None)

        def lora_load(act, k):
            src = lora_tile((gate_w, up_w, down_w), *lora_jobs[k])
            act.dma_start(lora_w[0:src.shape[0], k % 4, 0:src.shape[1]], src).then_inc(lora_w_loaded[k % 4], 16)

        def lora_store(act, k):
            act.wait_ge(lora_added, k + 1)
            dst = lora_tile((lora_d[0], lora_d[1], lorad_d), *lora_jobs[k])
            act.dma_start(dst, lora_out[0:dst.shape[0], k % 4, 0:dst.shape[1]]).then_inc(lora_stored[k % 4], 16)
            if k + 4 < len(lora_jobs):
                lora_load(act, k + 4)

        def lora_take(act, k):
            m, n, _ = lora_jobs[k]
            h, w = (height(m, n), D) if m < 2 else (P, FF1 // 4)
            act.wait_ge(lora_ready, k + 1)
            if k >= 4:
                act.wait_ge(lora_stored[k % 4], 16 * (k // 4))
            nc.scalar.copy(lora_out[0:h, k % 4, 0:w], ps[0:h, 6 + k % 2, 0:w]).then_inc(lora_taken, 1)
            if k >= 2:
                lora_store(act, k - 2)

        LORA_IN = {j: range(5 * (j - 2), 5 * (j - 1)) for j in range(2, 1 + ND)}
        LORA_LATE = range(LORA_IN[ND][-1] + 1, len(lora_jobs))

        def all_lora_stored(engine):
            for k in range(4):
                engine.wait_ge(lora_stored[k], 16 * len(lora_jobs[k::4]))

        L1_ORDER = ([("f", 0, i) for i in range(4)] + [("e", 0, 0), ("e", 0, 1), ("f", 1, 0), ("e", 0, 2), ("f", 1, 1),
                    ("f", 1, 2), ("e", 0, 3), ("f", 1, 3)] + [("e", 1, i) for i in range(4)])

        def spectrum(act, c, ft):
            k = 4 * c + ft
            act.wait_ge(f_ready, k + 1)
            nc.scalar.activation(spec[:, c, ft, :], ps[:, ft, :], ACT.Copy, scale=1.0 / (XS * TS)).then_inc(f_taken, 1)
            if k >= 2:
                act.wait_ge(sqp_ready, k - 1)
            nc.scalar.activation(sq[:, k % 2, :], ps[:, ft, :], ACT.Square, scale=1.0 / (4 * XS * TS)).then_inc(sq_ready, 1)
            if k >= 4:
                act.wait_ge(c_ready, 4)
            act.wait_ge(sq_ready, k + 1)
            nc.scalar.copy(sqp[:, 0, ft, :], sq[:, k % 2, :]).then_inc(sqh_ready, 1)

        def lag_terms(act, c, i):
            k = SUB * c + i
            act.wait_ge(top_ready, k + 1)
            nc.scalar.activation(etop[:, 0:TOPK], top[:, 0:TOPK], ACT.Exp, bias=ntop[:, 0:1],
                                 accum_out=wsum[:, k:k + 1]).then_inc(act_chain, 1)
            act.wait_ge(act_chain, k + 1)
            if k >= 2:
                act.wait_ge(pick_done, k - 1)
            nc.scalar.activation(expc[:, i % 2, :], corr[:, i % 2, 0:D], ACT.Exp, bias=ntop[:, 0:1]).then_inc(e_ready, 1)

        act_chain = sem("act_chain")

        def act_rest(act):
            act.wait_ge(scales0_ready, 1)
            for c in range(2):
                act_ffn(act, N0 * c, N0, lambda ht: sc0[:, 2, ht], lambda ht: sc0[:, 3, ht], P, c, 2 + c)
            act.wait_ge(f1_ready, 1)
            for b in range(2):
                act.wait_ge(pd_stored[b], 16 * ND // 2)
            for what, c, i in L1_ORDER:
                (spectrum if what == "f" else lag_terms)(act, c, i)
            for c in range(2):
                for ft in range(ND):
                    act.wait_ge(wf_ready, 4 * c + ft + 1)
                    if c:
                        act.wait_ge(prod_ready, 4)
                    nc.scalar.activation(wspec[:, ft, :], ps[:, ft, :], ACT.Copy, scale=16.0 / (TS * TS)).then_inc(wf_taken, 1)
                for k in range(4):
                    act.wait_ge(prod_ready, 4 * c + k + 1)
                    if c:
                        act.wait_ge(y_ready, 4 * SUB + SUB)
                    ft = (k // 2) + 2 * (k % 2)
                    nc.scalar.copy(sqp[:, 0, ft, :], prod[k]).then_inc(prodh_ready, 1)
            for c in range(2):
                act_ffn(act, 2 * N0 + N1 * c, N1, lambda ht: gs1[:, ht], lambda ht: r1[:, ht], TAIL, 2 + c, 6 + c)

        def act_ffn(act, base, tiles, gate_scale, up_scale, tail, before, q):
            def tile(ht, h, first):
                n = base + ht
                b = n % 2
                act.wait_ge(gu_ready, n + 1)
                if not first or base > 0:
                    act.wait_ge(hs_ready, n - 1)
                gsc, usc = gate_scale(bass.ds(ht, 1)), up_scale(bass.ds(ht, 1))
                nc.scalar.activation(sg[0:h, b, :], ps[0:h, 2 * b, :], ACT.Silu, scale=gsc[0:h, :]).then_inc(sg_ready, 1)
                nc.scalar.activation(u_sb[0:h, b, :], ps[0:h, 2 * b + 1, :], ACT.Copy, scale=usc[0:h, :]).then_inc(gu_free, 1)

            def high(ht, h, first):
                n = base + ht
                act.wait_ge(hs_ready, n + 1)
                if not first:
                    act.wait_ge(down_done, n - 1 - before)
                elif before:
                    act.wait_ge(y_ready, SUB * q)
                nc.scalar.copy(hid[0:h, 0, n % 2, :], hs[0:h, n % 2, :]).then_inc(hi_ready, 1)

            tile(0, P, True)
            tile(1, P, True)
            high(0, P, True)
            tile(2, P, False)
            high(1, P, True)
            with act.Fori(3, tiles - 1) as ht:
                tile(ht, P, False)
                high(ht - 1, P, False)
            tile(tiles - 1, tail, False)
            high(tiles - 2, P, False)
            high(tiles - 1, tail, False)

        def pool_lora(pool):
            for k, (m, n, j) in enumerate(lora_jobs):
                h, w = (height(m, n), D) if m < 2 else (P, FF1 // 4)
                pool.wait_ge(lora_taken, k + 1)
                pool.wait_ge(lora_w_loaded[k % 4], 16 * (k // 4 + 1))
                nc.gpsimd.tensor_tensor(lora_out[0:h, k % 4, 0:w], lora_out[0:h, k % 4, 0:w], lora_w[0:h, k % 4, 0:w],
                                        ALU.add).then_inc(lora_added, 1)

        def pool_rest(pool):
            for c in range(2):
                pool_ffn(pool, N0 * c, N0, P)
            for k in range(8):
                pool.wait_ge(sqh_ready, k + 1)
                if k >= 4:
                    pool.wait_ge(c_ready, 4)
                nc.gpsimd.tensor_tensor(sqp[:, 1, k % 4, :], sq[:, k % 2, :], sqp[:, 0, k % 4, :], ALU.subtract).then_inc(sqp_ready, 1)
            for c in range(2):
                for k in range(4):
                    pool.wait_ge(prodh_ready, 4 * c + k + 1)
                    ft = (k // 2) + 2 * (k % 2)
                    nc.gpsimd.tensor_tensor(sqp[:, 1, ft, :], prod[k], sqp[:, 0, ft, :], ALU.subtract).then_inc(prodp_ready, 1)
            for c in range(2):
                pool_ffn(pool, 2 * N0 + N1 * c, N1, TAIL)

        def pool_ffn(pool, base, tiles, tail):
            def product(ht, h, first):
                n = base + ht
                pool.wait_ge(gu_free, n + 1)
                pool.wait_ge(sg_ready, n + 1)
                if not first or base > 0:
                    pool.wait_ge(hid_ready, n - 1)
                    pool.wait_ge(hi_ready, n - 1)
                nc.gpsimd.tensor_tensor(hs[0:h, n % 2, :], sg[0:h, n % 2, :], u_sb[0:h, n % 2, :], ALU.mult).then_inc(hs_ready, 1)

            def low(ht, h, first):
                n = base + ht
                pool.wait_ge(hi_ready, n + 1)
                nc.gpsimd.tensor_tensor(hid[0:h, 1, n % 2, :], hs[0:h, n % 2, :], hid[0:h, 0, n % 2, :], ALU.subtract).then_inc(hid_ready, 1)

            product(0, P, True)
            product(1, P, True)
            low(0, P, True)
            product(2, P, False)
            low(1, P, True)
            with pool.Fori(3, tiles - 1) as ht:
                product(ht, P, False)
                low(ht - 1, P, False)
            product(tiles - 1, tail, False)
            low(tiles - 2, P, False)
            low(tiles - 1, tail, False)

        TWO = ((0, 0), (0, 1))
        THREE = ((0, 0), (0, 1), (1, 0))

        def lora_job(pe, k, m, n, j):
            if k >= 2:
                pe.wait_ge(lora_taken, k - 1)
            h, w = (height(m, n), D) if m < 2 else (P, FF1 // 4)
            nc.tensor.matmul(ps[0:h, 6 + k % 2, 0:w], lora_bt[0:QROWS, m * N1 + n, 0:h],
                             lora_at[0:QROWS, A_AT[m] + j * w:A_AT[m] + (j + 1) * w], start=True, stop=True).then_inc(lora_ready, 1)

        def pe_rest(pe):
            pe.wait_ge(wo_loaded, 32)
            pe.wait_ge(ctx_stored, 16 * REP * (G - 1))
            pe.wait_ge(p_ready, 32 * G)

            def out_rows(c, i, chunks_of_ctx):
                for kt in chunks_of_ctx:
                    last = nc.tensor.matmul(ps[:, 4 + i, :], ctxt[:, kt, (SUB * c + i) * P:(SUB * c + i + 1) * P], wo[:, kt, :],
                                            start=kt == 0, stop=kt == ND - 1)
                return last

            for i in range(SUB):
                if i == 2:
                    pe.wait_ge(o_taken, G)
                out_rows(0, i, range(ND - 1))
            pe.wait_ge(ctx_stored_last, 16 * REP)
            for i in range(SUB):
                out_rows(0, i, [ND - 1]).then_inc(y_ready, 1)
            for i in range(SUB):
                pe.wait_ge(y_free, i + 1)
                out_rows(1, i, range(ND)).then_inc(y_ready, 1)
            for i in range(3):
                pe.wait_ge(w0_loaded[i], 16)
            pe.wait_ge(scales0_ready, N0)
            for c in range(2):
                pe.wait_ge(tr_done[c], 16 * SUB)
                pe_ffn(pe, N0 * c, N0, P, c, 2 + c, lambda p: w0g, lambda p: w0u, lambda p: w0d, TWO, ((0, 0), (1, 0)))
            pe.wait_ge(tables_loaded, 32)
            pe.wait_ge(gu_free, 2 * N0)
            pe.wait_ge(sg_ready, 2 * N0)
            for c in range(2):
                pe.wait_ge(tr_done[2 + c], 16 * SUB)
                for ft in range(ND):
                    if c:
                        pe.wait_ge(sq_ready, ft + 1)
                    product(pe, ps[:, ft, :], lambda w, kt: dft_sb[:, w, kt, ft * P:(ft + 1) * P],
                            lambda r, kt: xt[:, c, r, kt, :], f_ready)
                pe.wait_ge(sqp_ready, 4 * (c + 1))
                for i in range(SUB):
                    pe.wait_ge(y_free, SUB * (3 + c) + i + 1)
                    product(pe, ps[:, 4 + i, 0:LAGS], lambda w, kt: sqp[:, w, kt, i * P:(i + 1) * P],
                            lambda r, kt: pow_sb[:, r, kt, :], c_ready)
            pe.wait_ge(sq_ready, 8)
            for c in range(2):
                pe.wait_ge(tr_done[4 + c], 16 * SUB)
                for ft in range(ND):
                    if c:
                        pe.wait_ge(wf_taken, ft + 1)
                    product(pe, ps[:, ft, :], lambda w, kt: dft_sb[:, w, kt, ft * P:(ft + 1) * P],
                            lambda r, kt: wt[:, r, kt, :], wf_ready)
            for c in range(2):
                pe.wait_ge(inverse_loaded, 16)
                pe.wait_ge(prodp_ready, 4 * (c + 1))
                for i in range(SUB):
                    pe.wait_ge(y_free, SUB * (5 + c) + i + 1)
                    product(pe, ps[:, 4 + i, :], lambda w, kt: sqp[:, w, kt, i * P:(i + 1) * P],
                            lambda r, kt: inv_sb[:, r, kt, :], y_ready)
            pe.wait_ge(w1_loaded[0], 32)
            pe.wait_ge(w1_loaded[1], 32)
            pe.wait_ge(w1_loaded[2], 32)
            pe.wait_ge(wf_taken, 8)
            for c in range(2):
                pe.wait_ge(tr_done[6 + c], 16 * SUB)
                pe_ffn(pe, 2 * N0 + N1 * c, N1, TAIL, c, 8 + c, lambda p: w1g[:, p], lambda p: w1u[:, p], lambda p: w1d[:, p],
                       THREE, ((0, 0), (1, 0), (0, 1)))

        def product(pe, to, lhs, rhs, ready):
            for kt in range(ND):
                for w, r in THREE:
                    last = nc.tensor.matmul(to, lhs(w, kt), rhs(r, kt), start=(kt, w, r) == (0, 0, 0),
                                            stop=(kt, w, r) == (ND - 1, 1, 0))
            last.then_inc(ready, 1)

        def pe_ffn(pe, base, tiles, tail, c, k, gate, up, down, terms, down_terms):
            def hidden(ht, h, first):
                n = base + ht
                if not first or base > 0:
                    pe.wait_ge(gu_free, n - 1)
                    pe.wait_ge(sg_ready, n - 1)
                for o, w in ((0, gate), (1, up)):
                    for kt in range(ND):
                        for t in terms:
                            last = nc.tensor.matmul(ps[0:h, 2 * (n % 2) + o, :], w(t[0])[:, kt, bass.ds(ht * P, h)],
                                                    xt[:, c, t[1], kt, :], start=(kt, t) == (0, terms[0]),
                                                    stop=(kt, t) == (ND - 1, terms[-1]))
                last.then_inc(gu_ready, 1)

            def out_of(ht, h, first, last_tile):
                n = base + ht
                pe.wait_ge(hid_ready, n + 1)
                for i in range(SUB):
                    if first:
                        pe.wait_ge(y_free, SUB * (k - 1) + i + 1)
                    for t in down_terms:
                        last = nc.tensor.matmul(ps[:, 4 + i, :], hid[0:h, t[0], n % 2, i * P:(i + 1) * P], down(t[1])[0:h, ht, :],
                                                start=first and t == down_terms[0], stop=last_tile and t == down_terms[-1])
                    if last_tile:
                        last.then_inc(y_ready, 1)
                if not last_tile:
                    last.then_inc(down_done, 1)

            hidden(0, P, True)
            hidden(1, P, True)
            hidden(2, P, False)
            out_of(0, P, True, False)
            with pe.Fori(3, tiles - 1) as ht:
                hidden(ht, P, False)
                out_of(ht - 2, P, False, False)
            hidden(tiles - 1, tail, False)
            out_of(tiles - 3, P, False, False)
            out_of(tiles - 2, P, False, False)
            out_of(tiles - 1, tail, False, True)


        block = ctx.enter_context(nc.Block())

        def for_groups(eng, body):
            body(eng, 0, 0)
            with eng.Fori(1, G - 2) as g:
                body(eng, g, 1)
            body(eng, G - 2, G - 2)
            body(eng, G - 1, G - 1)

        PATHS = "ddmdmdm"
        RECIPROCAL_STEP, NORM_STEP, OUT_STEP = 2, 4, (0, 1)

        def load_q(sp, g):
            for s, (qp, _) in enumerate(TERMS):
                src = qp_d[qp].rearrange("(g h d) t -> g d h t", g=G, h=REP)
                sp.dma_start(qt6[HD * s:HD * (s + 1), g % RING, :, :], src[g]).then_inc(qt_loaded, 16)

        def maxima_path(sp, g):
            sp.wait_ge(m3_ready, g + 1)
            sp.sem_inc(sp_passed)
            sp.dma_start_transpose(mt[:, :], m3[:, :]).then_inc(mt_ready, 16)
            yield
            sp.wait_ge(mt_ready, 16 * (g + 1))
            sp.dma_start(mt_d[g], mt[:, :]).then_inc(mt_stored, 16)
            yield
            sp.wait_ge(mt_stored, 16 * (g + 1))
            sp.dma_start(qt6[QROWS:QROWS + MROWS, g % RING, :, :],
                         mt_d[g, 0:MROWS * REP * NT, :].rearrange("(i r) q -> i (r q)", i=MROWS)
                         .rearrange("i (h t) -> i h t", h=REP)).then_inc(m_loaded, 16)
            yield

        def den_path(sp, g):
            sp.wait_ge(o_taken, g + 1)
            sp.dma_start(den_d[g], osb[HD:P:32, :]).then_inc(den_stored, 16)
            yield
            sp.wait_ge(den_stored, 16 * (g + 1))
            sp.dma_start(dens[:, :], den_d[g].rearrange("h (a b) -> (h a) b", b=32)).then_inc(den_loaded, 16)
            yield
            sp.wait_ge(rec_ready, g + 1)
            sp.dma_start(rec_d[g].rearrange("h (a b) -> (h a) b", b=32), recs[:, :]).then_inc(rec_stored, 16)
            yield
            sp.wait_ge(rec_stored, 16 * (g + 1))
            for h in range(REP):
                sp.dma_start(recb[32 * h:32 * h + 32, :], rec_d[g, h:h + 1, :].broadcast_to([32, T])).then_inc(rec_loaded, 16)
            yield

        def ctx_store(sp, g, upper, stored=None):
            sp.wait_ge(ctx_ready, g + 1)
            for h in range(REP):
                at = REP * HD * upper + HD * h
                sp.dma_start(ctxt[at:at + HD, g - ND * upper, :], ctxn[32 * h:32 * h + HD, :]).then_inc(stored or ctx_stored, 16)

        def sp_group(sp, g, shape, upper=0, w0=None):
            if shape < G - 2:
                if shape > 0:
                    sp.wait_ge(st_ready, 32 * g)
                else:
                    sp.wait_ge(qt_loaded, 2 * 16 * len(TERMS))
                load_q(sp, g + 2)
            m = maxima_path(sp, g + 1) if shape < G - 1 else iter(())
            d = den_path(sp, g - 1) if shape > 0 else iter(())
            for path in PATHS:
                next(m if path == "m" else d, None)
            if shape > 0:
                ctx_store(sp, g - 1, upper)
            if w0 is not None:
                if w0 == 1:
                    all_lora_stored(sp)
                sp_weights0(sp, w0)

        def normalise(pool, g):
            pool.wait_ge(rec_loaded, 16 * REP * (g + 1))
            if not isinstance(g, int) or g > 0:
                pool.wait_ge(ctx_stored, 16 * REP * g)
            nc.gpsimd.tensor_tensor(ctxn[:, :], osb[:, :], recb[:, :], ALU.mult).then_inc(ctx_ready, 1)

        def pool_group(pool, g, shape):
            for kt in range(NT):
                pool.wait_ge(p_ready, 32 * g + 4 * kt + 4)
                diag = probs[:, kt % 2, :, kt * P:(kt + 1) * P]
                pool.sem_inc(pool_passed)
                nc.gpsimd.affine_select(out=diag, in_=diag, compare_op=ALU.is_ge, fill=0.0, base=0,
                                        pattern=[[0, REP], [1, P]], channel_multiplier=-1).then_inc(masked, 1)
                if kt == 0:
                    if shape > 0:
                        pool.wait_ge(pv_done, NT * g)
                    nc.gpsimd.tensor_copy(vcur[:, :, 0:HD], vall[:, :, g, :]).then_inc(vcur_ready, 1)
                if kt == NORM_STEP and shape > 0:
                    normalise(pool, g - 1)

        def row_max(dve, g, pos, first):
            qt = row_tile(pos)
            for h in range(REP):
                for c, (k0, k1, diagonal) in enumerate(chunks(qt)):
                    u = unit(pos, h, c)
                    dve.wait_ge(s_ready, UNITS * g + u + 1)
                    w = k1 - k0
                    if diagonal:
                        to = mx[:, h, qt:qt + 1] if c == 0 else mx2[:, h, qt - NT // 2:qt - NT // 2 + 1]
                        if pos > 0:
                            dve.wait_ge(s_taken, UNITS * g + unit(pos - 1, h, len(chunks(row_tile(pos - 1))) - 1) + 1)
                        elif not first:
                            dve.wait_ge(s_taken, UNITS * (g - 1) + unit(NT - 1, h, len(chunks(row_tile(NT - 1))) - 1) + 1)
                        dve.sem_inc(dve_passed)
                        nc.vector.tensor_tensor_reduce(
                            out=junk[:, h, 0:w], in0=s_bank(u)[:, 0:w], in1=strip[:, D - w:D], scale=1.0, scalar=3.0 * NEG,
                            op0=ALU.add, op1=ALU.max, accum_out=to).then_inc(s_taken, 1)
                    else:
                        nc.vector.reduce_max(mx[:, h, qt:qt + 1], s_bank(u)[:, 0:w],
                                             mybir.AxisListType.X).then_inc(s_taken, 1)

        def max_pieces(dve, g):
            dve.wait_ge(s_taken, UNITS * (g + 1))
            n = Chain(dve, max_chain, 4 * g)
            half = NT // 2
            n(nc.vector.tensor_tensor(mx[:, :, half:NT], mx[:, :, half:NT], mx2[:, :, :], ALU.max))
            p3 = m3[:, 0:MROWS * REP * NT].rearrange("p (i h t) -> p i h t", i=MROWS, h=REP)
            if not isinstance(g, int) or g > 0:
                dve.wait_ge(mt_ready, 16 * g)
            n(nc.vector.tensor_scalar(p3[:, 0], mx[:, :, :], -1.0, None, ALU.mult))
            n(nc.vector.scalar_tensor_tensor(out=mr[:, :, :], in0=mx[:, :, :], scalar=-1.0, in1=p3[:, 0],
                                             op0=ALU.mult, op1=ALU.subtract))
            n(nc.vector.tensor_copy(p3[:, 1], mr[:, :, :]))
            nc.vector.tensor_tensor(p3[:, 2], mr[:, :, :], p3[:, 1], ALU.subtract).then_inc(m3_ready, 1)
            dve.wait_ge(m3_ready, g + 1)

        max_chain = sem("max_chain")

        def ahead(g, kt, shape):
            n = NT + kt + LEAD
            if shape + n // NT >= G:
                return None
            return g + n // NT, n % NT

        def reciprocals(dve, g):
            dve.wait_ge(den_loaded, 16 * (g + 1))
            if not isinstance(g, int) or g > 0:
                dve.wait_ge(rec_stored, 16 * g)
            nc.vector.reciprocal(recs[:, :], dens[:, :]).then_inc(rec_ready, 1)

        def dve_group(dve, g, shape):
            for kt in range(NT):
                to = ahead(g, kt, shape)
                if to:
                    row_max(dve, *to, False)
                    if to[1] == NT - 1:
                        max_pieces(dve, to[0])
                if kt == RECIPROCAL_STEP and shape > 0:
                    reciprocals(dve, g - 1)

        def take_o(act, g):
            act.wait_ge(pv_done, NT * (g + 1))
            if not isinstance(g, int) or g > 0:
                act.wait_ge(ctx_ready, g)
            nc.scalar.copy(osb[:, :], o_flat).then_inc(o_taken, 1)

        def act_group(act, g, shape):
            for kt in range(NT):
                for h in range(REP):
                    n = 32 * g + 4 * kt + h
                    act.wait_ge(st_ready, n + 1)
                    if h == 0 and (kt >= 2 or shape > 0):
                        act.wait_ge(pv_done, NT * g + kt - 1)
                    nc.scalar.activation(probs[:, kt % 2, h, kt * P:T],
                                         st_bank(h).rearrange("p b n -> p (b n)")[:, kt * P:T],
                                         ACT.Exp, scale=HD ** -0.5).then_inc(p_ready, 1)
                    if (kt, h) == OUT_STEP and shape > 0:
                        take_o(act, g - 1)

        def scores(pe, g, pos, h, c, first):
            qt = row_tile(pos)
            u = unit(pos, h, c)
            k0, k1, _ = chunks(qt)[c]
            if u == 0:
                pe.wait_ge(qt_loaded, 16 * len(TERMS) * (g + 1))
            if not first or u >= 2:
                pe.wait_ge(s_taken, UNITS * g + u - 1)
            nc.tensor.matmul(s_bank(u)[:, 0:k1 - k0], qt6[0:QROWS, g % RING, h, qt * P:(qt + 1) * P],
                             kt6[0:QROWS, g, k0:k1], start=True, stop=True).then_inc(s_ready, 1)

        def scores_t(pe, g, kt, h, b, shape):
            n = 4 * kt + h
            if b == kt // 4 and (shape > 0 or n >= 2):
                pe.wait_ge(p_ready, 32 * g + n - 1)
            q0, q1 = max(kt * P, b * 512), (b + 1) * 512
            last = nc.tensor.matmul(st_bank(h)[:, b, q0 - b * 512:512], kt6[0:QROWS + MROWS, g, kt * P:(kt + 1) * P],
                                    qt6[0:QROWS + MROWS, g % RING, h, q0:q1], start=True, stop=True)
            if b == 1:
                last.then_inc(st_ready, 1)

        def row_ranges(kt):
            return [(max(q, kt * P), q + 2 * P) for q in range(T - 2 * P, kt * P - 2 * P, -2 * P)]

        def weighted(pe, g, kt, i, shape):
            q0, q1 = row_ranges(kt)[i]
            b, last_range = q0 // 512, i == len(row_ranges(kt)) - 1
            if i == 0:
                pe.wait_ge(p_ready, 32 * g + 4 * kt + 4)
                if kt == 0:
                    pe.wait_ge(vcur_ready, g + 1)
                    if shape > 0:
                        pe.wait_ge(o_taken, g)
            if last_range:
                pe.wait_ge(masked, NT * g + kt + 1)
            for h in range(REP):
                last = nc.tensor.matmul(o_bank[32 * h:32 * h + 32, b, q0 - b * 512:q1 - b * 512], vcur[:, kt, :],
                                        probs[:, kt % 2, h, q0:q1], start=kt == 0 and q1 % 512 == 0, stop=(kt + 1) * P == (b + 1) * 512,
                                        tile_position=(0, 32 * h))
            if last_range:
                last.then_inc(pv_done, 1)

        def pe_group(pe, g, shape):
            pe.wait_ge(m_loaded, 16 * (g + 1))
            for kt in range(NT):
                to = ahead(g, kt, shape)
                halves = 2 if kt < NT // 2 else 1
                for slot in range(REP * halves):
                    h, half = divmod(slot, halves)
                    if to:
                        scores(pe, *to, h, half, False)
                    scores_t(pe, g, kt, h, half if halves == 2 else 1, shape)
                    if slot in SUM_SLOTS[kt]:
                        i = SUM_SLOTS[kt].index(slot)
                        if kt > 0:
                            weighted(pe, g, kt - 1, i, shape)
                        elif shape > 0:
                            weighted(pe, g - 1, NT - 1, i, 1)

        SUM_SLOTS = ((2,), (3, 4, 6, 7), (3, 4, 6, 7), (3, 5, 7), (1, 2, 3), (2, 3), (2, 3), (2,))

        @block.sync
        def _(sp):
            for half in range(2):
                sp.dma_start(x[:, 4 * half:4 * half + 4, :], x_in[0].rearrange("(t p) d -> p t d", p=P)[:, 4 * half:4 * half + 4, :]).then_inc(x_loaded[half], 16)
            sp.dma_start(wkv, Wkv.rearrange("(c p) n -> p c n", p=P)).then_inc(wkv_loaded, 16)
            sp.dma_start(wq, Wq.rearrange("(c p) n -> p c n", p=P)).then_inc(wq_loaded, 16)
            for upper in range(2):
                half = slice(upper * D // 2, (upper + 1) * D // 2)
                sp.dma_start(wo[upper * P // 2:(upper + 1) * P // 2, :, :],
                             Wo[half, :].rearrange("(c p) n -> p c n", p=P // 2)).then_inc(wo_loaded, 16)
            sp.wait_ge(lora_clear, 1)
            sp_lora(sp)
            sp_lora_stack(sp)
            for j in range(1 + ND):
                sp.wait_ge(pieces_ready, j + 1)
                for i in range(3):
                    dst = kp_d[i] if j == 0 else qp_d[i, (j - 1) * P:j * P, :]
                    sp.dma_start(dst, pc[i][:, j % 2, :]).then_inc(pieces_stored[j % 2], 16)
                if j == 0:
                    sp.wait_ge(pieces_stored[0], 48)
                    for s, (_, kp) in enumerate(TERMS):
                        sp.dma_start(kt6[HD * s:HD * (s + 1), :, :],
                                     kp_d[kp].rearrange("(g d) t -> d g t", g=G)).then_inc(kt_loaded, 16)
                if j == 1:
                    sp.wait_ge(pieces_stored[1], 48)
                    load_q(sp, 0)
                    sp.wait_ge(qt_loaded, 16 * len(TERMS))
            sp.wait_ge(pieces_stored[0], 48 * 3)
            sp.wait_ge(pieces_stored[1], 48 * 2)
            sp_early(sp)
            load_q(sp, 1)
            for _ in maxima_path(sp, 0):
                pass
            sp_group(sp, 0, 0, 0, 0)
            with sp.Fori(1, ND + 1) as g:
                sp_group(sp, g, 1)
            sp_group(sp, ND + 1, 1, 1, 1)
            sp_group(sp, G - 2, G - 2, 1, 2)
            sp_group(sp, G - 1, G - 1, 1)
            sp.wait_ge(pv_done, NT * G)
            for _ in den_path(sp, G - 1):
                pass
            ctx_store(sp, G - 1, 1, ctx_stored_last)
            sp_rest(sp)

        @block.gpsimd
        def _(pool):
            nc.gpsimd.memset(ident[:, :], 0.0).then_inc(ident_zero, 1)
            pool.wait_ge(ident_zero, 1)
            nc.gpsimd.affine_select(out=ident[:, :], in_=ident[:, :], compare_op=ALU.not_equal, fill=1.0,
                                    base=0, pattern=[[-1, P]], channel_multiplier=1).then_inc(ident_ready, 1)
            nc.gpsimd.memset(strip[:, :], 0.0).then_inc(pool_chain, 1)
            pool.wait_ge(pool_chain, 1)
            nc.gpsimd.affine_select(out=strip[:, D - P:D], in_=strip[:, D - P:D], compare_op=ALU.is_ge, fill=NEG,
                                    base=0, pattern=[[-1, P]], channel_multiplier=1).then_inc(strip_ready, 1)
            pool.wait_ge(x_loaded[1], 16)
            pool.dma_start(w16_d[0], gate_t).then_inc(w0_cast[0], 16)
            nc.gpsimd.memset(vcur[:, :, HD:HD + 1], 1.0).then_inc(pool_chain, 1)
            nc.gpsimd.memset(vcur[:, :, HD + 1:32], 0.0).then_inc(pool_chain, 1)
            pool.wait_ge(pool_chain, 3)
            nc.gpsimd.memset(kt6[QROWS:P, :, :], 1.0).then_inc(ones_ready, 1)
            pool.wait_ge(ones_ready, 1)
            pool.wait_ge(v_ready, 1)
            pool_lora(pool)
            pool.dma_start(w16_d[1], up_t).then_inc(w0_cast[1], 16)
            pool.dma_start(w16_d[2], down_t).then_inc(w0_cast[2], 16)
            for_groups(pool, pool_group)
            normalise(pool, G - 1)
            pool_rest(pool)

        @block.vector
        def _(dve):
            link = Chain(dve, dve_chain)
            link.later(nc.vector.memset(m3[:, :], 0.0))
            link.later(nc.vector.memset(lora_b[:, :, :], 0.0))
            link.later(nc.vector.memset(lora_bs[:, :, QROWS:P], 0.0))
            link.settle()
            nc.vector.memset(lora_bres[:, :, :], 0.0).then_inc(lora_clear, 1)
            dve.wait_ge(x_loaded[0], 16)
            for t in range(NT):
                if t == 4:
                    dve.wait_ge(x_loaded[1], 16)
                link.later(nc.vector.bn_stats(stats[:, t, :], x[:, t, :]))
            link.settle()
            for t in range(NT):
                link.later(nc.vector.bn_aggr(mv[:, t, :], stats[:, t, :]))
            link.settle()
            link(nc.vector.tensor_scalar(var[:, :], mv[:, :, 1], LN_EPS, None, ALU.add))
            rsqrt(link, NT)
            for t in range(NT):
                nc.vector.tensor_scalar(xn[:, t, :], x[:, t, :], mv[:, t, 0:1], rstd[:, t:t + 1],
                                        ALU.subtract, ALU.mult).then_inc(xn_ready, 1)
            lora_pieces(dve, link)
            EARLY = 1
            for j in range(1 + ND):
                if j == ND:
                    dve.wait_ge(strip_ready, 1)
                    for pos in range(EARLY):
                        row_max(dve, 0, pos, True)
                b = j % 2
                dve.wait_ge(piece0, j + 1)
                nc.vector.tensor_tensor(res[:, b, :], ps[:, 2 + 2 * b:4 + 2 * b, :].rearrange("p b n -> p (b n)"), pc[0][:, b, :],
                                        ALU.subtract).then_inc(res_ready, 1)
                dve.wait_ge(res_ready, j + 1)
                link(nc.vector.tensor_copy(pc[1][:, b, :], res[:, b, :]))
                nc.vector.tensor_tensor(pc[2][:, b, :], res[:, b, :], pc[1][:, b, :], ALU.subtract).then_inc(pieces_ready, 1)
            for pos in range(EARLY, NT):
                row_max(dve, 0, pos, True)
            max_pieces(dve, 0)
            for pos in range(LEAD):
                row_max(dve, 1, pos, False)
            for_groups(dve, dve_group)
            reciprocals(dve, G - 1)
            dve_rest(dve)

        @block.scalar
        def _(act):
            act.wait_ge(wkv_loaded, 16)
            nc.scalar.copy(wk.rearrange("p c (g d) -> p c g d", g=G),
                           wkv.rearrange("p c (g two d) -> p c g two d", g=G, two=2)[:, :, :, 0, :]).then_inc(wk_ready, 1)
            for t in range(NT):
                act.wait_ge(xnt_psum, t + 1)
                nc.scalar.copy(xnt[:, :, t * P:(t + 1) * P],
                               ps[:, t, :].rearrange("p (c q) -> p c q", c=ND)).then_inc(xnt_ready, 1)
            for j in range(1 + ND):
                for k in LORA_IN.get(j, ()):
                    lora_take(act, k)
                b = j % 2
                act.wait_ge(proj_psum, j + 1)
                if j >= 2:
                    act.wait_ge(pieces_stored[b], 48 * (j // 2))
                    act.wait_ge(pieces_ready, j - 1)
                nc.scalar.copy(pc[0][:, b, :], ps[:, 2 + 2 * b:4 + 2 * b, :].rearrange("p b n -> p (b n)")).then_inc(piece0, 1)
                if j == 0:
                    act.wait_ge(v_psum, 1)
                    nc.scalar.copy(vall[:, :, :, :].rearrange("p t g d -> p (t g d)"),
                                   ps[:, 6:8, :].rearrange("p b n -> p (b n)")).then_inc(v_ready, 1)
                    for k in range(4):
                        lora_load(act, k)
            for k in LORA_LATE:
                lora_take(act, k)
            for k in range(len(lora_jobs) - 2, len(lora_jobs)):
                lora_store(act, k)
            all_lora_stored(act)
            for_groups(act, act_group)
            take_o(act, G - 1)
            act_rest(act)

        @block.tensor
        def _(pe):
            pe.wait_ge(ident_ready, 1)
            for t in range(NT):
                pe.wait_ge(xn_ready, t + 1)
                for c in range(ND):
                    last = nc.tensor.transpose(ps[:, t, c * P:(c + 1) * P], xn[:, t, c * P:(c + 1) * P], ident[:, :])
                last.then_inc(xnt_psum, 1)
            pe.wait_ge(xnt_ready, NT)
            pe.wait_ge(wkv_loaded, 16)
            kvw = wkv.rearrange("p c (g two d) -> p c g two d", g=G, two=2)

            def project(j, weights, between):
                for half in range(2):
                    for c in range(ND):
                        last = nc.tensor.matmul(ps[:, 2 + 2 * (j % 2) + half, :], weights(c), xnt[:, c, half * 512:(half + 1) * 512],
                                                start=c == 0, stop=c == ND - 1)
                        if (half, c) == (1, ND - 1):
                            last.then_inc(proj_psum, 1)
                        between(half * ND + c)

            early = [(g, pos, h, c) for g, last_pos in ((0, NT), (1, LEAD)) for pos in range(last_pos)
                     for h in range(REP) for c in range(len(chunks(row_tile(pos))))]

            def early_scores():
                g, *rest = early.pop(0)
                scores(pe, g, *rest, g == 0)

            pe.wait_ge(wk_ready, 1)
            project(0, lambda c: wk[:, c, :], lambda i: None)
            for t in range(NT):
                for c in range(ND):
                    last = nc.tensor.matmul(ps[:, 6 + t // 4, (t % 4) * P:(t % 4 + 1) * P], xnt[:, c, t * P:(t + 1) * P],
                                            kvw[:, c, :, 1, :], start=c == 0, stop=c == ND - 1)
            last.then_inc(v_psum, 1)
            pe.wait_ge(wq_loaded, 16)
            for j in range(1, 1 + ND):
                if j >= 2:
                    pe.wait_ge(res_ready, j - 1)
                if j == 2:
                    pe.wait_ge(v_ready, 1)
                    pe.wait_ge(lora_stacked, 16 * 7)
                if j == ND:
                    pe.wait_ge(kt_loaded, 16 * len(TERMS))

                def between(i):
                    if j in LORA_IN and i < len(LORA_IN[j]):
                        lora_job(pe, LORA_IN[j][i], *lora_jobs[LORA_IN[j][i]])
                    if j == ND:
                        early_scores()

                project(j, lambda c: wq[:, c, (j - 1) * P:j * P], between)
            jobs = list(LORA_LATE)
            left = len(early)
            for i in range(left):
                early_scores()
                while (left - i) * len(LORA_LATE) < len(jobs) * left:
                    lora_job(pe, jobs[0], *lora_jobs[jobs.pop(0)])
            for k in jobs:
                lora_job(pe, k, *lora_jobs[k])
            pe.wait_ge(lora_taken, len(lora_jobs))
            pe.wait_ge(ones_ready, 1)
            pe.wait_ge(v_ready, 1)
            for_groups(pe, pe_group)
            weighted(pe, G - 1, NT - 1, 0, 1)
            pe_rest(pe)


def tables():
    import numpy as np
    n, half = np.arange(D), D // 2

    def angle(a, b):
        return 2 * np.pi * (np.outer(a, b) % D) / D

    def in_pieces(a):
        high = a.astype(np.float16)
        return np.stack([high, (a - high).astype(np.float16)])

    f = np.arange(half)
    forward = np.concatenate([np.cos(angle(n, f)), np.sin(angle(n, f))], 1)
    forward[:, half] = np.cos(angle(n, [half]))[:, 0]
    twice = np.where(f == 0, 1.0, 2.0)[:, None] / D
    power = np.concatenate([twice * np.cos(angle(f, n)), 2.0 / D * np.cos(angle(f, n))], 0)
    back = np.concatenate([twice * np.cos(angle(f, n)), -2.0 / D * np.sin(angle(f, n))], 0)
    power[half] = back[half] = np.cos(angle([half], n))[0] / D
    return in_pieces(forward * 2.0 ** 10), in_pieces(power[:, :LAGS] * 2.0 ** 18), in_pieces(back * 2.0 ** 18)


_INS = ["L0_attn_x", "L0_attn_Wq", "L0_attn_Wkv", "L0_attn_Wo", "L0_attn_bo",
        "L0_ffn_gate_t", "L0_ffn_up_t", "L0_ffn_down_t", "L0_ffn_gate_s", "L0_ffn_up_s", "L0_ffn_down_s",
        "L1_ffn_gate_w", "L1_ffn_up_w", "L1_ffn_down_w", "L1_ffn_gate_a", "L1_ffn_gate_b",
        "L1_ffn_up_a", "L1_ffn_up_b", "L1_ffn_down_a", "L1_ffn_down_b"]
_OUTS = [((1, T, D), "float32")]


def kernel(**inputs):
    import numpy as _np
    import concourse.bacc as _bacc
    from concourse import mybir as _mybir
    from concourse.bass_utils import run_bass_kernel_spmd as _run

    nc = _bacc.Bacc("TRN2", target_bir_lowering=False, num_devices=1)
    arrays, args = {}, []

    def give(name, a):
        arrays[name] = a
        args.append(nc.dram_tensor(name, a.shape, _mybir.dt.from_np(a.dtype), kind="ExternalInput").ap())

    for name in _INS:
        give(f"in_{name}_dram", _np.ascontiguousarray(inputs[name]))
    for name, a in zip(("dft", "power", "inverse"), tables()):
        give(f"table_{name}_dram", a)
    for i, (shape, dtype) in enumerate(_OUTS):
        args.append(nc.dram_tensor(f"out_{i}_dram", shape, _mybir.dt.from_np(_np.dtype(dtype)), kind="ExternalOutput").ap())
    build(nc, *args)
    r = _run(nc, [arrays], core_ids=[0])
    return r.results[0]["out_0_dram"]
```

```python
from contextlib import ExitStack

import concourse.bass as bass
from concourse import mybir

P = 128
T, D = 1024, 512
NT, ND = T // P, D // P
H, G, HD = 32, 8, 16
REP = H // G
TERMS = ((0, 0), (0, 1), (1, 0), (1, 1), (0, 2), (2, 0))
QROWS = HD * len(TERMS)
MROWS = 3
RING = 3
LEAD = 6
UNITS = REP * (NT // 2) * 3
NEG = -1.0e30
LN_EPS = 1.0e-5

FF0, FF1, RANK = 1792, 1376, 16
N0, N1 = FF0 // P, -(-FF1 // P)
TAIL = FF1 - (N1 - 1) * P
FF1P = N1 * P
LAGS = D // 2 + 1
TOPK = 6
SENT = -3.0e38
PICKED = 3.0e38
CH, SUB = T // 2, 4

F32, F16, BF16, I32 = mybir.dt.float32, mybir.dt.float16, mybir.dt.bfloat16, mybir.dt.int32
ALU = mybir.AluOpType
ACT = mybir.ActivationFunctionType


def row_tile(pos):
    return NT - 1 - (pos - LEAD) % NT


def unit(pos, h, c):
    before = sum(REP * len(chunks(row_tile(i))) for i in range(pos))
    return before + len(chunks(row_tile(pos))) * h + c


def chunks(qt):
    if qt < NT // 2:
        return [(0, (qt + 1) * P, True)]
    return [(0, D, False), (D, (qt + 1) * P, True)]


EARLY_UNITS = REP * len(chunks(row_tile(0)))
AHEAD_UNITS = UNITS + unit(LEAD, 0, 0)


class Chain:

    def __init__(self, engine, sem, base=0):
        self.engine, self.sem, self.n = engine, sem, base

    def later(self, instruction):
        self.n = self.n + 1
        instruction.then_inc(self.sem, 1)

    def settle(self):
        self.engine.wait_ge(self.sem, self.n)

    def __call__(self, instruction):
        self.later(instruction)
        self.settle()


def build(nc, x_in, Wq, Wkv, Wo, bo, gate_t, up_t, down_t, gate_s, up_s, down_s,
          gate_w, up_w, down_w, gate_a, gate_b, up_a, up_b, down_a, down_b, dft, power, inverse, out):
    with ExitStack() as ctx:
        def sb(name, shape, dt=F32):
            return ctx.enter_context(nc.sbuf_tensor(name, shape, dt))

        def sem(name):
            return ctx.enter_context(nc.semaphore(name))

        def dram(name, shape, dt=F32):
            return nc.dram_tensor(name, shape, dt, kind="Internal").ap()

        ARENA = 202.5
        arena = sb("arena", [P, int(ARENA * 256)])

        def room(kib, shape, dt=F32):
            n = 1
            for k in shape:
                n *= k
            words = -(-n * (4 if dt in (F32, I32) else 2) // 4)
            start = int(kib * 256)
            assert start + words <= ARENA * 256
            v = arena[:, start:start + words]
            v = v if dt == F32 else v.bitcast(dt)
            names = "abcd"[:len(shape)]
            if len(shape) > 1:
                v = v.rearrange("p (" + " ".join(names) + ") -> p " + " ".join(names),
                                **{names[i]: shape[i] for i in range(len(shape))})
            return v

        x = room(0, [NT, D])
        pc = [room(16 + 4 * i, [2, T], BF16) for i in range(3)]
        res = room(28, [2, T])
        w0g = room(37, [ND, FF0], F16)
        w0u = room(51, [ND, FF0], F16)
        w0d = room(65, [N0, D], BF16)
        probs = room(80, [2, REP, T])
        qt6 = room(112, [RING, REP, T], BF16)
        kt6 = room(136, [G, T], BF16)
        ctxt = room(152, [ND, T])
        wo = room(168, [ND, D])
        osb = room(176, [T])
        recb = room(180, [T])
        ctxn = room(184, [T])
        vall = room(188, [NT, G, HD])
        junk = room(192, [REP, D], BF16)
        vcur = room(196, [NT, 32])
        strip = room(197, [D], BF16)
        wq = room(80, [ND, D])
        wkv = room(88, [ND, 2 * G * HD])
        wk = room(92, [ND, P])
        xnt = room(96, [ND, T])
        xn = room(152, [NT, D])
        prep_p = room(96, [2, 2, D])
        prep_n = room(104, [2, 4, D], F16)
        prep_dp = room(29, [FF1])
        prep_dn = [room(80, [2, FF1P], F16), room(85.5, [2, FF1P], F16)]
        prep_de = room(91, [FF1])
        prep_pw = room(96.375, [FF1])
        dft_sb = room(16, [2, ND, D], F16)
        pow_sb = room(24, [2, ND, LAGS], F16)
        inv_sb = room(28.5, [2, ND, D], F16)
        w1d = room(37, [2, N1, D], F16)
        spec = [room(101.75, [ND, CH]), room(67.25, [ND, CH])]
        sq = [room(109.75, [2, CH]), room(75.25, [2, CH])]
        w1g = room(80, [2, ND, FF1], F16)
        w1u = room(101.5, [2, ND, FF1], F16)
        xt = room(123, [2, 2, ND, CH], F16)
        y = room(139, [SUB, D])
        corr = [room(113.75, [SUB, D + 2]), room(59, [SUB, D + 2])]
        u_sb = room(147, [2, CH])
        wspec = room(152, [ND, CH])
        sqp = room(160, [2, ND, CH], F16)
        wt = room(168, [2, ND, CH], F16)
        nat = room(180.25, [SUB, 2, D], F16)
        hid = room(188.25, [2, 2, CH], F16)
        hs = room(192.25, [2, CH])
        sg = room(196.25, [2, CH])
        expc = room(176, [2, D])
        picked = room(200.25, [D + 2])
        mx = sb("mx", [P, REP, NT])
        mx2 = sb("mx2", [P, REP, NT // 2])
        mr = sb("mr", [P, REP, NT])
        m3 = sb("m3", [P, P], BF16)
        mt = sb("mt", [P, P], BF16)
        dens = sb("dens", [P, 32])
        recs = sb("recs", [P, 32])
        ident = sb("ident", [P, P])
        stats = sb("stats", [P, NT, 6])
        mv = sb("mv", [P, NT, 2])
        var = sb("var", [P, NT])
        rstd = sb("rstd", [P, NT])
        nw = sb("nw", [P, 3, NT])

        qp_d = dram("qp_d", [3, H * HD, T], BF16)
        kp_d = dram("kp_d", [3, G * HD, T], BF16)
        mt_d = dram("mt_d", [G, P, P], BF16)
        den_d = dram("den_d", [G, REP, T])
        rec_d = dram("rec_d", [G, REP, T])

        ps = ctx.enter_context(nc.psum_tensor("ps", [P, 8, 512], F32))
        def s_bank(g, u):
            if isinstance(g, int) and EARLY_UNITS <= UNITS * g + u < AHEAD_UNITS:
                return ps[:, (UNITS * g + u) % 4, :]
            return ps[:, u % 2, :]

        st_bank = lambda n: ps[:, 2 + 2 * (n % 2):4 + 2 * (n % 2), :]
        o_bank = ps[:, 6:8, :]
        o_flat = o_bank.rearrange("p b n -> p (b n)")

        x_loaded = [sem("x_loaded0"), sem("x_loaded1")]
        wkv_loaded, wq_loaded, wo_loaded = sem("wkv_loaded"), sem("wq_loaded"), sem("wo_loaded")
        ident_ready, ident_zero = sem("ident_ready"), sem("ident_zero")
        strip_ready = sem("strip_ready")
        dve_passed, pool_passed, sp_passed = sem("dve_passed"), sem("pool_passed"), sem("sp_passed")
        dve_chain, late_chain, pool_chain = sem("dve_chain"), sem("late_chain"), sem("pool_chain")
        xn_ready, xnt_psum, xnt_ready = sem("xn_ready"), sem("xnt_psum"), sem("xnt_ready")
        wk_ready = sem("wk_ready")
        proj_psum, v_psum, v_ready = sem("proj_psum"), sem("v_psum"), sem("v_ready")
        piece0, res_ready, pieces_ready = sem("piece0"), sem("res_ready"), sem("pieces_ready")
        pieces_stored = [sem("pieces_stored0"), sem("pieces_stored1")]
        kt_loaded, qt_loaded, ones_ready = sem("kt_loaded"), sem("qt_loaded"), sem("ones_ready")
        s_ready, s_taken = sem("s_ready"), sem("s_taken")
        m3_ready, mt_ready, mt_stored, m_loaded = sem("m3_ready"), sem("mt_ready"), sem("mt_stored"), sem("m_loaded")
        st_ready, p_ready, masked, pv_done, vcur_ready = sem("st_ready"), sem("p_ready"), sem("masked"), sem("pv_done"), sem("vcur_ready")
        o_taken, den_stored, den_loaded = sem("o_taken"), sem("den_stored"), sem("den_loaded")
        rec_ready, rec_stored, rec_loaded = sem("rec_ready"), sem("rec_stored"), sem("rec_loaded")
        ctx_ready, ctx_stored, ctx_stored_last = sem("ctx_ready"), sem("ctx_stored"), sem("ctx_stored_last")
        out_done = sem("out_done")

        def rsqrt(link, n):
            v, r = var[:, 0:n], rstd[:, 0:n]
            link(nc.vector.tensor_scalar(r.bitcast(I32), v.bitcast(I32), -0.5, float(0x5F3759DF), ALU.mult, ALU.add))
            for _ in range(3):
                link(nc.vector.tensor_tensor(nw[:, 0, 0:n], r, r, ALU.mult))
                link(nc.vector.scalar_tensor_tensor(out=nw[:, 1, 0:n], in0=nw[:, 0, 0:n], scalar=-0.5, in1=v,
                                                    op0=ALU.mult, op1=ALU.mult))
                link(nc.vector.scalar_tensor_tensor(out=r, in0=nw[:, 1, 0:n], scalar=1.5, in1=r,
                                                    op0=ALU.add, op1=ALU.mult))

        XS, WS, TS = 2.0 ** 10, 2.0 ** 8, 2.0 ** 10
        EXPONENT = 0x7F800000

        y_ready, y_free = sem("y_ready"), sem("y_free")
        tr_done = [sem(f"tr_done{j}") for j in range(8)]
        nat_ready = sem("nat_ready")
        rows_loaded = sem("rows_loaded")
        scales0_loaded, scales0_ready = sem("scales0_loaded"), sem("scales0_ready")
        w0_cast = [sem(f"w0_cast{i}") for i in range(3)]
        w0_loaded = [sem(f"w0_loaded{i}") for i in range(3)]
        lora_added = sem("lora_added")
        lora_clear, lora_split, lora_stacked = sem("lora_clear"), sem("lora_split"), sem("lora_stacked")
        lora_w_loaded = [sem(f"lora_w_loaded{i}") for i in range(4)]
        lora_in, lora_ready, lora_taken = sem("lora_in"), sem("lora_ready"), sem("lora_taken")
        lora_stored = [sem(f"lora_stored{i}") for i in range(4)]
        prep_loaded = [sem("prep_loaded0"), sem("prep_loaded1")]
        prep_done = sem("prep_done")
        prep_stored = [sem("prep_stored0"), sem("prep_stored1")]
        exps_ready, pw_stored, pw_loaded = sem("exps_ready"), sem("pw_stored"), sem("pw_loaded")
        prep_chain = sem("prep_chain")
        pd_loaded, pd_used, pd_done, pd_stored = sem("pd_loaded"), sem("pd_used"), sem("pd_done"), [sem("pd_stored0"), sem("pd_stored1")]
        drow_stored, drow_loaded = sem("drow_stored"), sem("drow_loaded")
        w1_loaded = [sem(f"w1_loaded{i}") for i in range(3)]
        tables_loaded, inverse_loaded = sem("tables_loaded"), sem("inverse_loaded")
        gu_ready, gu_free, sg_ready, hs_ready, hi_ready, hid_ready, down_done = (
            sem("gu_ready"), sem("gu_free"), sem("sg_ready"), sem("hs_ready"), sem("hi_ready"), sem("hid_ready"), sem("down_done"))
        f_ready, f_taken, sq_ready, sqh_ready, sqp_ready, c_ready = (
            sem("f_ready"), sem("f_taken"), sem("sq_ready"), sem("sqh_ready"), sem("sqp_ready"), sem("c_ready"))
        top_ready, e_ready = sem("top_ready"), sem("e_ready")
        wf_ready, wf_taken, prod_ready, prodh_ready, prodp_ready = (
            sem("wf_ready"), sem("wf_taken"), sem("prod_ready"), sem("prodh_ready"), sem("prodp_ready"))
        f1_ready = sem("f1_ready")
        x_done, pick_done = sem("x_done"), sem("pick_done")

        w16_d = [dram("w0g_d", [FF0, D], F16), dram("w0u_d", [FF0, D], F16), dram("w0d_d", [D, FF0], BF16)]
        lora_d = dram("lora_d", [2, FF1, D])
        lorad_d = dram("lorad_d", [D, FF1])
        w1n_d = dram("w1n_d", [4, FF1, D], F16)
        w1dn_d = dram("w1dn_d", [2, D, FF1P], F16)
        pw_d = dram("pw_d", [FF1P])
        drow_d = dram("drow_d", [D])

        row_b = sb("row_b", [P, D], F32)
        sc0 = sb("sc0", [P, 4, N0])
        ex0 = sb("ex0", [P, 4, N0])
        e1 = sb("e1", [P, 2, N1])
        ie1 = sb("ie1", [P, 2, 1])
        gs1 = sb("gs1", [P, N1])
        r1 = sb("r1", [P, N1])
        pw1 = sb("pw1", [P, N1])
        f1 = sb("f1", [P, ND])
        top = sb("top", [P, 8])
        ntop = sb("ntop", [P, 2])
        etop = sb("etop", [P, 8])
        wsum = sb("wsum", [P, 8])
        rsum = sb("rsum", [P, 8])
        notdc = sb("notdc", [P, 1])

        NB = 2 * N1 + ND
        A_AT = (0, D, 2 * D)
        NA = 2 * D + FF1
        lora_a = room(112, [NA])
        lora_ares = room(122, [NA])
        lora_ap = room(37, [3, NA], BF16)
        lora_at = room(51.5, [NA], BF16)
        lora_bs = room(56.5, [NB, P], BF16)
        lora_bt = room(63, [NB, P], BF16)
        lora_b = room(69.5, [NB, RANK])
        lora_bres = room(71.25, [NB, RANK])
        lora_out = room(176, [4, D])
        lora_w = room(152, [4, D])
        lora_jobs = [(m, n, 0) for m in range(2) for n in range(N1)] + [(2, n, j) for n in range(ND) for j in range(4)]

        AT0 = {"rows": 5, "correlate": 7, "lags": 8, "spectrum": 13}
        AT1 = {"spectrum": 4, "pieces": 5, "back": 6}

        def bank(stage, c, i):
            if c and stage == "correlate":
                return 4 + i
            n = 2 * N0 + AT1.get(stage, 0) if c else N0 + AT0.get(stage, N0)
            return (2 * (n % 2) + i) % 4

        def height(m, n):
            return TAIL if m < 2 and n == N1 - 1 else P

        def sp_early(sp):
            sp.dma_start(sc0[:, 0, :], gate_s.rearrange("(n p) -> p n", p=P), allow_slow_non_contiguous=True).then_inc(scales0_loaded, 16)
            sp.dma_start(sc0[:, 1, :], up_s.rearrange("(n p) -> p n", p=P), allow_slow_non_contiguous=True).then_inc(scales0_loaded, 16)
            sp.dma_start(row_b[:, :], bo.rearrange("(a d) -> a d", a=1).broadcast_to([P, D])).then_inc(rows_loaded, 16)

        def sp_lora(sp):
            full = (N1 - 1) * P
            for m, b in enumerate((gate_b, up_b)):
                sp.dma_start(lora_b[:, m * N1:(m + 1) * N1 - 1, :], b[0:full, :].rearrange("(n p) r -> p n r", p=P)).then_inc(lora_in, 16)
                sp.dma_start(lora_b[0:TAIL, (m + 1) * N1 - 1, :], b[full:FF1, :]).then_inc(lora_in, 16)
            sp.dma_start(lora_b[:, 2 * N1:NB, :], down_b.rearrange("(n p) r -> p n r", p=P)).then_inc(lora_in, 16)
            for at, a in zip(A_AT, (gate_a, up_a, down_a)):
                sp.dma_start(lora_a[0:RANK, at:at + a.shape[1]], a).then_inc(lora_in, 16)

        def sp_lora_stack(sp):
            sp.wait_ge(lora_split, 1)
            sp.dma_start_transpose(lora_bt[:, :, :], lora_bs.rearrange("p n c -> p (n c)")).then_inc(lora_stacked, 16)
            for t, (_, piece) in enumerate(TERMS):
                sp.dma_start(lora_at[RANK * t:RANK * (t + 1), :], lora_ap[0:RANK, piece, :]).then_inc(lora_stacked, 16)

        def lora_tile(w, m, n, j):
            if m < 2:
                return w[m][n * P:n * P + height(m, n), :]
            return w[2][n * P:(n + 1) * P, j * (FF1 // 4):(j + 1) * (FF1 // 4)]

        def sp_weights0(sp, i):
            sp.wait_ge(w0_cast[i], 16)
            sp.dma_start_transpose((w0g, w0u, w0d)[i], w16_d[i]).then_inc(w0_loaded[i], 16)

        def transposes(sp, use, dst):
            for i in range(SUB):
                sp.wait_ge(nat_ready, SUB * use + i + 1)
                sp.dma_start_transpose(dst.rearrange("p i c n -> p (i c) n")[:, :, i * P:(i + 1) * P],
                                       nat[:, i, :, :].rearrange("p i d -> p (i d)")).then_inc(tr_done[use], 16)

        def prep_load(sp, ht, b, h):
            sp.dma_start(prep_p[0:h, b, :, :], lora_d[:, bass.ds(ht * P, h), :].rearrange("m p d -> p m d")).then_inc(prep_loaded[b], 16)

        def prep_store(sp, ht, b, h):
            sp.wait_ge(prep_done, 2 * (ht + 1))
            sp.dma_start(w1n_d[:, bass.ds(ht * P, h), :].rearrange("i p d -> p i d"), prep_n[0:h, b, :, :]).then_inc(prep_stored[b], 16)

        def down_load(sp, o):
            if o > 0:
                sp.wait_ge(pd_used, o)
            sp.dma_start(prep_dp, lorad_d[o * P:(o + 1) * P, :]).then_inc(pd_loaded, 16)

        def down_store(sp, o):
            sp.wait_ge(pd_done, o + 1)
            sp.dma_start(w1dn_d[:, o * P:(o + 1) * P, :].rearrange("i p n -> p i n"), prep_dn[o % 2]).then_inc(pd_stored[o % 2], 16)

        def sp_rest(sp):
            all_lora_stored(sp)
            for ht in range(2):
                prep_load(sp, ht, ht, P)
            for c in range(2):
                transposes(sp, c, xt[:, c])
            sp.wait_ge(y_free, 4 * 2)
            sp.dma_start(row_b[:, :], down_s.rearrange("(a d) -> a d", a=1).broadcast_to([P, D])).then_inc(rows_loaded, 16)
            with sp.Fori(0, (N1 - 3) // 2) as pair:
                for b in range(2):
                    prep_store(sp, 2 * pair + b, b, P)
                    prep_load(sp, 2 * pair + b + 2, b, P)
            prep_store(sp, N1 - 3, 0, P)
            prep_load(sp, N1 - 1, 0, TAIL)
            prep_store(sp, N1 - 2, 1, P)
            prep_store(sp, N1 - 1, 0, TAIL)
            sp.wait_ge(exps_ready, 1)
            sp.dma_start(pw_d.rearrange("(n p) -> p n", p=P), pw1[:, :], allow_slow_non_contiguous=True).then_inc(pw_stored, 16)
            down_load(sp, 0)
            sp.dma_start(dft_sb, dft.rearrange("i (c p) n -> p i c n", p=P)).then_inc(tables_loaded, 16)
            sp.dma_start(pow_sb, power.rearrange("i (c p) n -> p i c n", p=P)).then_inc(tables_loaded, 16)
            sp.wait_ge(pw_stored, 16)
            sp.dma_start(prep_pw[:, :], pw_d[0:FF1].rearrange("(a n) -> a n", a=1).broadcast_to([P, FF1])).then_inc(pw_loaded, 16)
            transposes(sp, 2, xt[:, 0])
            for o in range(2):
                down_load(sp, o + 1)
                down_store(sp, o)
            transposes(sp, 3, wt)
            down_load(sp, 3)
            for o in range(2, ND):
                down_store(sp, o)
            sp.wait_ge(pd_used, ND)
            sp.dma_start(inv_sb, inverse.rearrange("i (c p) n -> p i c n", p=P)).then_inc(inverse_loaded, 16)
            sp.wait_ge(f1_ready, 1)
            sp.dma_start(drow_d.rearrange("(n p) -> p n", p=P), f1[:, :], allow_slow_non_contiguous=True).then_inc(drow_stored, 16)
            for b in range(2):
                sp.wait_ge(pd_stored[b], 16 * ND // 2)
            sp.wait_ge(prep_stored[0], 16 * (N1 // 2 + 1))
            sp.wait_ge(prep_stored[1], 16 * (N1 // 2))
            for piece in range(2):
                sp.dma_start_transpose(w1g[:, piece], w1n_d[piece]).then_inc(w1_loaded[0], 16)
            sp.wait_ge(prodp_ready, 4)
            for piece in range(2):
                sp.dma_start_transpose(w1u[:, piece], w1n_d[2 + piece]).then_inc(w1_loaded[1], 16)
            transposes(sp, 4, xt[:, 1])
            sp.wait_ge(gu_ready, 2 * N0)
            for piece in range(2):
                sp.dma_start_transpose(w1d[:, piece], w1dn_d[piece]).then_inc(w1_loaded[2], 16)
            transposes(sp, 5, xt[:, 0])
            sp.wait_ge(y_free, 4 * 5)
            sp.wait_ge(drow_stored, 16)
            sp.dma_start(row_b[:, :], drow_d.rearrange("(a d) -> a d", a=1).broadcast_to([P, D])).then_inc(drow_loaded, 16)
            transposes(sp, 6, wt)
            transposes(sp, 7, xt[:, 1])
            for c in range(2):
                sp.wait_ge(x_done, c + 1)
                sp.dma_start(out[0].rearrange("(t p) d -> p t d", p=P)[:, SUB * c:SUB * (c + 1), :],
                             x[:, SUB * c:SUB * (c + 1), :]).then_inc(out_done, 16)
            sp.wait_ge(out_done, 32)

        def norm_add(dve, link, q, k, c, take, use):
            for i in range(SUB):
                dve.wait_ge(y_ready, SUB * q + i + 1)
                take(i).then_inc(y_free, 1)
                dve.wait_ge(y_free, SUB * k + i + 1)
                link.later(nc.vector.bn_stats(stats[:, i, :], y[:, i, :]))
            xc = x[:, SUB * c:SUB * (c + 1), :]

            def moments():
                link.settle()
                for i in range(SUB):
                    link.later(nc.vector.bn_aggr(mv[:, i, :], stats[:, i, :]))
                link.settle()
                link(nc.vector.tensor_scalar(var[:, 0:SUB], mv[:, 0:SUB, 1], LN_EPS, None, ALU.add))
                rsqrt(link, SUB)

            moments()
            for i in range(SUB):
                link.later(nc.vector.tensor_scalar(y[:, i, :], y[:, i, :], mv[:, i, 0:1], rstd[:, i:i + 1],
                                                   ALU.subtract, ALU.mult))
            link.settle()
            if use is None:
                nc.vector.tensor_tensor(xc, xc, y, ALU.add).then_inc(x_done, 1)
                dve.wait_ge(x_done, c + 1)
                return
            link(nc.vector.tensor_tensor(xc, xc, y, ALU.add))
            for i in range(SUB):
                link.later(nc.vector.bn_stats(stats[:, i, :], xc[:, i, :]))
            moments()
            link(nc.vector.tensor_scalar(rstd[:, 0:SUB], rstd[:, 0:SUB], XS, None, ALU.mult))
            for i in range(SUB):
                link.later(nc.vector.tensor_scalar(y[:, i, :], xc[:, i, :], mv[:, i, 0:1], rstd[:, i:i + 1],
                                                   ALU.subtract, ALU.mult))
            link.settle()
            pieces(dve, link, use, y)

        def pieces(dve, link, use, v):
            if use > 0:
                dve.wait_ge(tr_done[use - 1], 16 * SUB)
            for i in range(SUB):
                link.later(nc.vector.tensor_copy(nat[:, i, 0, :], v[:, i, :]))
            link.settle()
            for i in range(SUB):
                nc.vector.tensor_tensor(nat[:, i, 1, :], v[:, i, :], nat[:, i, 0, :], ALU.subtract).then_inc(nat_ready, 1)
            dve.wait_ge(nat_ready, SUB * (use + 1))

        def exponent(link, to, of, least):
            link(nc.vector.tensor_scalar(to.bitcast(I32), of.bitcast(I32), EXPONENT, None, ALU.bitwise_and))
            link(nc.vector.tensor_scalar(to, to, least, None, ALU.max))

        def inverse_of(link, to, of, shift):
            link(nc.vector.tensor_scalar(to.bitcast(I32), of.bitcast(I32), -1.0, float((254 + shift) << 23), ALU.mult, ALU.add))

        def lora_pieces(dve, link):
            dve.wait_ge(lora_in, 16 * 8)
            b, r, p = lora_b[:, :, :], lora_bres[:, :, :], lora_bs.rearrange("p n (s r) -> p n s r", r=RANK)
            slots = [[t for t in range(len(TERMS)) if TERMS[t][0] == piece] for piece in range(3)]
            a, ar = lora_a[0:RANK, :], lora_ares[0:RANK, :]
            ap = [lora_ap[0:RANK, i, :] for i in range(3)]
            link.later(nc.vector.tensor_copy(p[:, :, slots[0][0], :], b))
            link(nc.vector.tensor_copy(ap[0], a))
            link.later(nc.vector.tensor_tensor(r, b, p[:, :, slots[0][0], :], ALU.subtract))
            link(nc.vector.tensor_tensor(ar, a, ap[0], ALU.subtract))
            link.later(nc.vector.tensor_copy(p[:, :, slots[1][0], :], r))
            link(nc.vector.tensor_copy(ap[1], ar))
            link.later(nc.vector.tensor_tensor(p[:, :, slots[2][0], :], r, p[:, :, slots[1][0], :], ALU.subtract))
            for piece in range(2):
                for t in slots[piece][1:]:
                    link.later(nc.vector.tensor_copy(p[:, :, t, :], p[:, :, slots[piece][0], :]))
            link.settle()
            nc.vector.tensor_tensor(ap[2], ar, ap[1], ALU.subtract).then_inc(lora_split, 1)

        def scales0(dve, link):
            dve.wait_ge(scales0_loaded, 32)
            exponent(link, ex0[:, 0, :], sc0[:, 0, :], 2.0 ** -40)
            exponent(link, ex0[:, 1, :], sc0[:, 1, :], 2.0 ** -40)
            inverse_of(link, ex0[:, 2, :], ex0[:, 0, :], 0)
            inverse_of(link, ex0[:, 3, :], ex0[:, 1, :], 0)
            link(nc.vector.tensor_scalar(sc0[:, 2, :], sc0[:, 0, :], 1.0 / XS, None, ALU.mult))
            link(nc.vector.tensor_tensor(sc0[:, 3, :], sc0[:, 1, :], ex0[:, 2, :], ALU.mult))
            link(nc.vector.tensor_scalar(sc0[:, 3, :], sc0[:, 3, :], 1.0 / (32 * XS), None, ALU.mult))
            link(nc.vector.tensor_tensor(sc0[:, 3, :], sc0[:, 3, :], ex0[:, 3, :], ALU.mult))
            link(nc.vector.tensor_tensor(ex0[:, 0, :], ex0[:, 0, :], ex0[:, 1, :], ALU.mult))
            link(nc.vector.tensor_scalar(ex0[:, 0, :], ex0[:, 0, :], 32.0, None, ALU.mult))
            dve.wait_ge(w0_loaded[2], 16)
            for ht in range(N0):
                nc.vector.tensor_scalar(w0d[:, ht, :], w0d[:, ht, :], ex0[:, 0, ht:ht + 1], None, ALU.mult).then_inc(scales0_ready, 1)

        def prepare_hidden(dve, link):
            link(nc.vector.memset(e1[:, :, :], 1.0))

            def tile(ht, b, h, use):
                chain = Chain(dve, prep_chain, PREP_LINKS * ht)
                p, e = prep_p[0:h, b, :, :], e1[0:h, :, bass.ds(ht, 1)]
                dve.wait_ge(prep_loaded[b], 16 * (use + 1))
                chain(nc.vector.tensor_reduce(e, p, mybir.AxisListType.X, ALU.max, apply_absolute_value=True))
                exponent(chain, e, e, 2.0 ** -60)
                inverse_of(chain, ie1[0:h, :, :], e, 8)
                if not isinstance(use, int) or use > 0:
                    dve.wait_ge(prep_stored[b], 16 * use)
                for m in range(2):
                    chain.later(nc.vector.tensor_scalar(prep_n[0:h, b, 2 * m, :], p[:, m, :], ie1[0:h, m, :], None, ALU.mult))
                chain.settle()
                for m in range(2):
                    nc.vector.scalar_tensor_tensor(out=prep_n[0:h, b, 2 * m + 1, :], in0=p[:, m, :], scalar=ie1[0:h, m, :],
                                                   in1=prep_n[0:h, b, 2 * m, :], op0=ALU.mult, op1=ALU.subtract).then_inc(prep_done, 1)

            tile(0, 0, P, 0)
            tile(1, 1, P, 0)
            with dve.Fori(1, (N1 - 1) // 2) as pair:
                for b in range(2):
                    tile(2 * pair + b, b, P, pair)
            tile(N1 - 1, 0, TAIL, (N1 - 1) // 2)
            dve.wait_ge(prep_done, 2 * N1)
            link(nc.vector.tensor_scalar(gs1[:, :], e1[:, 0, :], 1.0 / (XS * WS), None, ALU.mult))
            inverse_of(link, r1[:, :], e1[:, 0, :], 0)
            link(nc.vector.tensor_scalar(r1[:, :], r1[:, :], 1.0 / (32 * XS * WS), None, ALU.mult))
            link(nc.vector.tensor_tensor(pw1[:, :], e1[:, 0, :], e1[:, 1, :], ALU.mult))
            nc.vector.tensor_scalar(pw1[:, :], pw1[:, :], 32.0, None, ALU.mult).then_inc(exps_ready, 1)

        PREP_LINKS = 6

        def prepare_down(dve, link, tiles):
            for o in tiles:
                dn = prep_dn[o % 2]
                if o < 2:
                    link(nc.vector.memset(dn[:, :, FF1:FF1P], 0.0))
                dve.wait_ge(pw_loaded, 16)
                dve.wait_ge(pd_loaded, 16 * (o + 1))
                nc.vector.tensor_tensor(prep_de[:, :], prep_dp, prep_pw[:, :], ALU.mult).then_inc(pd_used, 1)
                dve.wait_ge(pd_used, o + 1)
                scaled_pieces(dve, link, prep_de[:, :], f1[:, o:o + 1], ie1[:, 0, :], dn[:, 0, 0:FF1], dn[:, 1, 0:FF1], pd_done,
                              (pd_stored[o % 2], 16) if o >= 2 else None)
                dve.wait_ge(pd_done, o + 1)
            if tiles[-1] == ND - 1:
                nc.vector.tensor_scalar(f1[:, :], f1[:, :], 1.0 / WS, None, ALU.mult).then_inc(f1_ready, 1)

        def scaled_pieces(dve, link, v, e, ie, high, low, done, stored):
            link(nc.vector.tensor_reduce(e, v, mybir.AxisListType.X, ALU.max, apply_absolute_value=True))
            exponent(link, e, e, 2.0 ** -60)
            inverse_of(link, ie, e, 8)
            if stored:
                dve.wait_ge(*stored)
            link(nc.vector.tensor_scalar(high, v, ie, None, ALU.mult))
            nc.vector.scalar_tensor_tensor(out=low, in0=v, scalar=ie, in1=high, op0=ALU.mult, op1=ALU.subtract).then_inc(done, 1)

        def correlations(dve, link, c, i):
            dve.wait_ge(c_ready, SUB * c + i + 1)
            cr, p = corr[c][:, i, :], ps[:, bank("correlate", c, i), :]
            link(nc.vector.tensor_scalar(cr[:, 0:LAGS], p[:, 0:LAGS], 2.0 ** -14, None, ALU.mult))
            nc.vector.tensor_scalar(cr[:, LAGS:D], p[:, D - LAGS:0:-1], 2.0 ** -14, None, ALU.mult).then_inc(y_free, 1)
            dve.wait_ge(y_free, SUB * (3, 6)[c] + i + 1)

        def top_lags(dve, link, c, i):
            n = SUB * c + i
            cr = corr[c][:, i, :]
            if n > 0:
                dve.wait_ge(e_ready, n)
            link(nc.vector.max(out=top[:, :], in_=cr[:, 0:D]))
            link(nc.vector.tensor_scalar(ntop[:, 0:1], top[:, 0:1], -1.0, None, ALU.mult))
            nc.vector.memset(top[:, TOPK:8], SENT).then_inc(top_ready, 1)
            dve.wait_ge(top_ready, n + 1)
            link(nc.vector.match_replace(out=picked[:, :], in_to_replace=top[:, :], in_values=cr, imm_value=PICKED))
            dve.wait_ge(e_ready, n + 1)
            nc.vector.scalar_tensor_tensor(out=y[:, i, :], in0=picked[:, 0:D], scalar=PICKED, in1=expc[:, i % 2, :],
                                           op0=ALU.is_equal, op1=ALU.mult).then_inc(pick_done, 1)
            dve.wait_ge(pick_done, n + 1)

        def softmax_sums(dve, link, c):
            r = rsum[:, SUB * c:SUB * (c + 1)]
            dve.wait_ge(e_ready, SUB * (c + 1))
            link(nc.vector.reciprocal(r, wsum[:, SUB * c:SUB * (c + 1)]))
            link(nc.vector.tensor_scalar(r, r, 2.0 ** -22, None, ALU.mult))

        def spectra(dve, link, c):
            dve.wait_ge(wf_taken, 4 * (c + 1))
            dve.wait_ge(sqp_ready, 4 * (c + 1))
            half = ND // 2
            for j in range(half):
                a, b = spec[c][:, j, :], spec[c][:, half + j, :]
                al, be = wspec[:, j, :], wspec[:, half + j, :]
                t = y
                link.later(nc.vector.tensor_tensor(t[:, 0, :], a, al, ALU.mult))
                link.later(nc.vector.tensor_tensor(t[:, 1, :], b, be, ALU.mult))
                link.later(nc.vector.tensor_tensor(t[:, 2, :], a, be, ALU.mult))
                link.later(nc.vector.tensor_tensor(t[:, 3, :], b, al, ALU.mult))
                link.settle()
                if j == 0:
                    nc.vector.scalar_tensor_tensor(out=prod[c][2 * j], in0=t[:, 1, :], scalar=notdc[:, 0:1], in1=t[:, 0, :],
                                                   op0=ALU.mult, op1=ALU.add).then_inc(prod_ready, 1)
                    link(nc.vector.tensor_tensor(prod[c][2 * j + 1], t[:, 2, :], t[:, 3, :], ALU.subtract))
                    nc.vector.tensor_copy(prod[c][1][0:1, :], t[0:1, 1, :]).then_inc(prod_ready, 1)
                else:
                    nc.vector.tensor_tensor(prod[c][2 * j], t[:, 0, :], t[:, 1, :], ALU.add).then_inc(prod_ready, 1)
                    nc.vector.tensor_tensor(prod[c][2 * j + 1], t[:, 2, :], t[:, 3, :], ALU.subtract).then_inc(prod_ready, 1)
                dve.wait_ge(prod_ready, 4 * c + 2 * j + 2)

        prod = [[sq[c][:, 0, :], sq[c][:, 1, :], spec[c][:, 0, :], spec[c][:, ND // 2, :]] for c in range(2)]

        def dve_rest(dve):
            link = Chain(dve, late_chain)
            scales0(dve, link)
            dve.wait_ge(rows_loaded, 16)

            def add_bias(i):
                return nc.vector.tensor_tensor(y[:, i, :], ps[:, 4 + i, :], row_b[:, :], ALU.add)

            def by_row_scale(i):
                return nc.vector.tensor_tensor(y[:, i, :], ps[:, 4 + i, :], row_b[:, :], ALU.mult)

            for c in range(2):
                norm_add(dve, link, c, c, c, add_bias, c)
            prepare_hidden(dve, link)
            dve.wait_ge(rows_loaded, 32)
            norm_add(dve, link, 2, 2, 0, by_row_scale, 2)
            prepare_down(dve, link, (0, 1))
            link(nc.vector.memset(notdc[:, :], 1.0))
            link(nc.vector.memset(notdc[0:1, :], 0.0))

            def weights(c, use):
                link(nc.vector.memset(corr[c][:, :, D:D + 2], SENT))
                for i in range(SUB):
                    correlations(dve, link, c, i)
                for i in range(SUB):
                    top_lags(dve, link, c, i)
                pieces(dve, link, use, y)
                softmax_sums(dve, link, c)

            def rolled(c, k, use):
                norm_add(dve, link, 4 + c, k, c,
                         lambda i: nc.vector.tensor_scalar(y[:, i, :], ps[:, bank("back", c, i), :], rsum[:, SUB * c + i:SUB * c + i + 1],
                                                           None, ALU.mult), use)

            weights(0, 3)
            prepare_down(dve, link, (2, 3))
            spectra(dve, link, 0)
            norm_add(dve, link, 3, 4, 1, by_row_scale, 4)
            rolled(0, 5, 5)
            weights(1, 6)
            spectra(dve, link, 1)
            rolled(1, 7, 7)
            dve.wait_ge(drow_loaded, 16)
            for c in range(2):
                norm_add(dve, link, 6 + c, 8 + c, c, by_row_scale, None)

        def lora_bank(k):
            return 6 + k % 2 if k < LORA_LATE[0] else 4 + (k - LORA_LATE[0]) % 4

        def lora_load(act, k):
            src = lora_tile((gate_w, up_w, down_w), *lora_jobs[k])
            act.dma_start(lora_w[0:src.shape[0], k % 4, 0:src.shape[1]], src).then_inc(lora_w_loaded[k % 4], 16)

        def lora_store(act, k):
            act.wait_ge(lora_added, k + 1)
            dst = lora_tile((lora_d[0], lora_d[1], lorad_d), *lora_jobs[k])
            act.dma_start(dst, lora_out[0:dst.shape[0], k % 4, 0:dst.shape[1]]).then_inc(lora_stored[k % 4], 16)
            if k + 4 < len(lora_jobs):
                lora_load(act, k + 4)

        def lora_take(act, k):
            m, n, _ = lora_jobs[k]
            h, w = (height(m, n), D) if m < 2 else (P, FF1 // 4)
            act.wait_ge(lora_ready, k + 1)
            if k >= 4:
                act.wait_ge(lora_stored[k % 4], 16 * (k // 4))
            nc.scalar.copy(lora_out[0:h, k % 4, 0:w], ps[0:h, lora_bank(k), 0:w]).then_inc(lora_taken, 1)
            if k >= 2:
                lora_store(act, k - 2)

        LORA_IN = {j: range(4 * (j - 2), 4 * (j - 1)) for j in range(2, 1 + ND)}
        LORA_LATE = range(LORA_IN[ND][-1] + 1, len(lora_jobs))

        def all_lora_stored(engine):
            for k in range(4):
                engine.wait_ge(lora_stored[k], 16 * len(lora_jobs[k::4]))

        def spectrum(act, c, ft):
            k = 4 * c + ft
            act.wait_ge(f_ready, k + 1)
            nc.scalar.activation(spec[c][:, ft, :], ps[:, bank("rows", c, ft), :], ACT.Copy, scale=1.0 / (XS * TS)).then_inc(f_taken, 1)
            if k >= 2:
                act.wait_ge(sqp_ready, k - 1)
            nc.scalar.activation(sq[c][:, k % 2, :], ps[:, bank("rows", c, ft), :], ACT.Square, scale=1.0 / (4 * XS * TS)).then_inc(sq_ready, 1)
            if c:
                act.wait_ge(y_ready, 5 * SUB)
            act.wait_ge(sq_ready, k + 1)
            nc.scalar.copy(sqp[:, 0, ft, :], sq[c][:, k % 2, :]).then_inc(sqh_ready, 1)

        def lag_terms(act, c, i):
            k = SUB * c + i
            act.wait_ge(top_ready, k + 1)
            nc.scalar.activation(etop[:, 0:TOPK], top[:, 0:TOPK], ACT.Exp, bias=ntop[:, 0:1],
                                 accum_out=wsum[:, k:k + 1]).then_inc(act_chain, 1)
            act.wait_ge(act_chain, k + 1)
            if k >= 2:
                act.wait_ge(pick_done, k - 1)
            nc.scalar.activation(expc[:, i % 2, :], corr[c][:, i, 0:D], ACT.Exp, bias=ntop[:, 0:1]).then_inc(e_ready, 1)

        act_chain = sem("act_chain")

        def act_rest(act):
            act.wait_ge(scales0_ready, 1)
            act_ffn(act, 0, N0, lambda ht: sc0[:, 2, ht], lambda ht: sc0[:, 3, ht], P, 0, 2)

            def rows_spectrum(c):
                for ft in range(ND):
                    spectrum(act, c, ft)

            def first_spectrum():
                act.wait_ge(prep_stored[0], 16 * (N1 // 2 + 1))
                act.wait_ge(prep_stored[1], 16 * (N1 // 2))
                rows_spectrum(0)

            act_ffn(act, N0, N0, lambda ht: sc0[:, 2, ht], lambda ht: sc0[:, 3, ht], P, 1, 3,
                    {AT0["rows"]: first_spectrum, AT0["spectrum"]: lambda: weight_spectrum(act, 0),
                     **{AT0["lags"] + i: lambda i=i: lag_terms(act, 0, i) for i in range(SUB)}})
            product_high(act, 0)
            rows_spectrum(1)
            act_ffn(act, 2 * N0, N1, lambda ht: gs1[:, ht], lambda ht: r1[:, ht], TAIL, 2, 5,
                    {0: lambda: [lag_terms(act, 1, i) for i in range(SUB)], AT1["spectrum"]: lambda: weight_spectrum(act, 1),
                     AT1["pieces"]: lambda: product_high(act, 1)})
            act_ffn(act, 2 * N0 + N1, N1, lambda ht: gs1[:, ht], lambda ht: r1[:, ht], TAIL, 3, 7)

        def weight_spectrum(act, c):
            for ft in range(ND):
                act.wait_ge(wf_ready, 4 * c + ft + 1)
                if c:
                    act.wait_ge(prod_ready, 4)
                nc.scalar.activation(wspec[:, ft, :], ps[:, bank("spectrum", c, ft), :], ACT.Copy, scale=16.0 / TS).then_inc(wf_taken, 1)

        def product_high(act, c):
            act.wait_ge(c_ready, SUB * (c + 1))
            for k in range(4):
                act.wait_ge(prod_ready, 4 * c + k + 1)
                ft = (k // 2) + 2 * (k % 2)
                nc.scalar.copy(sqp[:, 0, ft, :], prod[c][k]).then_inc(prodh_ready, 1)

        def looped(engine, start, end, body):
            if end - start > 1:
                with engine.Fori(start, end) as ht:
                    body(ht)
            elif end > start:
                body(start)

        def all_tiles(engine, tiles, steps, inserts, first):
            start = first
            for at in sorted(inserts):
                if first <= at < tiles:
                    looped(engine, start, at, steps)
                    inserts[at]()
                    start = at
            looped(engine, start, tiles - 1, steps)

        def act_ffn(act, base, tiles, gate_scale, up_scale, tail, before, q, inserts={}):
            def tile(ht, h, first):
                n = base + ht
                b = n % 2
                act.wait_ge(gu_ready, n + 1)
                if not first or base > 0:
                    act.wait_ge(hs_ready, n - 1)
                gsc, usc = gate_scale(bass.ds(ht, 1)), up_scale(bass.ds(ht, 1))
                nc.scalar.activation(sg[0:h, b, :], ps[0:h, 2 * b, :], ACT.Silu, scale=gsc[0:h, :]).then_inc(sg_ready, 1)
                nc.scalar.activation(u_sb[0:h, b, :], ps[0:h, 2 * b + 1, :], ACT.Copy, scale=usc[0:h, :]).then_inc(gu_free, 1)

            def high(ht, h, first):
                n = base + ht
                act.wait_ge(hs_ready, n + 1)
                if not first:
                    act.wait_ge(down_done, n - 1 - before)
                elif before:
                    act.wait_ge(y_ready, SUB * q)
                nc.scalar.copy(hid[0:h, 0, n % 2, :], hs[0:h, n % 2, :]).then_inc(hi_ready, 1)

            def steps(ht):
                tile(ht, P, False)
                high(ht - 1, P, False)

            if 0 in inserts:
                inserts[0]()
            tile(0, P, True)
            tile(1, P, True)
            high(0, P, True)
            tile(2, P, False)
            high(1, P, True)
            all_tiles(act, tiles, steps, inserts, 3)
            tile(tiles - 1, tail, False)
            high(tiles - 2, P, False)
            high(tiles - 1, tail, False)

        def pool_lora(pool):
            for k, (m, n, j) in enumerate(lora_jobs):
                h, w = (height(m, n), D) if m < 2 else (P, FF1 // 4)
                pool.wait_ge(lora_taken, k + 1)
                pool.wait_ge(lora_w_loaded[k % 4], 16 * (k // 4 + 1))
                nc.gpsimd.tensor_tensor(lora_out[0:h, k % 4, 0:w], lora_out[0:h, k % 4, 0:w], lora_w[0:h, k % 4, 0:w],
                                        ALU.add).then_inc(lora_added, 1)

        def pool_rest(pool):
            pool_ffn(pool, 0, N0, P)
            pool_ffn(pool, N0, N0, P, {AT0["rows"]: lambda: power_low(pool, 0)})
            product_low(pool, 0)
            power_low(pool, 1)
            pool_ffn(pool, 2 * N0, N1, TAIL, {AT1["pieces"]: lambda: product_low(pool, 1)})
            pool_ffn(pool, 2 * N0 + N1, N1, TAIL)

        def power_low(pool, c):
            for ft in range(ND):
                pool.wait_ge(sqh_ready, 4 * c + ft + 1)
                nc.gpsimd.tensor_tensor(sqp[:, 1, ft, :], sq[c][:, ft % 2, :], sqp[:, 0, ft, :], ALU.subtract).then_inc(sqp_ready, 1)

        def product_low(pool, c):
            for k in range(4):
                pool.wait_ge(prodh_ready, 4 * c + k + 1)
                ft = (k // 2) + 2 * (k % 2)
                nc.gpsimd.tensor_tensor(sqp[:, 1, ft, :], prod[c][k], sqp[:, 0, ft, :], ALU.subtract).then_inc(prodp_ready, 1)

        def pool_ffn(pool, base, tiles, tail, inserts={}):
            def product(ht, h, first):
                n = base + ht
                pool.wait_ge(gu_free, n + 1)
                pool.wait_ge(sg_ready, n + 1)
                if not first or base > 0:
                    pool.wait_ge(hid_ready, n - 1)
                    pool.wait_ge(hi_ready, n - 1)
                nc.gpsimd.tensor_tensor(hs[0:h, n % 2, :], sg[0:h, n % 2, :], u_sb[0:h, n % 2, :], ALU.mult).then_inc(hs_ready, 1)

            def low(ht, h, first):
                n = base + ht
                pool.wait_ge(hi_ready, n + 1)
                nc.gpsimd.tensor_tensor(hid[0:h, 1, n % 2, :], hs[0:h, n % 2, :], hid[0:h, 0, n % 2, :], ALU.subtract).then_inc(hid_ready, 1)

            product(0, P, True)
            product(1, P, True)
            low(0, P, True)
            product(2, P, False)
            low(1, P, True)
            def steps(ht):
                product(ht, P, False)
                low(ht - 1, P, False)

            all_tiles(pool, tiles, steps, inserts, 3)
            product(tiles - 1, tail, False)
            low(tiles - 2, P, False)
            low(tiles - 1, tail, False)

        TWO = ((0, 0), (0, 1))
        THREE = ((0, 0), (0, 1), (1, 0))

        def lora_job(pe, k, m, n, j):
            if k < LORA_LATE[0]:
                if k >= 2:
                    pe.wait_ge(lora_taken, k - 1)
            elif k >= LORA_LATE[2]:
                pe.wait_ge(lora_taken, max(LORA_LATE[0], k - 3))
            h, w = (height(m, n), D) if m < 2 else (P, FF1 // 4)
            nc.tensor.matmul(ps[0:h, lora_bank(k), 0:w], lora_bt[0:QROWS, m * N1 + n, 0:h],
                             lora_at[0:QROWS, A_AT[m] + j * w:A_AT[m] + (j + 1) * w], start=True, stop=True).then_inc(lora_ready, 1)

        def pe_rest(pe):
            pe.wait_ge(wo_loaded, 32)
            pe.wait_ge(ctx_stored, 16 * REP * (G - 1))
            pe.wait_ge(p_ready, 32 * G)

            def out_rows(c, i, chunks_of_ctx):
                for kt in chunks_of_ctx:
                    last = nc.tensor.matmul(ps[:, 4 + i, :], ctxt[:, kt, (SUB * c + i) * P:(SUB * c + i + 1) * P], wo[:, kt, :],
                                            start=kt == 0, stop=kt == ND - 1)
                return last

            for i in range(SUB):
                if i == 2:
                    pe.wait_ge(o_taken, G)
                out_rows(0, i, range(ND - 1))
            pe.wait_ge(ctx_stored_last, 16 * REP)
            for i in range(SUB):
                out_rows(0, i, [ND - 1]).then_inc(y_ready, 1)
            for i in range(SUB):
                pe.wait_ge(y_free, i + 1)
                out_rows(1, i, range(ND)).then_inc(y_ready, 1)
            for i in range(3):
                pe.wait_ge(w0_loaded[i], 16)
            pe.wait_ge(scales0_ready, N0)
            def banks_free(n):
                pe.wait_ge(gu_free, n)
                pe.wait_ge(sg_ready, n)

            def rows_spectrum(c, free):
                pe.wait_ge(tr_done[(2, 4)[c]], 16 * SUB)
                for ft in range(ND):
                    free(ft)
                    product(pe, ps[:, bank("rows", c, ft), :], lambda w, kt: dft_sb[:, w, kt, ft * P:(ft + 1) * P],
                            lambda r, kt: xt[:, c, r, kt, :], f_ready)

            def correlate(c, free):
                pe.wait_ge(sqp_ready, 4 * (c + 1))
                for i in range(SUB):
                    free(i)
                    product(pe, ps[:, bank("correlate", c, i), 0:LAGS], lambda w, kt: sqp[:, w, kt, i * P:(i + 1) * P],
                            lambda r, kt: pow_sb[:, r, kt, :], c_ready)

            def weight_spectra(c, free):
                pe.wait_ge(tr_done[(3, 6)[c]], 16 * SUB)
                for ft in range(ND):
                    free(ft)
                    product(pe, ps[:, bank("spectrum", c, ft), :], lambda w, kt: dft_sb[:, w, kt, ft * P:(ft + 1) * P],
                            lambda r, kt: wt[:, r, kt, :], wf_ready)

            def back(c, free):
                pe.wait_ge(prodp_ready, 4 * (c + 1))
                for i in range(SUB):
                    free(i)
                    product(pe, ps[:, bank("back", c, i), :], lambda w, kt: sqp[:, w, kt, i * P:(i + 1) * P],
                            lambda r, kt: inv_sb[:, r, kt, :], y_ready)

            def stages(base, c, at):
                run = {}
                for ht, stage, taken, n in at:
                    def free(i, ht=ht):
                        if i % 2 == 0:
                            banks_free(base + ht - 1 + i // 2)

                    def before(stage=stage, free=free, taken=taken, n=n):
                        stage(c, free)
                        pe.wait_ge(taken, n - 2)
                    run.setdefault(ht, []).append(before)
                    run.setdefault(ht + 1, []).insert(0, lambda taken=taken, n=n: pe.wait_ge(taken, n))
                return {ht: lambda fs=fs: [f() for f in fs] for ht, fs in run.items()}

            pe.wait_ge(tr_done[0], 16 * SUB)
            pe_ffn(pe, 0, N0, P, 0, 2, lambda p: w0g, lambda p: w0u, lambda p: w0d, TWO, ((0, 0), (1, 0)))
            pe.wait_ge(tr_done[1], 16 * SUB)
            pe.wait_ge(tables_loaded, 32)
            pe_ffn(pe, N0, N0, P, 1, 3, lambda p: w0g, lambda p: w0u, lambda p: w0d, TWO, ((0, 0), (1, 0)),
                   stages(N0, 0, ((AT0["rows"], rows_spectrum, sq_ready, 4), (AT0["correlate"], correlate, y_free, 4 * SUB),
                                  (AT0["spectrum"], weight_spectra, wf_taken, 4))))
            banks_free(2 * N0)
            pe.wait_ge(inverse_loaded, 16)
            pe.wait_ge(wf_taken, 4)
            back(0, lambda i: None)
            rows_spectrum(1, lambda ft: pe.wait_ge(y_free, 5 * SUB + ft + 1))
            correlate(1, lambda i: pe.wait_ge(y_free, 4 * SUB + i + 1))
            for m in range(3):
                pe.wait_ge(w1_loaded[m], 32)
            pe.wait_ge(tr_done[5], 16 * SUB)
            w1 = lambda p: w1g[:, p], lambda p: w1u[:, p], lambda p: w1d[:, p]
            pe_ffn(pe, 2 * N0, N1, TAIL, 0, 7, *w1, THREE, ((0, 0), (1, 0), (0, 1)),
                   stages(2 * N0, 1, ((AT1["spectrum"], weight_spectra, wf_taken, 8), (AT1["back"], back, y_free, 8 * SUB))))
            pe.wait_ge(tr_done[7], 16 * SUB)
            pe_ffn(pe, 2 * N0 + N1, N1, TAIL, 1, 9, *w1, THREE, ((0, 0), (1, 0), (0, 1)))

        def product(pe, to, lhs, rhs, ready):
            for kt in range(ND):
                for w, r in THREE:
                    last = nc.tensor.matmul(to, lhs(w, kt), rhs(r, kt), start=(kt, w, r) == (0, 0, 0),
                                            stop=(kt, w, r) == (ND - 1, 1, 0))
            last.then_inc(ready, 1)

        def pe_ffn(pe, base, tiles, tail, c, k, gate, up, down, terms, down_terms, inserts={}):
            def hidden(ht, h, first):
                n = base + ht
                if not first or base > 0:
                    pe.wait_ge(gu_free, n - 1)
                    pe.wait_ge(sg_ready, n - 1)
                for o, w in ((0, gate), (1, up)):
                    for kt in range(ND):
                        for t in terms:
                            last = nc.tensor.matmul(ps[0:h, 2 * (n % 2) + o, :], w(t[0])[:, kt, bass.ds(ht * P, h)],
                                                    xt[:, c, t[1], kt, :], start=(kt, t) == (0, terms[0]),
                                                    stop=(kt, t) == (ND - 1, terms[-1]))
                last.then_inc(gu_ready, 1)

            def out_of(ht, h, first, last_tile):
                n = base + ht
                pe.wait_ge(hid_ready, n + 1)
                for i in range(SUB):
                    if first:
                        pe.wait_ge(y_free, SUB * (k - 1) + i + 1)
                    for t in down_terms:
                        last = nc.tensor.matmul(ps[:, 4 + i, :], hid[0:h, t[0], n % 2, i * P:(i + 1) * P], down(t[1])[0:h, ht, :],
                                                start=first and t == down_terms[0], stop=last_tile and t == down_terms[-1])
                    if last_tile:
                        last.then_inc(y_ready, 1)
                if not last_tile:
                    last.then_inc(down_done, 1)

            hidden(0, P, True)
            hidden(1, P, True)
            hidden(2, P, False)
            out_of(0, P, True, False)

            def steps(ht):
                hidden(ht, P, False)
                out_of(ht - 2, P, False, False)

            all_tiles(pe, tiles, steps, inserts, 3)
            hidden(tiles - 1, tail, False)
            out_of(tiles - 3, P, False, False)
            out_of(tiles - 2, P, False, False)
            out_of(tiles - 1, tail, False, True)

        block = ctx.enter_context(nc.Block())

        def for_groups(eng, body):
            body(eng, 0, 0)
            with eng.Fori(1, G - 2) as g:
                body(eng, g, 1)
            body(eng, G - 2, G - 2)
            body(eng, G - 1, G - 1)

        HOPS = (("den", 0), ("den", 1), ("max", 0), ("den", 2), ("max", 1), ("den", 3), ("max", 2))
        RECIPROCAL_STEP, NORM_STEP, OUT_STEP = 2, 4, (0, 1)

        def load_q(sp, g):
            for s, (qp, _) in enumerate(TERMS):
                src = qp_d[qp].rearrange("(g h d) t -> g d h t", g=G, h=REP)
                sp.dma_start(qt6[HD * s:HD * (s + 1), g % RING, :, :], src[g]).then_inc(qt_loaded, 16)

        def maxima_hop(sp, g, hop):
            if hop == 0:
                sp.wait_ge(m3_ready, g + 1)
                sp.sem_inc(sp_passed)
                sp.dma_start_transpose(mt[:, :], m3[:, :]).then_inc(mt_ready, 16)
            elif hop == 1:
                sp.wait_ge(mt_ready, 16 * (g + 1))
                sp.dma_start(mt_d[g], mt[:, :]).then_inc(mt_stored, 16)
            else:
                sp.wait_ge(mt_stored, 16 * (g + 1))
                sp.dma_start(qt6[QROWS:QROWS + MROWS, g % RING, :, :],
                             mt_d[g, 0:MROWS * REP * NT, :].rearrange("(i r) q -> i (r q)", i=MROWS)
                             .rearrange("i (h t) -> i h t", h=REP)).then_inc(m_loaded, 16)

        def den_hop(sp, g, hop):
            if hop == 0:
                sp.wait_ge(o_taken, g + 1)
                sp.dma_start(den_d[g], osb[HD:P:32, :]).then_inc(den_stored, 16)
            elif hop == 1:
                sp.wait_ge(den_stored, 16 * (g + 1))
                sp.dma_start(dens[:, :], den_d[g].rearrange("h (a b) -> (h a) b", b=32)).then_inc(den_loaded, 16)
            elif hop == 2:
                sp.wait_ge(rec_ready, g + 1)
                sp.dma_start(rec_d[g].rearrange("h (a b) -> (h a) b", b=32), recs[:, :]).then_inc(rec_stored, 16)
            else:
                sp.wait_ge(rec_stored, 16 * (g + 1))
                for h in range(REP):
                    sp.dma_start(recb[32 * h:32 * h + 32, :], rec_d[g, h:h + 1, :].broadcast_to([32, T])).then_inc(rec_loaded, 16)

        def ctx_store(sp, g, upper, stored=None):
            sp.wait_ge(ctx_ready, g + 1)
            for h in range(REP):
                at = REP * HD * upper + HD * h
                sp.dma_start(ctxt[at:at + HD, g - ND * upper, :], ctxn[32 * h:32 * h + HD, :]).then_inc(stored or ctx_stored, 16)

        def sp_group(sp, g, shape, upper=0, w0=None):
            if shape < G - 2:
                if shape > 0:
                    sp.wait_ge(st_ready, 32 * g)
                else:
                    sp.wait_ge(qt_loaded, 2 * 16 * len(TERMS))
                load_q(sp, g + 2)
            for path, hop in HOPS:
                if path == "den" and shape > 0:
                    den_hop(sp, g - 1, hop)
                if path == "max" and shape < G - 1:
                    maxima_hop(sp, g + 1, hop)
            if shape > 0:
                ctx_store(sp, g - 1, upper)
            if w0 is not None:
                if w0 == 1:
                    all_lora_stored(sp)
                sp_weights0(sp, w0)

        def normalise(pool, g):
            pool.wait_ge(rec_loaded, 16 * REP * (g + 1))
            if not isinstance(g, int) or g > 0:
                pool.wait_ge(ctx_stored, 16 * REP * g)
            nc.gpsimd.tensor_tensor(ctxn[:, :], osb[:, :], recb[:, :], ALU.mult).then_inc(ctx_ready, 1)

        def pool_group(pool, g, shape):
            for kt in range(NT):
                pool.wait_ge(p_ready, 32 * g + 4 * kt + 4)
                diag = probs[:, kt % 2, :, kt * P:(kt + 1) * P]
                pool.sem_inc(pool_passed)
                nc.gpsimd.affine_select(out=diag, in_=diag, compare_op=ALU.is_ge, fill=0.0, base=0,
                                        pattern=[[0, REP], [1, P]], channel_multiplier=-1).then_inc(masked, 1)
                if kt == 0:
                    if shape > 0:
                        pool.wait_ge(pv_done, NT * g)
                    nc.gpsimd.tensor_copy(vcur[:, :, 0:HD], vall[:, :, g, :]).then_inc(vcur_ready, 1)
                if kt == NORM_STEP and shape > 0:
                    normalise(pool, g - 1)

        def row_max(dve, g, pos, first):
            qt = row_tile(pos)
            for h in range(REP):
                for c, (k0, k1, diagonal) in enumerate(chunks(qt)):
                    u = unit(pos, h, c)
                    dve.wait_ge(s_ready, UNITS * g + u + 1)
                    w = k1 - k0
                    if diagonal:
                        to = mx[:, h, qt:qt + 1] if c == 0 else mx2[:, h, qt - NT // 2:qt - NT // 2 + 1]
                        if pos > 0:
                            dve.wait_ge(s_taken, UNITS * g + unit(pos - 1, h, len(chunks(row_tile(pos - 1))) - 1) + 1)
                        elif not first:
                            dve.wait_ge(s_taken, UNITS * (g - 1) + unit(NT - 1, h, len(chunks(row_tile(NT - 1))) - 1) + 1)
                        dve.sem_inc(dve_passed)
                        nc.vector.tensor_tensor_reduce(
                            out=junk[:, h, 0:w], in0=s_bank(g, u)[:, 0:w], in1=strip[:, D - w:D], scale=1.0, scalar=3.0 * NEG,
                            op0=ALU.add, op1=ALU.max, accum_out=to).then_inc(s_taken, 1)
                    else:
                        nc.vector.reduce_max(mx[:, h, qt:qt + 1], s_bank(g, u)[:, 0:w],
                                             mybir.AxisListType.X).then_inc(s_taken, 1)

        def max_pieces(dve, g):
            dve.wait_ge(s_taken, UNITS * (g + 1))
            n = Chain(dve, max_chain, 4 * g)
            half = NT // 2
            n(nc.vector.tensor_tensor(mx[:, :, half:NT], mx[:, :, half:NT], mx2[:, :, :], ALU.max))
            p3 = m3[:, 0:MROWS * REP * NT].rearrange("p (i h t) -> p i h t", i=MROWS, h=REP)
            if not isinstance(g, int) or g > 0:
                dve.wait_ge(mt_ready, 16 * g)
            n(nc.vector.tensor_scalar(p3[:, 0], mx[:, :, :], -1.0, None, ALU.mult))
            n(nc.vector.scalar_tensor_tensor(out=mr[:, :, :], in0=mx[:, :, :], scalar=-1.0, in1=p3[:, 0],
                                             op0=ALU.mult, op1=ALU.subtract))
            n(nc.vector.tensor_copy(p3[:, 1], mr[:, :, :]))
            nc.vector.tensor_tensor(p3[:, 2], mr[:, :, :], p3[:, 1], ALU.subtract).then_inc(m3_ready, 1)
            dve.wait_ge(m3_ready, g + 1)

        max_chain = sem("max_chain")

        def ahead(g, kt, shape):
            n = NT + kt + LEAD
            if shape + n // NT >= G:
                return None
            return g + n // NT, n % NT

        def reciprocals(dve, g):
            dve.wait_ge(den_loaded, 16 * (g + 1))
            if not isinstance(g, int) or g > 0:
                dve.wait_ge(rec_stored, 16 * g)
            nc.vector.reciprocal(recs[:, :], dens[:, :]).then_inc(rec_ready, 1)

        def dve_group(dve, g, shape):
            for kt in range(NT):
                to = ahead(g, kt, shape)
                if to:
                    row_max(dve, *to, False)
                    if to[1] == NT - 1:
                        max_pieces(dve, to[0])
                if kt == RECIPROCAL_STEP and shape > 0:
                    reciprocals(dve, g - 1)

        def take_o(act, g):
            act.wait_ge(pv_done, NT * (g + 1))
            if not isinstance(g, int) or g > 0:
                act.wait_ge(ctx_ready, g)
            nc.scalar.copy(osb[:, :], o_flat).then_inc(o_taken, 1)

        def act_group(act, g, shape):
            for kt in range(NT):
                for h in range(REP):
                    n = 32 * g + 4 * kt + h
                    act.wait_ge(st_ready, n + 1)
                    if h == 0 and (kt >= 2 or shape > 0):
                        act.wait_ge(pv_done, NT * g + kt - 1)
                    nc.scalar.activation(probs[:, kt % 2, h, kt * P:T],
                                         st_bank(h).rearrange("p b n -> p (b n)")[:, kt * P:T],
                                         ACT.Exp, scale=HD ** -0.5).then_inc(p_ready, 1)
                    if (kt, h) == OUT_STEP and shape > 0:
                        take_o(act, g - 1)

        def scores(pe, g, pos, h, c, first):
            qt = row_tile(pos)
            u = unit(pos, h, c)
            k0, k1, _ = chunks(qt)[c]
            if u == 0:
                pe.wait_ge(qt_loaded, 16 * len(TERMS) * (g + 1))
            n = UNITS * g + u
            if isinstance(g, int) and EARLY_UNITS <= n < AHEAD_UNITS:
                pe.wait_ge(s_taken, max(EARLY_UNITS, n - 3))
                if n < EARLY_UNITS + 4:
                    pe.wait_ge(res_ready, 1 + ND)
            elif not first or u >= 2:
                pe.wait_ge(s_taken, n - 1)
            nc.tensor.matmul(s_bank(g, u)[:, 0:k1 - k0], qt6[0:QROWS, g % RING, h, qt * P:(qt + 1) * P],
                             kt6[0:QROWS, g, k0:k1], start=True, stop=True).then_inc(s_ready, 1)

        def scores_t(pe, g, kt, h, b, shape):
            n = 4 * kt + h
            if b == kt // 4 and (shape > 0 or n >= 2):
                pe.wait_ge(p_ready, 32 * g + n - 1)
            q0, q1 = max(kt * P, b * 512), (b + 1) * 512
            last = nc.tensor.matmul(st_bank(h)[:, b, q0 - b * 512:512], kt6[0:QROWS + MROWS, g, kt * P:(kt + 1) * P],
                                    qt6[0:QROWS + MROWS, g % RING, h, q0:q1], start=True, stop=True)
            if b == 1:
                last.then_inc(st_ready, 1)

        def row_ranges(kt):
            return [(max(q, kt * P), q + 2 * P) for q in range(T - 2 * P, kt * P - 2 * P, -2 * P)]

        def weighted(pe, g, kt, i, shape):
            q0, q1 = row_ranges(kt)[i]
            b, last_range = q0 // 512, i == len(row_ranges(kt)) - 1
            if i == 0:
                pe.wait_ge(p_ready, 32 * g + 4 * kt + 4)
                if kt == 0:
                    pe.wait_ge(vcur_ready, g + 1)
                    if shape > 0:
                        pe.wait_ge(o_taken, g)
            if last_range:
                pe.wait_ge(masked, NT * g + kt + 1)
            for h in range(REP):
                last = nc.tensor.matmul(o_bank[32 * h:32 * h + 32, b, q0 - b * 512:q1 - b * 512], vcur[:, kt, :],
                                        probs[:, kt % 2, h, q0:q1], start=kt == 0 and q1 % 512 == 0, stop=(kt + 1) * P == (b + 1) * 512,
                                        tile_position=(0, 32 * h))
            if last_range:
                last.then_inc(pv_done, 1)

        def pe_group(pe, g, shape):
            pe.wait_ge(m_loaded, 16 * (g + 1))
            for kt in range(NT):
                to = ahead(g, kt, shape)
                halves = 2 if kt < NT // 2 else 1
                for slot in range(REP * halves):
                    h, half = divmod(slot, halves)
                    if to:
                        scores(pe, *to, h, half, False)
                    scores_t(pe, g, kt, h, half if halves == 2 else 1, shape)
                    if slot in SUM_SLOTS[kt]:
                        i = SUM_SLOTS[kt].index(slot)
                        if kt > 0:
                            weighted(pe, g, kt - 1, i, shape)
                        elif shape > 0:
                            weighted(pe, g - 1, NT - 1, i, 1)

        SUM_SLOTS = ((2,), (3, 4, 6, 7), (3, 4, 6, 7), (3, 5, 7), (1, 2, 3), (2, 3), (2, 3), (2,))

        @block.sync
        def _(sp):
            for half in range(2):
                sp.dma_start(x[:, 4 * half:4 * half + 4, :], x_in[0].rearrange("(t p) d -> p t d", p=P)[:, 4 * half:4 * half + 4, :]).then_inc(x_loaded[half], 16)
            sp.dma_start(wkv, Wkv.rearrange("(c p) n -> p c n", p=P)).then_inc(wkv_loaded, 16)
            sp.dma_start(wq, Wq.rearrange("(c p) n -> p c n", p=P)).then_inc(wq_loaded, 16)
            for upper in range(2):
                half = slice(upper * D // 2, (upper + 1) * D // 2)
                sp.dma_start(wo[upper * P // 2:(upper + 1) * P // 2, :, :],
                             Wo[half, :].rearrange("(c p) n -> p c n", p=P // 2)).then_inc(wo_loaded, 16)
            sp.wait_ge(lora_clear, 1)
            sp_lora(sp)
            sp_lora_stack(sp)
            for j in range(1 + ND):
                sp.wait_ge(pieces_ready, j + 1)
                for i in range(3):
                    dst = kp_d[i] if j == 0 else qp_d[i, (j - 1) * P:j * P, :]
                    sp.dma_start(dst, pc[i][:, j % 2, :]).then_inc(pieces_stored[j % 2], 16)
                if j == 0:
                    sp.wait_ge(pieces_stored[0], 48)
                    for s, (_, kp) in enumerate(TERMS):
                        sp.dma_start(kt6[HD * s:HD * (s + 1), :, :],
                                     kp_d[kp].rearrange("(g d) t -> d g t", g=G)).then_inc(kt_loaded, 16)
                if j == 1:
                    sp.wait_ge(pieces_stored[1], 48)
                    load_q(sp, 0)
                    sp.wait_ge(qt_loaded, 16 * len(TERMS))
            sp.wait_ge(pieces_stored[0], 48 * 3)
            sp.wait_ge(pieces_stored[1], 48 * 2)
            sp_early(sp)
            load_q(sp, 1)
            for hop in range(3):
                maxima_hop(sp, 0, hop)
            sp_group(sp, 0, 0, 0, 0)
            with sp.Fori(1, ND + 1) as g:
                sp_group(sp, g, 1)
            sp_group(sp, ND + 1, 1, 1, 1)
            sp_group(sp, G - 2, G - 2, 1, 2)
            sp_group(sp, G - 1, G - 1, 1)
            for hop in range(4):
                den_hop(sp, G - 1, hop)
            ctx_store(sp, G - 1, 1, ctx_stored_last)
            sp_rest(sp)

        @block.gpsimd
        def _(pool):
            nc.gpsimd.memset(ident[:, :], 0.0).then_inc(ident_zero, 1)
            pool.wait_ge(ident_zero, 1)
            nc.gpsimd.affine_select(out=ident[:, :], in_=ident[:, :], compare_op=ALU.not_equal, fill=1.0,
                                    base=0, pattern=[[-1, P]], channel_multiplier=1).then_inc(ident_ready, 1)
            nc.gpsimd.memset(strip[:, :], 0.0).then_inc(pool_chain, 1)
            pool.wait_ge(pool_chain, 1)
            nc.gpsimd.affine_select(out=strip[:, D - P:D], in_=strip[:, D - P:D], compare_op=ALU.is_ge, fill=NEG,
                                    base=0, pattern=[[-1, P]], channel_multiplier=1).then_inc(strip_ready, 1)
            pool.wait_ge(x_loaded[1], 16)
            pool.dma_start(w16_d[0], gate_t).then_inc(w0_cast[0], 16)
            nc.gpsimd.memset(vcur[:, :, HD:HD + 1], 1.0).then_inc(pool_chain, 1)
            nc.gpsimd.memset(vcur[:, :, HD + 1:32], 0.0).then_inc(pool_chain, 1)
            pool.wait_ge(pool_chain, 3)
            nc.gpsimd.memset(kt6[QROWS:P, :, :], 1.0).then_inc(ones_ready, 1)
            pool.wait_ge(ones_ready, 1)
            pool.wait_ge(v_ready, 1)
            pool_lora(pool)
            pool.dma_start(w16_d[1], up_t).then_inc(w0_cast[1], 16)
            pool.dma_start(w16_d[2], down_t).then_inc(w0_cast[2], 16)
            for_groups(pool, pool_group)
            normalise(pool, G - 1)
            pool_rest(pool)

        @block.vector
        def _(dve):
            link = Chain(dve, dve_chain)
            link.later(nc.vector.memset(m3[:, :], 0.0))
            link(nc.vector.memset(lora_b[:, :, :], 0.0))
            nc.vector.memset(lora_bs[:, :, QROWS:P], 0.0).then_inc(lora_clear, 1)
            dve.wait_ge(lora_clear, 1)
            dve.wait_ge(x_loaded[0], 16)
            for t in range(NT):
                if t == 4:
                    dve.wait_ge(x_loaded[1], 16)
                link.later(nc.vector.bn_stats(stats[:, t, :], x[:, t, :]))
            link.settle()
            for t in range(NT):
                link.later(nc.vector.bn_aggr(mv[:, t, :], stats[:, t, :]))
            link.settle()
            link(nc.vector.tensor_scalar(var[:, :], mv[:, :, 1], LN_EPS, None, ALU.add))
            rsqrt(link, NT)
            for t in range(NT):
                nc.vector.tensor_scalar(xn[:, t, :], x[:, t, :], mv[:, t, 0:1], rstd[:, t:t + 1],
                                        ALU.subtract, ALU.mult).then_inc(xn_ready, 1)
            lora_pieces(dve, link)
            for j in range(1 + ND):
                if j == ND:
                    dve.wait_ge(strip_ready, 1)
                    row_max(dve, 0, 0, True)
                b = j % 2
                dve.wait_ge(piece0, j + 1)
                nc.vector.tensor_tensor(res[:, b, :], ps[:, 2 + 2 * b:4 + 2 * b, :].rearrange("p b n -> p (b n)"), pc[0][:, b, :],
                                        ALU.subtract).then_inc(res_ready, 1)
                dve.wait_ge(res_ready, j + 1)
                link(nc.vector.tensor_copy(pc[1][:, b, :], res[:, b, :]))
                nc.vector.tensor_tensor(pc[2][:, b, :], res[:, b, :], pc[1][:, b, :], ALU.subtract).then_inc(pieces_ready, 1)
            for pos in range(1, NT):
                row_max(dve, 0, pos, True)
            max_pieces(dve, 0)
            for pos in range(LEAD):
                row_max(dve, 1, pos, False)
            for_groups(dve, dve_group)
            reciprocals(dve, G - 1)
            dve_rest(dve)

        @block.scalar
        def _(act):
            act.wait_ge(wkv_loaded, 16)
            nc.scalar.copy(wk.rearrange("p c (g d) -> p c g d", g=G),
                           wkv.rearrange("p c (g two d) -> p c g two d", g=G, two=2)[:, :, :, 0, :]).then_inc(wk_ready, 1)
            for t in range(NT):
                act.wait_ge(xnt_psum, t + 1)
                nc.scalar.copy(xnt[:, :, t * P:(t + 1) * P],
                               ps[:, t, :].rearrange("p (c q) -> p c q", c=ND)).then_inc(xnt_ready, 1)
            for j in range(1 + ND):
                for k in LORA_IN.get(j, ()):
                    lora_take(act, k)
                b = j % 2
                act.wait_ge(proj_psum, j + 1)
                if j >= 2:
                    act.wait_ge(pieces_stored[b], 48 * (j // 2))
                    act.wait_ge(pieces_ready, j - 1)
                nc.scalar.copy(pc[0][:, b, :], ps[:, 2 + 2 * b:4 + 2 * b, :].rearrange("p b n -> p (b n)")).then_inc(piece0, 1)
                if j == 0:
                    act.wait_ge(v_psum, 1)
                    nc.scalar.copy(vall[:, :, :, :].rearrange("p t g d -> p (t g d)"),
                                   ps[:, 6:8, :].rearrange("p b n -> p (b n)")).then_inc(v_ready, 1)
                    for k in range(4):
                        lora_load(act, k)
            for k in LORA_LATE:
                lora_take(act, k)
            for k in range(len(lora_jobs) - 2, len(lora_jobs)):
                lora_store(act, k)
            all_lora_stored(act)
            for_groups(act, act_group)
            take_o(act, G - 1)
            act_rest(act)

        @block.tensor
        def _(pe):
            pe.wait_ge(ident_ready, 1)
            for t in range(NT):
                pe.wait_ge(xn_ready, t + 1)
                for c in range(ND):
                    last = nc.tensor.transpose(ps[:, t, c * P:(c + 1) * P], xn[:, t, c * P:(c + 1) * P], ident[:, :])
                last.then_inc(xnt_psum, 1)
            pe.wait_ge(xnt_ready, NT)
            pe.wait_ge(wkv_loaded, 16)
            kvw = wkv.rearrange("p c (g two d) -> p c g two d", g=G, two=2)

            def project(j, weights, between):
                for half in range(2):
                    for c in range(ND):
                        last = nc.tensor.matmul(ps[:, 2 + 2 * (j % 2) + half, :], weights(c), xnt[:, c, half * 512:(half + 1) * 512],
                                                start=c == 0, stop=c == ND - 1)
                        if (half, c) == (1, ND - 1):
                            last.then_inc(proj_psum, 1)
                        between(half * ND + c)

            early = [(g, pos, h, c) for g, last_pos in ((0, NT), (1, LEAD)) for pos in range(last_pos)
                     for h in range(REP) for c in range(len(chunks(row_tile(pos))))]

            def early_scores():
                g, *rest = early.pop(0)
                scores(pe, g, *rest, g == 0)

            pe.wait_ge(wk_ready, 1)
            project(0, lambda c: wk[:, c, :], lambda i: None)
            for t in range(NT):
                for c in range(ND):
                    last = nc.tensor.matmul(ps[:, 6 + t // 4, (t % 4) * P:(t % 4 + 1) * P], xnt[:, c, t * P:(t + 1) * P],
                                            kvw[:, c, :, 1, :], start=c == 0, stop=c == ND - 1)
            last.then_inc(v_psum, 1)
            pe.wait_ge(wq_loaded, 16)
            for j in range(1, 1 + ND):
                if j >= 2:
                    pe.wait_ge(res_ready, j - 1)
                if j == 2:
                    pe.wait_ge(v_ready, 1)
                    pe.wait_ge(lora_stacked, 16 * 7)
                if j == ND:
                    pe.wait_ge(kt_loaded, 16 * len(TERMS))

                def between(i):
                    if j in LORA_IN and i < len(LORA_IN[j]):
                        lora_job(pe, LORA_IN[j][i], *lora_jobs[LORA_IN[j][i]])
                    if j == ND:
                        early_scores()

                project(j, lambda c: wq[:, c, (j - 1) * P:j * P], between)
            pe.wait_ge(res_ready, ND)
            done, left = 0, len(early)
            for i in range(left):
                early_scores()
                while done * left < len(LORA_LATE) * (i + 1):
                    k = LORA_LATE[done]
                    lora_job(pe, k, *lora_jobs[k])
                    done += 1
            pe.wait_ge(lora_taken, len(lora_jobs))
            pe.wait_ge(s_taken, AHEAD_UNITS)
            pe.wait_ge(ones_ready, 1)
            for_groups(pe, pe_group)
            weighted(pe, G - 1, NT - 1, 0, 1)
            pe_rest(pe)


def tables():
    import numpy as np
    n, half = np.arange(D), D // 2

    def angle(a, b):
        return 2 * np.pi * (np.outer(a, b) % D) / D

    def in_pieces(a):
        high = a.astype(np.float16)
        return np.stack([high, (a - high).astype(np.float16)])

    f = np.arange(half)
    forward = np.concatenate([np.cos(angle(n, f)), np.sin(angle(n, f))], 1)
    forward[:, half] = np.cos(angle(n, [half]))[:, 0]
    twice = np.where(f == 0, 1.0, 2.0)[:, None] / D
    power = np.concatenate([twice * np.cos(angle(f, n)), 2.0 / D * np.cos(angle(f, n))], 0)
    back = np.concatenate([twice * np.cos(angle(f, n)), -2.0 / D * np.sin(angle(f, n))], 0)
    power[half] = back[half] = np.cos(angle([half], n))[0] / D
    return in_pieces(forward * 2.0 ** 10), in_pieces(power[:, :LAGS] * 2.0 ** 18), in_pieces(back * 2.0 ** 18)


_INS = ["L0_attn_x", "L0_attn_Wq", "L0_attn_Wkv", "L0_attn_Wo", "L0_attn_bo",
        "L0_ffn_gate_t", "L0_ffn_up_t", "L0_ffn_down_t", "L0_ffn_gate_s", "L0_ffn_up_s", "L0_ffn_down_s",
        "L1_ffn_gate_w", "L1_ffn_up_w", "L1_ffn_down_w", "L1_ffn_gate_a", "L1_ffn_gate_b",
        "L1_ffn_up_a", "L1_ffn_up_b", "L1_ffn_down_a", "L1_ffn_down_b"]
_OUTS = [((1, T, D), "float32")]


def kernel(**inputs):
    import numpy as _np
    import concourse.bacc as _bacc
    from concourse import mybir as _mybir
    from concourse.bass_utils import run_bass_kernel_spmd as _run

    nc = _bacc.Bacc("TRN2", target_bir_lowering=False, num_devices=1)
    arrays, args = {}, []

    def give(name, a):
        arrays[name] = a
        args.append(nc.dram_tensor(name, a.shape, _mybir.dt.from_np(a.dtype), kind="ExternalInput").ap())

    for name in _INS:
        give(f"in_{name}_dram", _np.ascontiguousarray(inputs[name]))
    for name, a in zip(("dft", "power", "inverse"), tables()):
        give(f"table_{name}_dram", a)
    for i, (shape, dtype) in enumerate(_OUTS):
        args.append(nc.dram_tensor(f"out_{i}_dram", shape, _mybir.dt.from_np(_np.dtype(dtype)), kind="ExternalOutput").ap())
    build(nc, *args)
    r = _run(nc, [arrays], core_ids=[0])
    return r.results[0]["out_0_dram"]
```
